# Optimizing a Trainium2 kernel written in Bass

```python
import numpy as np
import jax
import jax.numpy as jnp

def _softmax(x, axis=-1):
    return jax.nn.softmax(x, axis=axis)

def _gelu(x):
    return jax.nn.gelu(x, approximate=True)

def _silu(x):
    return jax.nn.silu(x)

def _sigmoid(x):
    return jax.nn.sigmoid(x)

def _layernorm(x, axis=-1, eps=1e-05):
    m = jnp.mean(x, axis=axis, keepdims=True)
    v = jnp.var(x, axis=axis, keepdims=True)
    return (x - m) / jnp.sqrt(v + eps)

def _scatter_add(tgt, idx, src, axis=0):
    return tgt.at[idx].add(src)

def _segment_sum(src, seg, n):
    return jax.ops.segment_sum(src, seg, n)
kernel_name = 'mk_gnn_ffn_d1_gnn_r32_11287c'

def setup_inputs(seed: int=0):
    np.random.seed(seed)
    _w = jnp.asarray

    def _rec_inputs():
        import jax
        import jax.numpy as jnp
        _gk = jax.random.key(seed)
        x = -0.0003713 + 1 * jax.random.normal(jax.random.fold_in(_gk, 1), (3125, 256), jnp.float32)
        src = jax.random.randint(jax.random.fold_in(_gk, 2), (50000,), 0, 3125, jnp.int32)
        dst = jnp.minimum((3125 * jax.random.uniform(jax.random.fold_in(_gk, 3), (50000,)) ** 2.0).astype(jnp.int32), 99999)
        _o = jnp.argsort(dst, stable=True)
        src = src[_o]
        dst = dst[_o]
        edge_type_2 = jax.random.randint(jax.random.fold_in(_gk, 12), (50000,), 0, 2, jnp.int32)
        edge_weight = jax.random.uniform(jax.random.fold_in(_gk, 13), (50000,), jnp.float32, 0.0, 0.999999)
        return (x, src, dst, edge_type_2, edge_weight)
    x, src, dst, edge_type_2, edge_weight = _rec_inputs()

    def _L0_gnn_setup():
        import jax, jax.numpy as jnp
        import numpy as np
        N, E = (50000, 25000)
        IN_CH, H, C = (256, 8, 32)
        HID = H * C
        T = 2
        FFN = 4 * HID
        EPS = 1e-05

        def _layernorm(h, g, b):
            mu = jnp.mean(h, axis=-1, keepdims=True)
            var = jnp.mean(jnp.square(h - mu), axis=-1, keepdims=True)
            return (h - mu) * jax.lax.rsqrt(var + EPS) * g + b

        def _gat_forward(x, edge_index, edge_type, edge_weight, W_src, W_dst, att_src, att_dst, bias, ln1_g, ln1_b, ln2_g, ln2_b, ffn_W1, ffn_b1, ffn_W2, ffn_b2):
            n = x.shape[0]
            loop = jnp.arange(n, dtype=edge_index.dtype)
            src = jnp.concatenate([edge_index[0], loop])
            dst = jnp.concatenate([edge_index[1], loop])
            etype = jnp.concatenate([edge_type, jnp.zeros((n,), edge_type.dtype)])
            ew = jnp.concatenate([edge_weight, jnp.ones((n,), edge_weight.dtype)])
            x_src = (x @ W_src.T).reshape(n, H, C)
            x_dst = (x @ W_dst.T).reshape(n, H, C)
            xs_j = x_src[src]
            xd_i = x_dst[dst]
            a_s = att_src[etype]
            a_d = att_dst[etype]
            alpha = jnp.sum(xs_j * a_s, axis=-1) + jnp.sum(xd_i * a_d, axis=-1)
            alpha = jnp.where(alpha >= 0, alpha, 0.2 * alpha)
            m = jax.lax.stop_gradient(jax.ops.segment_max(alpha, dst, num_segments=n))
            a = jnp.exp(alpha - m[dst])
            denom = jax.ops.segment_sum(a, dst, num_segments=n)
            a = a / denom[dst]
            a = a * ew[:, None]
            msg = xs_j * a[:, :, None]
            out = jax.ops.segment_sum(msg, dst, num_segments=n)
            out = out.reshape(n, H * C) + bias
            h = _layernorm(out + x, ln1_g, ln1_b)
            ff = jax.nn.gelu(h @ ffn_W1.T + ffn_b1, approximate=False) @ ffn_W2.T + ffn_b2
            return _layernorm(h + ff, ln2_g, ln2_b)
        key = jax.random.key(seed)
        ks = jax.random.split(key, 16)
        s_in = 1.0 / np.sqrt(IN_CH)
        s_h = 1.0 / np.sqrt(HID)
        return {'x': jax.random.normal(ks[0], (N, IN_CH), jnp.float32), 'edge_index': jax.random.randint(ks[1], (2, E), 0, N, jnp.int32), 'edge_type': jax.random.randint(ks[2], (E,), 0, T, jnp.int32), 'edge_weight': jax.random.uniform(ks[3], (E,), jnp.float32), 'W_src': jax.random.normal(ks[4], (H * C, IN_CH), jnp.float32) * s_in, 'W_dst': jax.random.normal(ks[5], (H * C, IN_CH), jnp.float32) * s_in, 'att_src': jax.random.normal(ks[6], (T, H, C), jnp.float32) * (1.0 / np.sqrt(C)), 'att_dst': jax.random.normal(ks[7], (T, H, C), jnp.float32) * (1.0 / np.sqrt(C)), 'bias': jnp.zeros((HID,), jnp.float32), 'ln1_g': jnp.ones((HID,), jnp.float32), 'ln1_b': jnp.zeros((HID,), jnp.float32), 'ln2_g': jnp.ones((HID,), jnp.float32), 'ln2_b': jnp.zeros((HID,), jnp.float32), 'ffn_W1': jax.random.normal(ks[8], (FFN, HID), jnp.float32) * s_h, 'ffn_b1': jnp.zeros((FFN,), jnp.float32), 'ffn_W2': jax.random.normal(ks[9], (HID, FFN), jnp.float32) * (1.0 / np.sqrt(FFN)), 'ffn_b2': jnp.zeros((HID,), jnp.float32)}
    _L0_gnn_all = _L0_gnn_setup()
    _L0_gnn_in = {k: v for k, v in _L0_gnn_all.items() if k in ('W_src', 'W_dst', 'att_src', 'att_dst', 'bias', 'ln1_g', 'ln1_b', 'ln2_g', 'ln2_b', 'ffn_W1', 'ffn_b1', 'ffn_W2', 'ffn_b2')}
    del _L0_gnn_all

    def _L0_ffn_setup():
        import jax, jax.numpy as jnp
        import numpy as np
        B, S, H, F, E, K = (8, 128, 256, 512, 16, 2)
        EPS = 1e-05
        key = jax.random.key(seed)
        ks = jax.random.split(key, 9)
        sc = 0.02
        return {'x': jax.random.normal(ks[0], (B, S, H), dtype=jnp.float32), 'gate_w': jax.random.normal(ks[1], (H, E), dtype=jnp.float32) * sc, 'gate_b': jnp.zeros((E,), dtype=jnp.float32), 'w1': jax.random.normal(ks[2], (E, H, F), dtype=jnp.float32) * sc, 'b1': jnp.zeros((E, F), dtype=jnp.float32), 'w2': jax.random.normal(ks[3], (E, F, H), dtype=jnp.float32) * sc, 'b2': jnp.zeros((E, H), dtype=jnp.float32), 'gamma': jnp.ones((H,), dtype=jnp.float32), 'beta': jnp.zeros((H,), dtype=jnp.float32)}
    _L0_ffn_all = _L0_ffn_setup()
    _L0_ffn_in = {k: v for k, v in _L0_ffn_all.items() if k in ('gate_w', 'gate_b', 'w1', 'b1', 'w2', 'b2', 'gamma', 'beta')}
    del _L0_ffn_all
    return {'x': x, 'src': src, 'dst': dst, 'edge_type_2': edge_type_2, 'edge_weight': edge_weight, 'L0_gnn_W_src': _L0_gnn_in['W_src'], 'L0_gnn_W_dst': _L0_gnn_in['W_dst'], 'L0_gnn_att_src': _L0_gnn_in['att_src'], 'L0_gnn_att_dst': _L0_gnn_in['att_dst'], 'L0_gnn_bias': _L0_gnn_in['bias'], 'L0_gnn_ln1_g': _L0_gnn_in['ln1_g'], 'L0_gnn_ln1_b': _L0_gnn_in['ln1_b'], 'L0_gnn_ln2_g': _L0_gnn_in['ln2_g'], 'L0_gnn_ln2_b': _L0_gnn_in['ln2_b'], 'L0_gnn_ffn_W1': _L0_gnn_in['ffn_W1'], 'L0_gnn_ffn_b1': _L0_gnn_in['ffn_b1'], 'L0_gnn_ffn_W2': _L0_gnn_in['ffn_W2'], 'L0_gnn_ffn_b2': _L0_gnn_in['ffn_b2'], 'L0_ffn_gate_w': _L0_ffn_in['gate_w'], 'L0_ffn_gate_b': _L0_ffn_in['gate_b'], 'L0_ffn_w1': _L0_ffn_in['w1'], 'L0_ffn_b1': _L0_ffn_in['b1'], 'L0_ffn_w2': _L0_ffn_in['w2'], 'L0_ffn_b2': _L0_ffn_in['b2'], 'L0_ffn_gamma': _L0_ffn_in['gamma'], 'L0_ffn_beta': _L0_ffn_in['beta']}

def reference(x, src, dst, edge_type_2, edge_weight, L0_gnn_W_src, L0_gnn_W_dst, L0_gnn_att_src, L0_gnn_att_dst, L0_gnn_bias, L0_gnn_ln1_g, L0_gnn_ln1_b, L0_gnn_ln2_g, L0_gnn_ln2_b, L0_gnn_ffn_W1, L0_gnn_ffn_b1, L0_gnn_ffn_W2, L0_gnn_ffn_b2, L0_ffn_gate_w, L0_ffn_gate_b, L0_ffn_w1, L0_ffn_b1, L0_ffn_w2, L0_ffn_b2, L0_ffn_gamma, L0_ffn_beta):
    import jax
    import jax.numpy as jnp

    def _L0_gnn_ref(x, edge_index, edge_type, edge_weight, W_src, W_dst, att_src, att_dst, bias, ln1_g, ln1_b, ln2_g, ln2_b, ffn_W1, ffn_b1, ffn_W2, ffn_b2):
        import jax, jax.numpy as jnp
        import numpy as np
        N, E = (50000, 25000)
        IN_CH, H, C = (256, 8, 32)
        HID = H * C
        T = 2
        FFN = 4 * HID
        EPS = 1e-05

        def _layernorm(h, g, b):
            mu = jnp.mean(h, axis=-1, keepdims=True)
            var = jnp.mean(jnp.square(h - mu), axis=-1, keepdims=True)
            return (h - mu) * jax.lax.rsqrt(var + EPS) * g + b

        def _gat_forward(x, edge_index, edge_type, edge_weight, W_src, W_dst, att_src, att_dst, bias, ln1_g, ln1_b, ln2_g, ln2_b, ffn_W1, ffn_b1, ffn_W2, ffn_b2):
            n = x.shape[0]
            loop = jnp.arange(n, dtype=edge_index.dtype)
            src = jnp.concatenate([edge_index[0], loop])
            dst = jnp.concatenate([edge_index[1], loop])
            etype = jnp.concatenate([edge_type, jnp.zeros((n,), edge_type.dtype)])
            ew = jnp.concatenate([edge_weight, jnp.ones((n,), edge_weight.dtype)])
            x_src = (x @ W_src.T).reshape(n, H, C)
            x_dst = (x @ W_dst.T).reshape(n, H, C)
            xs_j = x_src[src]
            xd_i = x_dst[dst]
            a_s = att_src[etype]
            a_d = att_dst[etype]
            alpha = jnp.sum(xs_j * a_s, axis=-1) + jnp.sum(xd_i * a_d, axis=-1)
            alpha = jnp.where(alpha >= 0, alpha, 0.2 * alpha)
            m = jax.lax.stop_gradient(jax.ops.segment_max(alpha, dst, num_segments=n))
            a = jnp.exp(alpha - m[dst])
            denom = jax.ops.segment_sum(a, dst, num_segments=n)
            a = a / denom[dst]
            a = a * ew[:, None]
            msg = xs_j * a[:, :, None]
            out = jax.ops.segment_sum(msg, dst, num_segments=n)
            out = out.reshape(n, H * C) + bias
            h = _layernorm(out + x, ln1_g, ln1_b)
            ff = jax.nn.gelu(h @ ffn_W1.T + ffn_b1, approximate=False) @ ffn_W2.T + ffn_b2
            return _layernorm(h + ff, ln2_g, ln2_b)
        return _gat_forward(x, edge_index, edge_type, edge_weight, W_src, W_dst, att_src, att_dst, bias, ln1_g, ln1_b, ln2_g, ln2_b, ffn_W1, ffn_b1, ffn_W2, ffn_b2)

    def _L0_ffn_ref(x, gate_w, gate_b, w1, b1, w2, b2, gamma, beta):
        import jax, jax.numpy as jnp
        import numpy as np
        B, S, H, F, E, K = (8, 128, 256, 512, 16, 2)
        EPS = 1e-05
        gate_logits = x @ gate_w + gate_b
        topk_vals, topk_idx = jax.lax.top_k(gate_logits, K)
        topk_w = jax.nn.softmax(topk_vals, axis=-1)
        h = jax.nn.relu(jnp.einsum('bsh,ehf->bsef', x, w1) + b1)
        expert_out = jnp.einsum('bsef,efh->bseh', h, w2) + b2
        sel = jnp.take_along_axis(expert_out, topk_idx[:, :, :, None], axis=2)
        moe = jnp.sum(topk_w[..., None] * sel, axis=2)
        y = x + moe
        mu = jnp.mean(y, axis=-1, keepdims=True)
        var = jnp.var(y, axis=-1, keepdims=True)
        return (y - mu) / jnp.sqrt(var + EPS) * gamma + beta
    edge_index = jnp.stack([src, dst])
    x = x + _L0_gnn_ref(_layernorm(x, axis=-1), edge_index, edge_type_2, edge_weight, L0_gnn_W_src, L0_gnn_W_dst, L0_gnn_att_src, L0_gnn_att_dst, L0_gnn_bias, L0_gnn_ln1_g, L0_gnn_ln1_b, L0_gnn_ln2_g, L0_gnn_ln2_b, L0_gnn_ffn_W1, L0_gnn_ffn_b1, L0_gnn_ffn_W2, L0_gnn_ffn_b2)
    x = x + _L0_ffn_ref(_layernorm(x, axis=-1)[None], L0_ffn_gate_w, L0_ffn_gate_b, L0_ffn_w1, L0_ffn_b1, L0_ffn_w2, L0_ffn_b2, L0_ffn_gamma, L0_ffn_beta)[0]
    return x

_drawn_inputs = setup_inputs


def setup_inputs(seed=0):
    import zlib

    import numpy as np

    out = dict(_drawn_inputs(seed))
    spreads = {'L0_gnn_bias': (0.0, 0.1),
     'L0_gnn_ln1_g': (1.0, 0.2),
     'L0_gnn_ln1_b': (0.0, 0.1),
     'L0_gnn_ln2_g': (1.0, 0.2),
     'L0_gnn_ln2_b': (0.0, 0.1),
     'L0_gnn_ffn_b1': (0.0, 0.1),
     'L0_gnn_ffn_b2': (0.0, 0.1),
     'L0_ffn_gate_b': (0.0, 0.332),
     'L0_ffn_b1': (0.0, 0.8),
     'L0_ffn_b2': (0.0, 0.316),
     'L0_ffn_gamma': (1.0, 0.2),
     'L0_ffn_beta': (0.0, 0.1)}
    factors = {}
    for name, (base, spread) in spreads.items():
        noise = np.random.default_rng([zlib.crc32(name.encode()), seed]).standard_normal(out[name].shape)
        drawn = base * np.exp(spread * noise) if base else spread * noise
        out[name] = jnp.asarray(drawn.astype(out[name].dtype))
    for name, factor in factors.items():
        out[name] = (out[name] * factor).astype(out[name].dtype)
    return out
```

```python
import concourse.bass as bass
from concourse import mybir
from contextlib import ExitStack

P = 128
N_NODES = 3125
BLOCKS = -(-N_NODES // P)
ROWS = BLOCKS * P
N_EDGES = 50000
EDGE_TILES = -(-N_EDGES // P)
D = 256
KD = D // P
H, C = 8, 32
T = 2
F = 1024
KF = F // P
EXPERTS, FE = 16, 512
KE = FE // P
EPS = 1e-5
LOT = 8
LOTS = 4
STEP = LOTS * LOT
CHUNKS = P // H
PER_CHUNK = -(-(EDGE_TILES + BLOCKS) // CHUNKS)
SLOTS = CHUNKS * PER_CHUNK
STEPS = SLOTS // STEP
SLOT_GROUPS = -(-SLOTS // P)
SCAN = PER_CHUNK * P
NEG = -3.0e38
SUMS = D + 2 * H + 1
ASSIGN = 2 * BLOCKS
TILES = (2 * ROWS + EXPERTS * (P - 1)) // P
GROUP = 5
GT = GROUP * P

fp32 = mybir.dt.float32
bf16 = mybir.dt.bfloat16
u32 = mybir.dt.uint32
i32 = mybir.dt.int32
ALU = mybir.AluOpType
ACT = mybir.ActivationFunctionType
AX = mybir.AxisListType.X


def take(eng, sem, n=1):
    eng.wait_ge(sem, n)
    eng.sem_inc(sem, -n)


class Chain:

    def __init__(self, eng, sem):
        self.eng, self.sem, self.n = eng, sem, 0

    def __call__(self, ins):
        ins.then_inc(self.sem, 1)
        self.n += 1
        self.eng.wait_ge(self.sem, self.n)

    def also(self, ins):
        ins.then_inc(self.sem, 1)
        self.n += 1

    def close(self):
        self.eng.wait_ge(self.sem, self.n)
        self.eng.sem_inc(self.sem, -self.n)
        self.n = 0


def numbers(nc, eng, row, most):
    _, got = nc.values_load_multi_w_load_instructions(
        row, engines=[eng.engine], min_val=0, max_val=most,
        skip_runtime_bounds_check_because="the numbers are clamped on the chip when they are made")
    return got


def build(nc, a, out, scratch, stages=9):
    ctx = ExitStack()
    with ctx:
        def sem(name):
            return ctx.enter_context(nc.semaphore(name))

        def sb(name, shape, dt=fp32):
            return ctx.enter_context(nc.sbuf_tensor(name, shape, dt))

        banks = [ctx.enter_context(nc.psum_tensor(f"bank{i}", [P, 512], fp32)) for i in range(8)]

        ident = sb("ident", [P, P])
        ones = sb("ones", [P, P])
        before = sb("before", [P, P])
        lane = sb("lane", [P, P])
        part = sb("part", [P, 1])
        heads = sb("heads", [P, KD, H])
        arena = sb("arena", [P, 44000])

        def at(off, *dims, dt=fp32):
            n = 1
            for d in dims:
                n *= d
            assert off + n <= 44000, (off, n)
            v = arena[:, off:off + n]
            if dt != fp32:
                v = v.bitcast(dt)
            if len(dims) == 2:
                v = v.rearrange("p (a b) -> p a b", b=dims[1])
            elif len(dims) == 3:
                v = v.rearrange("p (a b c) -> p a b c", b=dims[1], c=dims[2])
            return v

        n_sems = []
        s_const = sem("constants_made")
        pool_step = sem("pool_step")
        dve_step = sem("dve_step")
        act_step = sem("act_step")

        dtab = sb("dtab", [P, BLOCKS, 3 * H])
        xb = at(0, BLOCKS, D)
        PW = D + 4 * H
        proj = at(BLOCKS * D, BLOCKS, PW)
        xs, sd = proj[:, :, 0:D], proj[:, :, D:]
        o = BLOCKS * (D + PW)
        wv = at(o, KD, D + 4 * H); o += KD * (D + 4 * H)
        wsrc = at(o, KD, D); o += KD * D
        wdst = at(o, KD, D); o += KD * D
        att = at(o, KD, 2 * T); o += KD * 2 * T
        attm = at(o, KD, 2 * T, H); o += KD * 2 * T * H
        stats = at(o, BLOCKS, 6); o += BLOCKS * 6
        mean = at(o, BLOCKS); o += BLOCKS
        rstd = at(o, BLOCKS); o += BLOCKS
        tmp1 = at(o, BLOCKS); o += BLOCKS
        xl = at(o, GROUP, D); o += GROUP * D
        xt = at(o, GROUP, KD, P); o += GROUP * KD * P

        s_x = sem("x_loaded")
        s_w = sem("proj_weights_loaded")
        s_var = sem("variances_ready")
        s_std = sem("deviations_ready")
        s_attm = sem("masked_attention_ready")
        s_v = sem("score_vectors_ready")
        s_vc = sem("score_vectors_copied")
        s_xl = sem("block_normalised")
        s_tr = sem("block_turned")
        s_xt = sem("turned_copied")
        s_pj = sem("block_projected")
        s_pjfree = sem("projection_copied")
        s_xlfree = sem("normalised_used")
        s_projd = sem("projections_copied")

        def turn_slot(j):
            return banks[j % 3][:, 0:D].rearrange("p (k n) -> p k n", k=KD)

        s_tab = sem("tables_ready")
        s_store = sem("tables_stored")

        def stats_to_scales(v, link, st, mn, rs, t, n_out):
            link(v.tensor_tensor(mn, st[:, :, 1], st[:, :, 4], ALU.add))
            link(v.tensor_tensor(t, st[:, :, 1], st[:, :, 4], ALU.subtract))
            link(v.tensor_scalar(mn, mn, 0.5, None, ALU.mult))
            link(v.tensor_tensor(t, t, t, ALU.mult))
            link(v.tensor_tensor(rs, st[:, :, 2], st[:, :, 5], ALU.add))
            link(v.tensor_scalar(rs, rs, 1.0 / D, EPS, ALU.mult, ALU.add))
            return v.scalar_tensor_tensor(out=rs, in0=t, scalar=0.25, in1=rs, op0=ALU.mult, op1=ALU.add)

        with nc.Block() as block:
            @block.sync
            def _(sp):
                sp.dma_start(xb, a["x"].rearrange("(t p) d -> p t d", p=P)).then_inc(s_x, 16)
                sp.dma_start(wv[:, :, 0:D], a["W_srcT"].rearrange("(k p) n -> p k n", p=P)).then_inc(s_w, 16)
                sp.dma_start(wsrc, a["W_src"].rearrange("(k p) n -> p k n", p=P)).then_inc(s_w, 16)
                sp.dma_start(wdst, a["W_dst"].rearrange("(k p) n -> p k n", p=P)).then_inc(s_w, 16)
                sp.dma_start(att, a["att"].rearrange("(k p) n -> p k n", p=P)).then_inc(s_w, 16)
                sp.wait_ge(s_tab, 1)
                sp.dma_start(scratch["xs"].rearrange("(t p) d -> p t d", p=P), xs).then_inc(s_store, 16)
                sp.dma_start(scratch["xln"].rearrange("(t p) d -> p t d", p=P), xb).then_inc(s_store, 16)
                sp.dma_start(scratch["s"].rearrange("(t p) d -> p t d", p=P), sd[:, :, 0:2 * H]).then_inc(s_store, 16)
                sp.wait_ge(s_store, 48)

            @block.gpsimd
            def _(g):
                link = Chain(g, pool_step)
                link.also(g.memset(ident[:, :], 0.0))
                link.also(g.memset(ones[:, :], 1.0))
                link.also(g.memset(before[:, :], 1.0))
                link.also(g.memset(heads[:, :, :], 1.0))
                link(g.iota(lane[:, :], pattern=[[1, P]], base=0, channel_multiplier=0,
                            allow_small_or_imprecise_dtypes=True))
                link.also(g.iota(part[:, :], pattern=[[1, 1]], base=0, channel_multiplier=1,
                                 allow_small_or_imprecise_dtypes=True))
                link.also(g.affine_select(out=ident[:, :], in_=ident[:, :], compare_op=ALU.not_equal, fill=1.0,
                                          base=0, pattern=[[-1, P]], channel_multiplier=1))
                link.also(g.affine_select(out=before[:, :], in_=before[:, :], compare_op=ALU.is_gt, fill=0.0,
                                          base=0, pattern=[[1, P]], channel_multiplier=-1))
                link(g.affine_select(out=heads[:, :, :], in_=heads[:, :, :], compare_op=ALU.is_ge, fill=0.0,
                                     base=0, pattern=[[P, KD], [-C, H]], channel_multiplier=1))
                link(g.affine_select(out=heads[:, :, :], in_=heads[:, :, :], compare_op=ALU.is_ge, fill=0.0,
                                     base=C - 1, pattern=[[-P, KD], [C, H]], channel_multiplier=-1))
                link.close()
                g.sem_inc(s_const, 1)

            @block.vector
            def _(v):
                link = Chain(v, dve_step)
                v.wait_ge(s_const, 1)
                v.wait_ge(s_w, 64)
                for k in range(KD):
                    for t in range(2 * T):
                        link.also(v.tensor_scalar(attm[:, k, t, :], heads[:, k, :], att[:, k, t:t + 1], None, ALU.mult))
                link.close()
                v.sem_inc(s_attm, 1)
                v.wait_ge(s_x, 16)
                for b in range(BLOCKS):
                    link.also(v.bn_stats(stats[:, b, :], xb[:, b, :]))
                v.wait_ge(dve_step, link.n)
                stats_to_scales(v, link, stats, mean, rstd, tmp1, 1).then_inc(s_var, 1)
                v.wait_ge(s_v, 1)
                v.tensor_copy(wv[:, :, D:], banks[7][:, 0:KD * 4 * H].rearrange("p (k n) -> p k n", k=KD)).then_inc(s_vc, 1)
                v.wait_ge(s_std, 1)
                link(v.reciprocal(rstd, rstd))
                link.close()
                v.sem_inc(s_xlfree, GROUP)
                with v.Fori(0, BLOCKS // GROUP) as g:
                    for j in range(GROUP):
                        b = bass.ds(g * GROUP + j, 1)
                        take(v, s_xlfree)
                        v.tensor_scalar(xl[:, j, :], xb[:, b, :], mean[:, b], rstd[:, b],
                                        ALU.subtract, ALU.mult).then_inc(s_xl, 1)
                for b in range(BLOCKS):
                    link.also(v.tensor_scalar(xb[:, b, :], xb[:, b, :], mean[:, b:b + 1], rstd[:, b:b + 1],
                                              ALU.subtract, ALU.mult))
                v.wait_ge(s_projd, 1)
                link.also(v.tensor_copy(dtab[:, :, 0:2 * H], sd[:, :, 2 * H:4 * H]))
                link(v.tensor_tensor(dtab[:, :, 2 * H:], sd[:, :, 0:H], sd[:, :, 2 * H:3 * H], ALU.add))
                link(v.scalar_tensor_tensor(out=dtab[:, :, 2 * H:], in0=dtab[:, :, 2 * H:], scalar=0.2,
                                            in1=dtab[:, :, 2 * H:], op0=ALU.mult, op1=ALU.max))
                link.close()
                v.sem_inc(s_tab, 1)

            @block.scalar
            def _(s):
                s.wait_ge(s_var, 1)
                s.activation(rstd, rstd, ACT.Sqrt).then_inc(s_std, 1)
                def turned_copy(j):
                    take(s, s_tr)
                    s.activation(xt[:, j, :, :], turn_slot(j), ACT.Copy).then_inc(s_xt, 1)

                def projected_copy(g, j):
                    take(s, s_pj)
                    s.activation(proj[:, bass.ds(g * GROUP + j, 1), :], banks[3 + j][:, 0:PW], ACT.Copy).then_inc(s_pjfree, 1)

                with s.Fori(0, BLOCKS // GROUP) as g:
                    turned_copy(0)
                    for j in range(1, GROUP):
                        turned_copy(j)
                        projected_copy(g, j - 1)
                    projected_copy(g, GROUP - 1)
                s.wait_ge(s_pjfree, GROUP)
                s.sem_inc(s_projd, 1)

            @block.tensor
            def _(pe):
                pe.wait_ge(s_attm, 1)
                for m in range(KD):
                    for w, (wt, c0) in enumerate(((wsrc, 0), (wdst, T))):
                        for k in range(KD):
                            last = pe.matmul(banks[7][:, m * 4 * H + w * 2 * H: m * 4 * H + (w + 1) * 2 * H],
                                             wt[:, k, m * P:(m + 1) * P], attm[:, k, c0:c0 + T, :],
                                             start=(k == 0), stop=(k == KD - 1))
                last.then_inc(s_v, 1)
                pe.wait_ge(s_vc, 1)
                pe.sem_inc(s_pjfree, GROUP)

                def turn(j):
                    take(pe, s_xl)
                    for k in range(KD):
                        last = pe.transpose(turn_slot(j)[:, k, :], xl[:, j, k * P:(k + 1) * P], ident[:, :])
                    last.then_inc(s_tr, 1)

                def project(j):
                    take(pe, s_xt)
                    pe.sem_inc(s_xlfree, 1)
                    take(pe, s_pjfree)
                    for k in range(KD):
                        last = pe.matmul(banks[3 + j][:, 0:PW], xt[:, j, k, :], wv[:, k, :], start=(k == 0), stop=(k == KD - 1))
                    last.then_inc(s_pj, 1)

                with pe.Fori(0, BLOCKS // GROUP) as g:
                    turn(0)
                    for j in range(1, GROUP):
                        turn(j)
                        project(j - 1)
                    project(GROUP - 1)

        if stages == 1:
            return

        AHEAD = LOTS * LOT
        src_at = sb("src_at", [P, SLOTS + AHEAD], u32)
        srct_at = sb("srct_at", [P, SLOTS + AHEAD], u32)
        local = sb("local", [P, SLOTS + LOT])
        key = sb("key", [P, SLOTS])
        kind = sb("kind", [P, SLOTS])
        weight = sb("weight", [P, SLOTS])
        blk = sb("blk", [P, SLOTS], i32)
        o = 0
        lastrow_i = at(o, EDGE_TILES, dt=i32)[0:1, :]; o += EDGE_TILES
        lastrow = at(o, EDGE_TILES)[0:1, :]; o += EDGE_TILES
        tilerow = at(o, EDGE_TILES)[0:1, :]; o += EDGE_TILES
        junk = at(o, EDGE_TILES); o += EDGE_TILES
        slot_tile = at(o, SLOT_GROUPS); o += SLOT_GROUPS
        slot_tile_i = at(o, SLOT_GROUPS, dt=u32); o += SLOT_GROUPS
        slot_blk = at(o, SLOT_GROUPS); o += SLOT_GROUPS
        slot_off = at(o, SLOT_GROUPS); o += SLOT_GROUPS
        slot_no = at(o, SLOT_GROUPS); o += SLOT_GROUPS
        diag = at(o, SLOT_GROUPS, P); o += SLOT_GROUPS * P
        raw = [at(o + i * SLOT_GROUPS * P, SLOT_GROUPS, P, dt=dt) for i, dt in enumerate((i32, i32, i32, fp32))]
        o += 4 * SLOT_GROUPS * P
        rsrc = at(o, SLOT_GROUPS, P); o += SLOT_GROUPS * P
        rsrct = at(o, SLOT_GROUPS, P); o += SLOT_GROUPS * P
        rdst = at(o, SLOT_GROUPS, P); o += SLOT_GROUPS * P
        rkind = at(o, SLOT_GROUPS, P); o += SLOT_GROUPS * P
        rlocal = at(o, SLOT_GROUPS, P); o += SLOT_GROUPS * P
        rok = at(o, SLOT_GROUPS, P); o += SLOT_GROUPS * P
        rkey = at(o, SLOT_GROUPS, P); o += SLOT_GROUPS * P

        s_last = sem("tile_ends_loaded")
        s_iota = sem("tile_numbers_made")
        s_lrow = sem("staircase_row_ready")
        s_lbc = sem("staircase_spread")
        s_stile = sem("slot_tiles_ready")
        s_diag = sem("block_diagonals_ready")
        s_bbc = sem("blocks_spread")
        s_rec = sem("edge_rows_gathered")
        s_rows = sem("slot_rows_ready")
        s_rt = sem("slot_rows_turned")
        s_rtc = sem("turned_rows_copied")
        with nc.Block() as block:
            @block.sync
            def _(sp):
                sp.dma_start(lastrow_i, a["dst"].rearrange("(a t) e -> a t e", a=1)[:, :, P - 1],
                             allow_slow_non_contiguous=True).then_inc(s_last, 16)

            @block.gpsimd
            def _(g):
                g.iota(tilerow, pattern=[[1, EDGE_TILES]], base=0, channel_multiplier=0,
                       allow_small_or_imprecise_dtypes=True).then_inc(s_iota, 1)
                g.wait_ge(s_iota, 1)
                g.iota(slot_no, pattern=[[P, SLOT_GROUPS]], base=0, channel_multiplier=1,
                       allow_small_or_imprecise_dtypes=True).then_inc(s_iota, 1)
                g.wait_ge(s_stile, 1)
                for i, name in enumerate(("src", "dst", "kind", "weight")):
                    for q in range(SLOT_GROUPS):
                        g.indirect_dma_start(out=raw[i][:, q, :], out_offset=None, in_=a[name],
                                             in_offset=bass.IndirectOffsetOnAxis(ap=slot_tile_i[:, q:q + 1], axis=0)
                                             ).then_inc(s_rec, 16)

            @block.vector
            def _(v):
                link = Chain(v, dve_step)
                v.wait_ge(s_last, 16)
                v.wait_ge(s_iota, 2)
                link(v.tensor_single_scalar(lastrow_i, lastrow_i, 7, ALU.arith_shift_right))
                link(v.tensor_copy(lastrow, lastrow_i))
                v.tensor_tensor(lastrow, lastrow, tilerow, ALU.add).then_inc(s_lrow, 1)
                v.wait_ge(s_lbc, 1)
                for q in range(SLOT_GROUPS):
                    link(v.tensor_scalar(junk, banks[0][:, 0:EDGE_TILES], slot_no[:, q:q + 1], 0.0,
                                         ALU.is_lt, ALU.add, accum_out=slot_tile[:, q:q + 1]))
                link(v.tensor_scalar(slot_tile, slot_tile, float(EDGE_TILES - 1), None, ALU.min))
                v.tensor_copy(slot_tile_i, slot_tile).then_inc(s_stile, 1)
                link(v.tensor_tensor(slot_blk, slot_no, slot_tile, ALU.subtract))
                link(v.tensor_scalar(slot_off, slot_blk, float(P), None, ALU.mult))
                for q in range(SLOT_GROUPS):
                    link.also(v.tensor_scalar(diag[:, q, :], ident[:, :], slot_blk[:, q:q + 1], None, ALU.mult))
                link.close()
                v.sem_inc(s_diag, 1)
                v.wait_ge(s_bbc, 1)
                link(v.tensor_scalar(blk[:, :], banks[1][:, 0:SLOTS], float(BLOCKS - 1), None, ALU.min))
                v.wait_ge(s_rec, 16 * 4 * SLOT_GROUPS)
                link.also(v.tensor_copy(rsrc, raw[0]))
                link.also(v.tensor_copy(rdst, raw[1]))
                link(v.tensor_copy(rkind, raw[2]))
                link.also(v.scalar_tensor_tensor(out=rsrct, in0=rsrc, scalar=2.0, in1=rkind, op0=ALU.mult, op1=ALU.add))
                for q in range(SLOT_GROUPS):
                    link(v.tensor_scalar(rlocal[:, q, :], rdst[:, q, :], slot_off[:, q:q + 1], None, ALU.subtract))
                link(v.tensor_scalar(rok, rlocal, 0.0, None, ALU.is_ge))
                link(v.scalar_tensor_tensor(out=rok, in0=rlocal, scalar=float(P), in1=rok, op0=ALU.is_lt, op1=ALU.mult))
                link(v.scalar_tensor_tensor(out=rlocal, in0=rlocal, scalar=1.0, in1=rok, op0=ALU.add, op1=ALU.mult))
                link(v.scalar_tensor_tensor(out=rkey, in0=rdst, scalar=1.0, in1=rok, op0=ALU.add, op1=ALU.mult))
                link.also(v.tensor_scalar(rlocal, rlocal, -1.0, None, ALU.add))
                link(v.tensor_scalar(rkey, rkey, -1.0, None, ALU.add))
                link.close()
                v.sem_inc(s_rows, 1)
                link.also(v.memset(src_at[:, SLOTS:], 0))
                link.also(v.memset(srct_at[:, SLOTS:], 0))
                link.also(v.memset(local[:, SLOTS:], -1.0))
                link.close()
                for i, dst in enumerate((src_at, srct_at, local, key, kind, weight)):
                    v.wait_ge(s_rt, i + 1)
                    v.tensor_copy(dst[:, 0:SLOTS], banks[2 + i % 2][:, 0:SLOTS]).then_inc(s_rtc, 1)
                v.wait_ge(s_rtc, 6)

            @block.tensor
            def _(pe):
                pe.wait_ge(s_lrow, 1)
                pe.matmul(banks[0][:, 0:EDGE_TILES], ones[0:1, :], lastrow, start=True, stop=True).then_inc(s_lbc, 1)
                pe.wait_ge(s_diag, 1)
                pe.matmul(banks[1][:, :], ones[:, :], diag.rearrange("p q n -> p (q n)"), start=True, stop=True).then_inc(s_bbc, 1)
                pe.wait_ge(s_rows, 1)
                for i, rows in enumerate((rsrc, rsrct, rlocal, rkey, rkind, raw[3])):
                    if i >= 2:
                        pe.wait_ge(s_rtc, i - 1)
                    for q in range(SLOT_GROUPS):
                        last = pe.transpose(banks[2 + i % 2][:, q * P:(q + 1) * P], rows[:, q, :], ident[:, :])
                    last.then_inc(s_rt, 1)

        if stages == 2:
            return

        o = 0
        alpha = at(o, SLOTS, H); o += SLOTS * H
        selfe = at(o, SLOTS, H); o += SLOTS * H
        mx = at(o, SLOTS, H); o += SLOTS * H
        edge_end = o
        sg = at(o, STEP, H); o += STEP * H
        idx_a = at(o, STEP, dt=u32); o += STEP
        hot = at(o, 2, LOT * P); o += 2 * LOT * P
        hotT = at(o, 2, LOT * P); o += 2 * LOT * P
        d0 = at(o, LOT, H); o += LOT * H
        d1 = at(o, LOT, H); o += LOT * H
        nkind = at(o, SLOTS); o += SLOTS

        s_ga = [sem(f"source_terms_gathered{h}") for h in range(LOTS)]
        s_gafree = [sem(f"source_terms_used{h}") for h in range(LOTS)]
        s_idx_a = sem("source_term_numbers_ready")
        s_hot = sem("onehots_ready")
        s_hott = sem("onehots_turned")
        s_hotc = sem("turned_onehots_copied")
        s_dsel = sem("destination_terms_selected")
        s_dfree = sem("destination_terms_used")

        def make_hot(v, buf, sl):
            return v.tensor_tensor(buf.rearrange("p (s n) -> p s n", n=P),
                                   lane[:, :].unsqueeze(1).to_broadcast([P, LOT, P]),
                                   local[:, sl].unsqueeze(2).to_broadcast([P, LOT, P]), ALU.is_equal)

        def gather(g, s_idx, s_done, rows, idx, table):
            with g.Fori(0, STEPS) as i:
                for h in range(LOTS):
                    take(g, s_idx)
                    for n in range(h * LOT, (h + 1) * LOT):
                        g.indirect_dma_start(out=rows[:, n, :], out_offset=None, in_=table,
                                             in_offset=bass.IndirectOffsetOnAxis(ap=idx[:, n:n + 1], axis=0)
                                             ).then_inc(s_done[h], 16)

        def copy_numbers(s, s_free, s_idx, idx, numbers_at, i, h):
            n = h % LOTS * LOT
            take(s, s_free[h % LOTS])
            s.activation(idx[:, n:n + LOT], numbers_at[:, bass.ds(i * STEP + h * LOT, LOT)], ACT.Copy).then_inc(s_idx, 1)

        with nc.Block() as block:
            @block.gpsimd
            def _(g):
                gather(g, s_idx_a, s_ga, sg, idx_a, scratch["s"].rearrange("n (t h) -> (n t) h", t=T))

            @block.vector
            def _(v):
                link = Chain(v, dve_step)
                link(v.tensor_scalar(nkind, kind[:, :], -1.0, 1.0, ALU.mult, ALU.add))
                link.close()
                for h in range(LOTS):
                    v.sem_inc(s_gafree[h], 1)
                make_hot(v, hot[:, 0, :], bass.ds(0, LOT)).then_inc(s_hot, 1)
                with v.Fori(0, STEPS) as i:
                    for h in range(LOTS):
                        sl = bass.ds(i * STEP + h * LOT, LOT)
                        make_hot(v, hot[:, (h + 1) % 2, :], bass.ds(i * STEP + (h + 1) * LOT, LOT)).then_inc(s_hot, 1)
                        take(v, s_dsel)
                        dsel = banks[4 + h % 2][:, 0:LOT * 3 * H].rearrange("p (s n) -> p s n", n=3 * H)
                        link.also(v.tensor_copy(selfe[:, sl, :], dsel[:, :, 2 * H:]))
                        link.also(v.tensor_tensor(d0, dsel[:, :, 0:H], nkind[:, sl].unsqueeze(2).to_broadcast([P, LOT, H]), ALU.mult))
                        link(v.tensor_tensor(d1, dsel[:, :, H:2 * H], kind[:, sl].unsqueeze(2).to_broadcast([P, LOT, H]), ALU.mult))
                        v.sem_inc(s_dfree, 1)
                        link(v.tensor_tensor(d0, d0, d1, ALU.add))
                        v.wait_ge(s_ga[h], (i + 1) * (16 * LOT))
                        link(v.tensor_tensor(d0, d0, sg[:, h * LOT:(h + 1) * LOT, :], ALU.add))
                        v.sem_inc(s_gafree[h], 1)
                        link(v.scalar_tensor_tensor(out=alpha[:, sl, :], in0=d0, scalar=0.2, in1=d0, op0=ALU.mult, op1=ALU.max))
                    link.close()

            @block.scalar
            def _(s):
                def turned_copy(h):
                    for q in range(2):
                        take(s, s_hott)
                        s.activation(hotT[:, h % 2, q * 512:(q + 1) * 512], banks[2 * (h % 2) + q][:, :], ACT.Copy).then_inc(s_hotc, 1)

                for h in range(LOTS - 1):
                    copy_numbers(s, s_gafree, s_idx_a, idx_a, srct_at, 0, h)
                turned_copy(0)
                with s.Fori(0, STEPS) as i:
                    for h in range(LOTS):
                        turned_copy(h + 1)
                        copy_numbers(s, s_gafree, s_idx_a, idx_a, srct_at, i, h + LOTS - 1)

            @block.tensor
            def _(pe):
                def turn(h):
                    take(pe, s_hot)
                    for q in range(2):
                        for j in range(4):
                            last = pe.transpose(banks[2 * (h % 2) + q][:, j * P:(j + 1) * P],
                                                hot[:, h % 2, (4 * q + j) * P:(4 * q + j + 1) * P], ident[:, :])
                        last.then_inc(s_hott, 1)

                pe.sem_inc(s_dfree, 2)
                turn(0)
                with pe.Fori(0, STEPS) as i:
                    for h in range(LOTS):
                        blocks = numbers(nc, pe, blk[0:1, bass.ds(i * STEP + h * LOT, LOT)], BLOCKS - 1)
                        take(pe, s_hotc, 2)
                        take(pe, s_dfree)
                        for j in range(LOT):
                            last = pe.matmul(banks[4 + h % 2][:, j * 3 * H:(j + 1) * 3 * H], hotT[:, h % 2, j * P:(j + 1) * P],
                                             dtab[:, bass.ds(blocks[j], 1), :], start=True, stop=True)
                        last.then_inc(s_dsel, 1)
                        turn(h + 1)

        if stages == 3:
            return

        o = edge_end
        both = at(o, 2, SCAN); o += 2 * SCAN
        turned, tkey = both[:, 0, :], both[:, 1, :]
        cut = at(o, SCAN + 1); o += SCAN + 1
        fwd = at(o, SCAN); o += SCAN
        pack = at(o, 2, 2, P); o += 4 * P
        backcol = at(o, 2, P); o += 2 * P
        ends = at(o, 4); o += 4
        endrow = at(o, CHUNKS, 4)[0:H]; o += CHUNKS * 4
        eval_ = at(o, 2 * CHUNKS)[0:H]; o += 2 * CHUNKS
        ekey = at(o, 2 * CHUNKS)[0:H]; o += 2 * CHUNKS
        ecut = at(o, 2 * CHUNKS + 1)[0:H]; o += 2 * CHUNKS + 1
        efwd = at(o, 2 * CHUNKS)[0:H]; o += 2 * CHUNKS
        ebwd = at(o, 2 * CHUNKS)[0:H]; o += 2 * CHUNKS
        eback = at(o, 2); o += 2
        sums_in = at(edge_end, SLOTS, 2 * H + 1)

        s_pack = sem("tile_column_packed")
        s_ptr = sem("tile_column_turned")
        s_pcp = sem("turned_column_copied")
        s_ends = sem("chunk_ends_ready")
        s_cr = sem("chunk_ends_moved")
        s_crback = sem("chunk_maxima_ready")
        s_bk = sem("maxima_column_packed")
        s_bt = sem("maxima_column_turned")
        s_btfree = sem("maxima_column_used")
        s_dif = sem("differences_ready")
        s_exp = sem("exponentials_ready")

        def column(v, k):
            return v.rearrange("p (c k) h -> p k c h", k=PER_CHUNK)[:, bass.ds(k, 1), :, :]

        with nc.Block() as block:
            @block.sync
            def _(sp):
                sp.wait_ge(s_ends, 1)
                sp.dma_start(scratch["ends"], ends).then_inc(s_cr, 16)
                sp.wait_ge(s_cr, 16)
                sp.dma_start(endrow, scratch["ends"].rearrange("(c h) v -> h c v", h=H)).then_inc(s_cr, 16)
                sp.wait_ge(s_crback, 1)
                sp.dma_start(scratch["ends2"].rearrange("(c h) v -> h c v", h=H),
                             ebwd.rearrange("h (c v) -> h c v", v=2)).then_inc(s_cr, 16)
                sp.wait_ge(s_cr, 48)
                sp.dma_start(eback, scratch["ends2"]).then_inc(s_cr, 16)

            @block.vector
            def _(v):
                link = Chain(v, dve_step)
                keyv = key[:, :].rearrange("p (c k) -> p k c", k=PER_CHUNK)
                v.sem_inc(s_pcp, 2)
                with v.Fori(0, PER_CHUNK // 2) as i:
                    for u in range(2):
                        v.wait_ge(s_pcp, 2 * i + (u + 1))
                        link.also(v.tensor_copy(pack[:, u, 0, :].rearrange("p (c h) -> p c h", h=H),
                                                column(alpha, 2 * i + u).rearrange("p a c h -> p (a c) h")))
                        link(v.tensor_copy(pack[:, u, 1, :].rearrange("p (c h) -> p c h", h=H),
                                           keyv[:, bass.ds(2 * i + u, 1), :].rearrange("p a c -> p (a c)").unsqueeze(2).to_broadcast([P, CHUNKS, H])))
                        v.sem_inc(s_pack, 1)
                    link.close()
                v.wait_ge(s_pcp, PER_CHUNK + 2)
                link.also(v.memset(cut[:, 0:1], NEG))
                link.also(v.memset(cut[:, SCAN:], NEG))
                link(v.tensor_tensor(cut[:, 1:SCAN], tkey[:, 1:], tkey[:, 0:SCAN - 1], ALU.not_equal))
                link(v.tensor_scalar(cut[:, 1:SCAN], cut[:, 1:SCAN], NEG, None, ALU.mult))
                link(v.tensor_tensor_scan(fwd, cut[:, 0:SCAN], turned, NEG, ALU.add, ALU.max))
                link(v.tensor_tensor_scan(turned[:, ::-1], cut[:, 1:][:, ::-1], fwd[:, ::-1], NEG, ALU.add, ALU.max))
                link.also(v.tensor_copy(ends[:, 0:1], turned[:, 0:1]))
                link.also(v.tensor_copy(ends[:, 1:2], turned[:, SCAN - 1:SCAN]))
                link.also(v.tensor_copy(ends[:, 2:3], tkey[:, 0:1]))
                link(v.tensor_copy(ends[:, 3:4], tkey[:, SCAN - 1:SCAN]))
                v.sem_inc(s_ends, 1)
                v.wait_ge(s_cr, 32)
                link.also(v.tensor_copy(eval_.rearrange("h (c v) -> h c v", v=2), endrow[:, :, 0:2]))
                link.also(v.tensor_copy(ekey.rearrange("h (c v) -> h c v", v=2), endrow[:, :, 2:4]))
                link.also(v.memset(ecut[:, 0:1], NEG))
                link(v.memset(ecut[:, 2 * CHUNKS:], NEG))
                link(v.tensor_tensor(ecut[:, 1:2 * CHUNKS], ekey[:, 1:], ekey[:, 0:2 * CHUNKS - 1], ALU.not_equal))
                link(v.tensor_scalar(ecut[:, 1:2 * CHUNKS], ecut[:, 1:2 * CHUNKS], NEG, None, ALU.mult))
                link(v.tensor_tensor_scan(efwd, ecut[:, 0:2 * CHUNKS], eval_, NEG, ALU.add, ALU.max))
                link(v.tensor_tensor_scan(ebwd[:, ::-1], ecut[:, 1:][:, ::-1], efwd[:, ::-1], NEG, ALU.add, ALU.max))
                v.sem_inc(s_crback, 1)
                v.wait_ge(s_cr, 64)
                for e in range(2):
                    link(v.tensor_scalar(fwd, tkey, ends[:, 2 + e:3 + e], NEG, ALU.not_equal, ALU.mult))
                    link(v.scalar_tensor_tensor(out=turned, in0=fwd, scalar=eback[:, e:e + 1], in1=turned,
                                                op0=ALU.add, op1=ALU.max))
                link.close()
                with v.Fori(0, PER_CHUNK // 2) as i:
                    for u in range(2):
                        v.tensor_copy(backcol[:, u, :], turned[:, bass.ds((2 * i + u) * P, P)]).then_inc(s_bk, 1)
                    for u in range(2):
                        take(v, s_bt)
                        link(v.tensor_tensor(column(mx, 2 * i + u).rearrange("p a c h -> p (a c) h"),
                                             banks[4 + u][:, 0:P].rearrange("p (c h) -> p c h", h=H),
                                             column(selfe, 2 * i + u).rearrange("p a c h -> p (a c) h"), ALU.max))
                    link.close()
                link.also(v.tensor_tensor(alpha, alpha, mx, ALU.subtract))
                link.also(v.tensor_tensor(selfe, selfe, mx, ALU.subtract))
                link.also(v.memset(sums_in[:, :, 2 * H:], 1.0))
                link.close()
                v.sem_inc(s_dif, 1)
                v.wait_ge(s_exp, 2)
                link(v.tensor_tensor(alpha, sums_in[:, :, 0:H], weight[:, :].unsqueeze(2).to_broadcast([P, SLOTS, H]), ALU.mult))
                link.close()

            @block.scalar
            def _(s):
                with s.Fori(0, PER_CHUNK // 2) as i:
                    for u in range(2):
                        take(s, s_ptr)
                        s.activation(both[:, :, bass.ds((2 * i + u) * P, P)],
                                     banks[u][:, 0:2 * P].rearrange("p (v e) -> p v e", v=2), ACT.Copy).then_inc(s_pcp, 1)
                s.wait_ge(s_dif, 1)
                s.activation(sums_in[:, :, 0:H], alpha, ACT.Exp).then_inc(s_exp, 1)
                s.activation(sums_in[:, :, H:2 * H], selfe, ACT.Exp).then_inc(s_exp, 1)

            @block.tensor
            def _(pe):
                with pe.Fori(0, PER_CHUNK // 2) as i:
                    for u in range(2):
                        take(pe, s_pack)
                        for w in range(2):
                            last = pe.transpose(banks[u][:, w * P:(w + 1) * P], pack[:, u, w, :], ident[:, :])
                        last.then_inc(s_ptr, 1)
                with pe.Fori(0, PER_CHUNK // 2) as i:
                    for u in range(2):
                        take(pe, s_bk)
                        pe.transpose(banks[4 + u][:, 0:P], backcol[:, u, :], ident[:, :]).then_inc(s_bt, 1)

        if stages == 4:
            return

        o = edge_end + SLOTS * (2 * H + 1)
        xg = at(o, STEP, SUMS); o += STEP * SUMS
        idx_b = at(o, STEP, dt=u32); o += STEP
        hot5 = at(o, 2, LOT * P); o += 2 * LOT * P
        acc_at = 30000
        assert o <= acc_at
        acc = at(acc_at, BLOCKS, SUMS)
        acc_odd = at(acc_at + BLOCKS * SUMS, BLOCKS, SUMS)

        s_gb = [sem(f"source_rows_gathered{h}") for h in range(LOTS)]
        s_lot = sem("lot_weighted")
        s_sum = sem("slot_summed")
        s_sumfree = sem("slot_sum_added")
        s_idx_b = sem("source_row_numbers_ready")
        s_part = sem("partial_sums_copied")
        s_partfree = sem("partial_sums_added")
        HB = LOT // 2
        parts = at(SLOTS * H, 4, HB, SUMS)
        with nc.Block() as block:
            @block.gpsimd
            def _(g):
                gather(g, s_idx_b, s_gb, xg[:, :, 0:D], idx_b, scratch["xs"])

            @block.scalar
            def _(s):
                def row_numbers(i, h):
                    n = h % LOTS * LOT
                    s.activation(idx_b[:, n:n + LOT], src_at[:, bass.ds(i * STEP + h * LOT, LOT)], ACT.Copy).then_inc(s_idx_b, 1)

                for h in range(LOTS):
                    row_numbers(0, h)
                s.sem_inc(s_sumfree, 2)
                with s.Fori(0, STEPS) as i:
                    for h in range(LOTS):
                        for q in range(2):
                            take(s, s_partfree)
                            for j in range(HB):
                                take(s, s_sum)
                                s.activation(parts[:, 2 * (h % 2) + q, j, :], banks[HB * q + j][:, 0:SUMS], ACT.Copy).then_inc(act_step, 1)
                            take(s, act_step, HB)
                            s.sem_inc(s_sumfree, 1)
                            s.sem_inc(s_part, 1)
                        row_numbers(i, h + LOTS)

            @block.vector
            def _(v):
                v.sem_inc(s_partfree, 4)
                link = Chain(v, dve_step)
                link.also(v.memset(acc, 0.0))
                link.also(v.memset(acc_odd, 0.0))
                link.close()

                def weigh(i, h):
                    sl = bass.ds(i * STEP + h * LOT, LOT)
                    link.also(make_hot(v, hot5[:, h % 2, :], sl))
                    link.also(v.tensor_copy(xg[:, h * LOT:(h + 1) * LOT, D:], sums_in[:, sl, :]))
                    v.wait_ge(s_gb[h], (i + 1) * (16 * LOT))
                    rows = xg[:, h * LOT:(h + 1) * LOT, 0:D].rearrange("p s (h c) -> p s h c", c=C)
                    link.also(v.tensor_tensor(rows, rows, alpha[:, sl, :].unsqueeze(3).to_broadcast([P, LOT, H, C]), ALU.mult))

                def weighed():
                    link.close()
                    v.sem_inc(s_lot, 1)

                def blocks_of(i, h):
                    return numbers(nc, v, blk[0:1, bass.ds(i * STEP + h * LOT, LOT)], BLOCKS - 1)

                def add(h, blocks):
                    for j in range(LOT):
                        if j % HB == 0:
                            take(v, s_part)
                        into = (acc, acc_odd)[j % 2][:, bass.ds(blocks[j], 1), :]
                        if j >= 2:
                            v.wait_ge(dve_step, link.n - 1)
                        link.also(v.tensor_tensor(into, into, parts[:, 2 * (h % 2) + j // HB, j % HB, :], ALU.add))
                        if j % HB == HB - 1:
                            v.wait_ge(dve_step, link.n)
                            v.sem_inc(s_partfree, 1)

                with v.Fori(0, STEPS) as i:
                    weigh(i, 0)
                    weighed()
                    for h in range(1, LOTS):
                        weigh(i, h)
                        blocks = blocks_of(i, h - 1)
                        weighed()
                        add(h - 1, blocks)
                    add(LOTS - 1, blocks_of(i, LOTS - 1))
                    link.close()
                link(v.tensor_tensor(acc, acc, acc_odd, ALU.add))
                link.close()

            @block.tensor
            def _(pe):
                with pe.Fori(0, STEPS) as i:
                    for h in range(LOTS):
                        take(pe, s_lot)
                        for j in range(LOT):
                            if j % HB == 0:
                                take(pe, s_sumfree)
                            pe.matmul(banks[j][:, 0:SUMS], hot5[:, h % 2, j * P:(j + 1) * P], xg[:, h * LOT + j, :],
                                      start=True, stop=True).then_inc(s_sum, 1)

        if stages == 5:
            return


        h1 = at(0, BLOCKS, D)
        xln = at(BLOCKS * D, BLOCKS, D)
        x1 = at(2 * BLOCKS * D, BLOCKS, D)
        x0 = at(3 * BLOCKS * D, BLOCKS, D)
        o = 4 * BLOCKS * D
        stats = at(o, BLOCKS, 6); o += BLOCKS * 6
        mean = at(o, BLOCKS); o += BLOCKS
        rstd = at(o, BLOCKS); o += BLOCKS
        tmp1 = at(o, BLOCKS); o += BLOCKS
        none_in = at(o, BLOCKS); o += BLOCKS
        rcount = at(o, BLOCKS); o += BLOCKS
        wself = at(o, BLOCKS, H); o += BLOCKS * H
        rden = at(o, BLOCKS, H); o += BLOCKS * H
        fb1 = at(o, KF); o += KF
        assert o <= acc_at
        fturn = at(acc_at, KD * GROUP, P)
        fmid = at(acc_at + KD * GT, KF, GT)
        o = acc_at + BLOCKS * SUMS
        vecs = at(o, 6, D); o += 6 * D
        fw1 = at(o, KD, F); o += KD * F
        fw2 = at(o, KF, D); o += KF * D
        hs = at(o, GROUP, D); o += GROUP * D

        s_nin = sem("node_rows_loaded")
        s_fw = sem("ffn_weights_loaded")
        s_var1 = sem("ln1_variances_ready")
        s_std1 = sem("ln1_deviations_ready")
        s_hs = sem("group_normalised")
        s_ft = sem("group_turned")
        s_ftc = sem("group_turned_copied")
        s_up = sem("hidden_ready")
        s_gelu = sem("gelu_ready")
        s_down = sem("ffn_row_ready")
        s_downfree = sem("ffn_row_used")
        s_var2 = sem("ln2_variances_ready")
        s_std2 = sem("ln2_deviations_ready")
        s_var3 = sem("ln3_variances_ready")
        s_std3 = sem("ln3_deviations_ready")
        s_x1 = sem("layer_output_ready")
        s_xn = sem("normed_output_ready")
        s_x1st = sem("layer_output_stored")

        def spread(vec):
            return vec.unsqueeze(1).to_broadcast([P, BLOCKS, D])

        def all_stats(v, link, rows):
            for b in range(BLOCKS):
                link.also(v.bn_stats(stats[:, b, :], rows[:, b, :]))
            v.wait_ge(dve_step, link.n)
            return stats_to_scales(v, link, stats, mean, rstd, tmp1, 1)

        half = GT // 2
        with nc.Block() as block:
            @block.sync
            def _(sp):
                sp.dma_start(h1, scratch["xs"].rearrange("(t p) d -> p t d", p=P)).then_inc(s_nin, 16)
                sp.dma_start(xln, scratch["xln"].rearrange("(t p) d -> p t d", p=P)).then_inc(s_nin, 16)
                sp.dma_start(x0, a["x"].rearrange("(t p) d -> p t d", p=P)).then_inc(s_nin, 16)
                sp.dma_start(fw1, a["ffn_W1T"].rearrange("(k p) n -> p k n", p=P)).then_inc(s_fw, 16)
                sp.dma_start(fw2, a["ffn_W2T"].rearrange("(k p) n -> p k n", p=P)).then_inc(s_fw, 16)
                sp.wait_ge(s_x1, 1)
                sp.dma_start(scratch["x1"].rearrange("(t p) d -> p t d", p=P), x1).then_inc(s_x1st, 16)
                sp.wait_ge(s_xn, 1)
                sp.dma_start(scratch["xn"].rearrange("(t p) d -> p t d", p=P), h1).then_inc(s_x1st, 16)
                sp.wait_ge(s_x1st, 32)

            @block.scalar
            def _(s):
                for n in range(6):
                    s.dma_start(vecs[:, n, :], a["vecs"][n:n + 1, :].to_broadcast([P, D])).then_inc(s_fw, 16)
                s.dma_start(fb1, a["ffn_b1"]).then_inc(s_fw, 16)
                s.wait_ge(s_var1, 1)
                s.activation(rstd, rstd, ACT.Sqrt).then_inc(s_std1, 1)
                s.wait_ge(s_fw, 16 * 9)
                with s.Fori(0, BLOCKS // GROUP) as i:
                    for q in range(3):
                        take(s, s_ft)
                        n = min(4, KD * GROUP - 4 * q)
                        s.activation(fturn[:, 4 * q:4 * q + n, :], banks[q][:, 0:n * P].rearrange("p (n e) -> p n e", e=P),
                                     ACT.Copy).then_inc(s_ftc, 1)
                    for f in range(KF):
                        for u in range(2):
                            take(s, s_up)
                            s.activation(fmid[:, f, u * half:(u + 1) * half], banks[3 + u][:, 0:half], ACT.Gelu,
                                         bias=fb1[:, f:f + 1]).then_inc(s_gelu, 1)
                s.wait_ge(s_var2, 1)
                s.activation(rstd, rstd, ACT.Sqrt).then_inc(s_std2, 1)
                s.wait_ge(s_var3, 1)
                s.activation(rstd, rstd, ACT.Sqrt).then_inc(s_std3, 1)

            @block.vector
            def _(v):
                link = Chain(v, dve_step)
                count = acc[:, :, D + 2 * H]
                link.also(v.tensor_scalar(none_in, count, 0.0, None, ALU.is_equal))
                link(v.tensor_scalar(rcount, count, 1.0, None, ALU.max))
                link(v.reciprocal(rcount, rcount))
                link(v.tensor_tensor(wself, acc[:, :, D + H:D + 2 * H], none_in.unsqueeze(2).to_broadcast([P, BLOCKS, H]), ALU.add))
                link(v.tensor_tensor(wself, wself, rcount.unsqueeze(2).to_broadcast([P, BLOCKS, H]), ALU.mult))
                link(v.tensor_tensor(rden, acc[:, :, D:D + H], wself, ALU.add))
                link(v.reciprocal(rden, rden))
                link(v.tensor_tensor(wself, wself, rden, ALU.mult))
                sums = acc[:, :, 0:D].rearrange("p t (h c) -> p t h c", c=C)
                link.also(v.tensor_tensor(sums, sums, rden.unsqueeze(3).to_broadcast([P, BLOCKS, H, C]), ALU.mult))
                v.wait_ge(s_nin, 48)
                own = h1.rearrange("p t (h c) -> p (t h) c", c=C)
                link(v.tensor_tensor(own, own, wself.rearrange("p t h -> p (t h)").unsqueeze(2).to_broadcast([P, BLOCKS * H, C]), ALU.mult))
                link(v.tensor_tensor(h1, h1, acc[:, :, 0:D], ALU.add))
                link(v.tensor_tensor(h1, h1, xln, ALU.add))
                v.wait_ge(s_fw, 16 * 9)
                link(v.tensor_tensor(h1, h1, spread(vecs[:, 0, :]), ALU.add))
                all_stats(v, link, h1).then_inc(s_var1, 1)
                v.wait_ge(s_std1, 1)
                link(v.reciprocal(rstd, rstd))
                link.close()
                v.sem_inc(s_downfree, 2)
                with v.Fori(0, BLOCKS // GROUP) as i:
                    for j in range(GROUP):
                        b = bass.ds(i * GROUP + j, 1)
                        link.also(v.tensor_scalar(hs[:, j, :], h1[:, b, :], mean[:, b], rstd[:, b], ALU.subtract, ALU.mult))
                    v.wait_ge(dve_step, link.n)
                    link(v.tensor_tensor(hs, hs, vecs[:, 1, :].unsqueeze(1).to_broadcast([P, GROUP, D]), ALU.mult))
                    link(v.tensor_tensor(hs, hs, vecs[:, 2, :].unsqueeze(1).to_broadcast([P, GROUP, D]), ALU.add))
                    v.sem_inc(s_hs, 1)
                    for j in range(GROUP):
                        take(v, s_down)
                        link(v.tensor_tensor(x1[:, bass.ds(i * GROUP + j, 1), :], banks[5 + j % 2][:, 0:D], hs[:, j, :], ALU.add))
                        v.sem_inc(s_downfree, 1)
                    link.close()
                link(v.tensor_tensor(x1, x1, spread(vecs[:, 5, :]), ALU.add))
                all_stats(v, link, x1).then_inc(s_var2, 1)
                v.wait_ge(s_std2, 1)
                link(v.reciprocal(rstd, rstd))
                for b in range(BLOCKS):
                    link.also(v.tensor_scalar(x1[:, b, :], x1[:, b, :], mean[:, b:b + 1], rstd[:, b:b + 1], ALU.subtract, ALU.mult))
                v.wait_ge(dve_step, link.n)
                link(v.tensor_tensor(x1, x1, spread(vecs[:, 3, :]), ALU.mult))
                link(v.tensor_tensor(x1, x1, spread(vecs[:, 4, :]), ALU.add))
                link(v.tensor_tensor(x1, x1, x0, ALU.add))
                v.sem_inc(s_x1, 1)
                all_stats(v, link, x1).then_inc(s_var3, 1)
                v.wait_ge(s_std3, 1)
                link(v.reciprocal(rstd, rstd))
                for b in range(BLOCKS):
                    link.also(v.tensor_scalar(h1[:, b, :], x1[:, b, :], mean[:, b:b + 1], rstd[:, b:b + 1], ALU.subtract, ALU.mult))
                link.close()
                v.sem_inc(s_xn, 1)

            @block.tensor
            def _(pe):
                pe.wait_ge(s_fw, 16 * 9)
                with pe.Fori(0, BLOCKS // GROUP) as i:
                    take(pe, s_hs)
                    for n in range(KD * GROUP):
                        k, j = divmod(n, GROUP)
                        last = pe.transpose(banks[n // 4][:, n % 4 * P:(n % 4 + 1) * P], hs[:, j, k * P:(k + 1) * P], ident[:, :])
                        if n % 4 == 3 or n == KD * GROUP - 1:
                            last.then_inc(s_ft, 1)
                    take(pe, s_ftc, 3)
                    turned_in = fturn.rearrange("p (k j) e -> p k (j e)", k=KD)
                    for f in range(KF):
                        for u in range(2):
                            if f >= 1:
                                take(pe, s_gelu)
                            for k in range(KD):
                                last = pe.matmul(banks[3 + u][:, 0:half], fw1[:, k, f * P:(f + 1) * P],
                                                 turned_in[:, k, u * half:(u + 1) * half], start=(k == 0), stop=(k == KD - 1))
                            last.then_inc(s_up, 1)
                    take(pe, s_gelu, 2)
                    for j in range(GROUP):
                        take(pe, s_downfree)
                        for f in range(KF):
                            last = pe.matmul(banks[5 + j % 2][:, 0:D], fmid[:, f, j * P:(j + 1) * P], fw2[:, f, :],
                                             start=(f == 0), stop=(f == KF - 1))
                        last.then_inc(s_down, 1)

        if stages == 6:
            return

        xn = at(0, BLOCKS, D)
        o = BLOCKS * D
        gw = at(o, KD, EXPERTS); o += KD * EXPERTS
        gb = at(o, EXPERTS); o += EXPERTS
        gx = at(o, 2, D); o += 2 * D
        gt = at(o, 2, KD, P); o += 2 * KD * P
        logits = at(o, BLOCKS, EXPERTS); o += BLOCKS * EXPERTS
        top = at(o, BLOCKS, 8); o += BLOCKS * 8
        topi = at(o, BLOCKS, 8, dt=u32); o += BLOCKS * 8
        topf = at(o, 2, BLOCKS); o += 2 * BLOCKS
        chosen = at(o, ASSIGN, EXPERTS); o += ASSIGN * EXPERTS
        rank = at(o, ASSIGN, EXPERTS); o += ASSIGN * EXPERTS
        total = at(o, ASSIGN, EXPERTS); o += ASSIGN * EXPERTS
        upto = at(o, ASSIGN, EXPERTS); o += ASSIGN * EXPERTS
        ntile = at(o, EXPERTS); o += EXPERTS
        ntile_i = at(o, EXPERTS, dt=i32); o += EXPERTS
        cum = at(o, EXPERTS); o += EXPERTS
        base = at(o, EXPERTS); o += EXPERTS
        tileno = at(o, TILES); o += TILES
        cmp = at(o, TILES, EXPERTS); o += TILES * EXPERTS
        tile_exp = at(o, TILES); o += TILES
        posf = at(o, ASSIGN); o += ASSIGN
        zeros = at(o, GROUP, D); o += GROUP * D
        mixw = sb("mixw", [P, 2, BLOCKS])
        pos = sb("pos", [P, ASSIGN], u32)
        texp = sb("texp", [P, TILES], i32)
        pick = sb("pick", [EXPERTS, TILES])

        s_gw = sem("gate_weights_loaded")
        s_zero = sem("zeros_made")
        s_zst = sem("expert_rows_cleared")
        s_tile = sem("tile_numbers_ready")
        s_gx = sem("gate_block_ready")
        s_gt = sem("gate_block_turned")
        s_gtc = sem("gate_turned_copied")
        s_lg = sem("logits_ready")
        s_e2 = sem("second_difference_ready")
        s_e2x = sem("second_exponential_ready")
        s_chosen = sem("choices_ready")
        s_ranks = sem("ranks_ready")
        s_pos = sem("rows_assigned")
        s_scat = sem("rows_scattered")
        with nc.Block() as block:
            @block.sync
            def _(sp):
                sp.dma_start(gw, a["gate_w"].rearrange("(k p) n -> p k n", p=P)).then_inc(s_gw, 16)
                sp.dma_start(gb, a["gate_b"].to_broadcast([P, EXPERTS])).then_inc(s_gw, 16)
                sp.wait_ge(s_zero, 1)
                for n in range(TILES // GROUP):
                    sp.dma_start(scratch["xe"][n * GT:(n + 1) * GT, :].rearrange("(t p) d -> p t d", p=P), zeros).then_inc(s_zst, 16)

            @block.gpsimd
            def _(g):
                g.memset(zeros, 0.0).then_inc(s_zero, 1)
                g.iota(tileno, pattern=[[1, TILES]], base=0, channel_multiplier=0,
                       allow_small_or_imprecise_dtypes=True).then_inc(s_tile, 1)
                g.wait_ge(s_pos, 1)
                g.wait_ge(s_zst, 16 * (TILES // GROUP))
                for j in range(ASSIGN):
                    g.indirect_dma_start(out=scratch["xe"], out_offset=bass.IndirectOffsetOnAxis(ap=pos[:, j:j + 1], axis=0),
                                         in_=xn[:, j % BLOCKS, :], in_offset=None).then_inc(s_scat, 16)
                g.wait_ge(s_scat, 16 * ASSIGN)

            @block.vector
            def _(v):
                link = Chain(v, dve_step)
                v.wait_ge(s_gw, 32)
                with v.Fori(0, BLOCKS) as i:
                    b = bass.ds(i, 1)
                    v.tensor_copy(gx[:, 0, :], xn[:, b, :]).then_inc(s_gx, 1)
                    take(v, s_lg)
                    link(v.tensor_tensor(logits[:, b, :], banks[1][:, 0:EXPERTS], gb, ALU.add))
                    link.close()
                for b in range(BLOCKS):
                    link.also(v.max(top[:, b, :], logits[:, b, :]))
                v.wait_ge(dve_step, link.n)
                for b in range(BLOCKS):
                    link.also(v.max_index(topi[:, b, :], top[:, b, :], logits[:, b, :]))
                link(v.tensor_tensor(mixw[:, 1, :], top[:, :, 1], top[:, :, 0], ALU.subtract))
                v.sem_inc(s_e2, 1)
                link.also(v.tensor_copy(topf[:, 0, :], topi[:, :, 0]))
                link(v.tensor_copy(topf[:, 1, :], topi[:, :, 1]))
                link(v.tensor_tensor(chosen, lane[:, 0:EXPERTS].unsqueeze(1).to_broadcast([P, ASSIGN, EXPERTS]),
                                     topf.rearrange("p k b -> p (k b)").unsqueeze(2).to_broadcast([P, ASSIGN, EXPERTS]), ALU.is_equal))
                v.sem_inc(s_chosen, 1)
                v.wait_ge(s_e2x, 1)
                link(v.tensor_scalar(mixw[:, 0, :], mixw[:, 1, :], 1.0, None, ALU.add))
                link(v.reciprocal(mixw[:, 0, :], mixw[:, 0, :]))
                link(v.tensor_tensor(mixw[:, 1, :], mixw[:, 1, :], mixw[:, 0, :], ALU.mult))
                v.wait_ge(s_ranks, 1)
                hw = ASSIGN // 2
                for u in range(2):
                    link.also(v.tensor_copy(rank[:, u * hw:(u + 1) * hw, :], banks[2 + u][:, 0:hw * EXPERTS].rearrange("p (j e) -> p j e", e=EXPERTS)))
                    link.also(v.tensor_copy(total[:, u * hw:(u + 1) * hw, :], banks[4 + u][:, 0:hw * EXPERTS].rearrange("p (j e) -> p j e", e=EXPERTS)))
                link.also(v.memset(cmp, 1.0))
                v.wait_ge(dve_step, link.n)
                for e in range(EXPERTS):
                    link.also(v.tensor_tensor_scan(upto[:, :, e], cmp[:, 0:ASSIGN, 0], total[:, :, e], 0.0, ALU.mult, ALU.add))
                v.wait_ge(dve_step, link.n)
                link(v.tensor_scalar(ntile_i, upto[:, ASSIGN - 1, :], float(P - 1), None, ALU.add))
                link(v.tensor_single_scalar(ntile_i, ntile_i, 7, ALU.arith_shift_right))
                link(v.tensor_copy(ntile, ntile_i))
                link(v.tensor_tensor_scan(cum, cmp[:, 0, :], ntile, 0.0, ALU.mult, ALU.add))
                link(v.tensor_tensor(base, cum, ntile, ALU.subtract))
                link(v.tensor_scalar(base, base, float(P), None, ALU.mult))
                link(v.tensor_tensor(upto, upto, total, ALU.subtract))
                link(v.tensor_tensor(rank, rank, upto, ALU.add))
                link(v.tensor_tensor(rank, rank, base.unsqueeze(1).to_broadcast([P, ASSIGN, EXPERTS]), ALU.add))
                link(v.tensor_tensor(rank, rank, chosen, ALU.mult))
                link(v.tensor_reduce(posf, rank, AX, ALU.add))
                link(v.tensor_copy(pos[:, :], posf))
                v.sem_inc(s_pos, 1)
                v.wait_ge(s_tile, 1)
                link(v.tensor_tensor(cmp, cum.unsqueeze(1).to_broadcast([P, TILES, EXPERTS]),
                                     tileno.unsqueeze(2).to_broadcast([P, TILES, EXPERTS]), ALU.is_le))
                link(v.tensor_reduce(tile_exp, cmp, AX, ALU.add))
                link(v.tensor_scalar(tile_exp, tile_exp, float(EXPERTS - 1), None, ALU.min))
                link.also(v.tensor_copy(texp[:, :], tile_exp))
                link(v.tensor_scalar(pick[:, :], tile_exp[0:EXPERTS], part[0:EXPERTS, :], None, ALU.is_equal))
                link.close()

            @block.scalar
            def _(s):
                with s.Fori(0, BLOCKS) as i:
                    take(s, s_gt)
                    s.activation(gt[:, 0, :, :], banks[0][:, 0:D].rearrange("p (k n) -> p k n", k=KD), ACT.Copy).then_inc(s_gtc, 1)
                s.wait_ge(s_e2, 1)
                s.activation(mixw[:, 1, :], mixw[:, 1, :], ACT.Exp).then_inc(s_e2x, 1)

            @block.tensor
            def _(pe):
                pe.wait_ge(s_gw, 32)
                with pe.Fori(0, BLOCKS) as i:
                    take(pe, s_gx)
                    for k in range(KD):
                        last = pe.transpose(banks[0][:, k * P:(k + 1) * P], gx[:, 0, k * P:(k + 1) * P], ident[:, :])
                    last.then_inc(s_gt, 1)
                    take(pe, s_gtc)
                    for k in range(KD):
                        last = pe.matmul(banks[1][:, 0:EXPERTS], gt[:, 0, k, :], gw[:, k, :], start=(k == 0), stop=(k == KD - 1))
                    last.then_inc(s_lg, 1)
                pe.wait_ge(s_chosen, 1)
                hw = ASSIGN // 2
                for u in range(2):
                    part_of = chosen[:, u * hw:(u + 1) * hw, :].rearrange("p j e -> p (j e)")
                    pe.matmul(banks[2 + u][:, 0:hw * EXPERTS], before[:, :], part_of, start=True, stop=True)
                    last = pe.matmul(banks[4 + u][:, 0:hw * EXPERTS], ones[:, :], part_of, start=True, stop=True)
                last.then_inc(s_ranks, 1)

        if stages == 7:
            return

        o = 0
        ew1 = at(o, EXPERTS, KD * FE); o += EXPERTS * KD * FE
        ew2 = at(o, EXPERTS, KE * D); o += EXPERTS * KE * D
        ein = at(o, GROUP, D); o += GROUP * D
        eturn = at(o, 2, KD, P); o += 2 * KD * P
        ehid = at(o, 2, FE); o += 2 * FE
        ehturn = at(o, 2, KE, P); o += 2 * KE * P
        eout = at(o, GROUP, D); o += GROUP * D
        epick = at(o, 2, P)[0:EXPERTS]; o += 2 * P
        eb1 = at(o, FE)[0:EXPERTS]; o += FE
        eb2 = at(o, D)[0:EXPERTS]; o += D

        s_ew = sem("expert_weights_loaded")
        s_ein = [sem(f"expert_tile_loaded{j}") for j in range(GROUP)]
        s_einfree = [sem(f"expert_tile_used{j}") for j in range(GROUP)]
        s_epick = sem("expert_picked")
        s_et = sem("expert_tile_turned")
        s_etc = sem("expert_turned_copied")
        s_eh = sem("expert_hidden_ready")
        s_er = sem("expert_hidden_clipped")
        s_eht = sem("expert_hidden_turned")
        s_ehc = sem("expert_hidden_copied")
        s_ey = sem("expert_product_ready")
        s_eyc = [sem(f"expert_output_ready{j}") for j in range(GROUP)]
        s_eys = [sem(f"expert_output_stored{j}") for j in range(GROUP)]
        s_eofree = [sem(f"expert_output_free{j}") for j in range(GROUP)]
        EX = TILES // GROUP
        xe_t = scratch["xe"].rearrange("(t p) d -> p t d", p=P)
        ye_t = scratch["ye"].rearrange("(t p) d -> p t d", p=P)
        with nc.Block() as block:
            @block.sync
            def _(sp):
                sp.dma_start(eb1, a["eb1"]).then_inc(s_ew, 16)
                sp.dma_start(eb2, a["eb2"]).then_inc(s_ew, 16)
                for e in range(EXPERTS):
                    sp.dma_start(ew1[:, e, :].rearrange("p (k f) -> p k f", k=KD), a["ew1"][e].rearrange("(k p) f -> p k f", p=P)).then_inc(s_ew, 16)
                    sp.dma_start(ew2[:, e, :].rearrange("p (k f) -> p k f", k=KE), a["ew2"][e].rearrange("(k p) f -> p k f", p=P)).then_inc(s_ew, 16)
                with sp.Fori(0, EX) as i:
                    for j in range(GROUP):
                        take(sp, s_einfree[j])
                        sp.dma_start(ein[:, j, :], xe_t[:, bass.ds(i * GROUP + j, 1), :]).then_inc(s_ein[j], 16)

            @block.gpsimd
            def _(g):
                with g.Fori(0, EX) as i:
                    for j in range(GROUP):
                        take(g, s_eyc[j])
                        g.dma_start(ye_t[:, bass.ds(i * GROUP + j, 1), :], eout[:, j, :]).then_inc(s_eys[j], 16)
                    for j in range(GROUP):
                        g.wait_ge(s_eys[j], 16 * (i + 1))
                        g.sem_inc(s_eofree[j], 1)

            @block.vector
            def _(v):
                for j in range(GROUP):
                    v.sem_inc(s_einfree[j], 1)
                    v.sem_inc(s_eofree[j], 1)
                with v.Fori(0, EX) as i:
                    for j in range(GROUP):
                        v.tensor_copy(epick[:, j % 2, :], pick[:, bass.ds(i * GROUP + j, 1)].to_broadcast([EXPERTS, P])).then_inc(s_epick, 1)
                        take(v, s_eht)
                        v.tensor_copy(ehturn[:, j % 2, :, :].rearrange("p k n -> p (k n)"), banks[4 + j % 2][:, :]).then_inc(s_ehc, 1)
                        take(v, s_ey)
                        take(v, s_eofree[j])
                        v.sem_inc(s_einfree[j], 1)
                        v.tensor_copy(eout[:, j, :], banks[6 + j % 2][:, 0:D]).then_inc(s_eyc[j], 1)

            @block.scalar
            def _(s):
                with s.Fori(0, EX) as i:
                    for j in range(GROUP):
                        take(s, s_et)
                        s.activation(eturn[:, j % 2, :, :].rearrange("p k n -> p (k n)"), banks[j % 2][:, 0:D], ACT.Copy).then_inc(s_etc, 1)
                        take(s, s_eh)
                        s.activation(ehid[:, j % 2, :], banks[2 + j % 2][:, :], ACT.Relu).then_inc(s_er, 1)

            @block.tensor
            def _(pe):
                pe.wait_ge(s_ew, 16 * (2 + 2 * EXPERTS))
                with pe.Fori(0, EX) as i:
                    for j in range(GROUP):
                        pe.wait_ge(s_ein[j], 16 * (i + 1))
                        for k in range(KD):
                            last = pe.transpose(banks[j % 2][:, k * P:(k + 1) * P], ein[:, j, k * P:(k + 1) * P], ident[:, :])
                        last.then_inc(s_et, 1)
                        e, = numbers(nc, pe, texp[0:1, bass.ds(i * GROUP + j, 1)], EXPERTS - 1)
                        take(pe, s_epick)
                        take(pe, s_etc)
                        hid = banks[2 + j % 2][:, :]
                        pe.matmul(hid, epick[:, j % 2, :], eb1, start=True, stop=False)
                        for k in range(KD):
                            last = pe.matmul(hid, eturn[:, j % 2, k, :], ew1[:, bass.ds(e, 1), k * FE:(k + 1) * FE],
                                             start=False, stop=(k == KD - 1))
                        last.then_inc(s_eh, 1)
                        take(pe, s_er)
                        for k in range(KE):
                            last = pe.transpose(banks[4 + j % 2][:, k * P:(k + 1) * P], ehid[:, j % 2, k * P:(k + 1) * P], ident[:, :])
                        last.then_inc(s_eht, 1)
                        take(pe, s_ehc)
                        prod = banks[6 + j % 2][:, 0:D]
                        pe.matmul(prod, epick[:, j % 2, :], eb2, start=True, stop=False)
                        for k in range(KE):
                            last = pe.matmul(prod, ehturn[:, j % 2, k, :], ew2[:, bass.ds(e, 1), k * D:(k + 1) * D],
                                             start=False, stop=(k == KE - 1))
                        last.then_inc(s_ey, 1)

        if stages == 8:
            return

        ya = at(0, BLOCKS, D)
        yb = at(BLOCKS * D, BLOCKS, D)
        x1 = at(2 * BLOCKS * D, BLOCKS, D)
        xn = at(3 * BLOCKS * D, BLOCKS, D)
        o = 4 * BLOCKS * D
        stats = at(o, BLOCKS, 6); o += BLOCKS * 6
        mean = at(o, BLOCKS); o += BLOCKS
        rstd = at(o, BLOCKS); o += BLOCKS
        tmp1 = at(o, BLOCKS); o += BLOCKS
        evec = at(o, 2, D); o += 2 * D
        s_c9 = sem("combine_inputs_loaded")
        s_y = sem("expert_rows_gathered")
        s_var9 = sem("ln4_variances_ready")
        s_std9 = sem("ln4_deviations_ready")
        s_fin = sem("result_ready")
        s_out = sem("result_stored")
        whole = N_NODES // P
        with nc.Block() as block:
            @block.sync
            def _(sp):
                sp.dma_start(x1, scratch["x1"].rearrange("(t p) d -> p t d", p=P)).then_inc(s_c9, 16)
                sp.dma_start(xn, scratch["xn"].rearrange("(t p) d -> p t d", p=P)).then_inc(s_c9, 16)
                for n in range(2):
                    sp.dma_start(evec[:, n, :], a["evecs"][n:n + 1, :].to_broadcast([P, D])).then_inc(s_c9, 16)
                sp.wait_ge(s_fin, 1)
                sp.dma_start(out[0:whole * P, :].rearrange("(t p) d -> p t d", p=P), ya[:, 0:whole, :]).then_inc(s_out, 16)
                sp.dma_start(out[whole * P:, :], ya[0:N_NODES - whole * P, whole, :]).then_inc(s_out, 16)
                sp.wait_ge(s_out, 32)

            @block.gpsimd
            def _(g):
                for j in range(ASSIGN):
                    g.indirect_dma_start(out=(ya, yb)[j // BLOCKS][:, j % BLOCKS, :], out_offset=None, in_=scratch["ye"],
                                         in_offset=bass.IndirectOffsetOnAxis(ap=pos[:, j:j + 1], axis=0)).then_inc(s_y, 16)

            @block.vector
            def _(v):
                link = Chain(v, dve_step)
                v.wait_ge(s_c9, 64)
                v.wait_ge(s_y, 16 * ASSIGN)
                link.also(v.tensor_tensor(ya, ya, mixw[:, 0, :].unsqueeze(2).to_broadcast([P, BLOCKS, D]), ALU.mult))
                link(v.tensor_tensor(yb, yb, mixw[:, 1, :].unsqueeze(2).to_broadcast([P, BLOCKS, D]), ALU.mult))
                link(v.tensor_tensor(ya, ya, yb, ALU.add))
                link(v.tensor_tensor(ya, ya, xn, ALU.add))
                for b in range(BLOCKS):
                    link.also(v.bn_stats(stats[:, b, :], ya[:, b, :]))
                v.wait_ge(dve_step, link.n)
                stats_to_scales(v, link, stats, mean, rstd, tmp1, 1).then_inc(s_var9, 1)
                v.wait_ge(s_std9, 1)
                link(v.reciprocal(rstd, rstd))
                for b in range(BLOCKS):
                    link.also(v.tensor_scalar(ya[:, b, :], ya[:, b, :], mean[:, b:b + 1], rstd[:, b:b + 1], ALU.subtract, ALU.mult))
                v.wait_ge(dve_step, link.n)
                link(v.tensor_tensor(ya, ya, spread(evec[:, 0, :]), ALU.mult))
                link(v.tensor_tensor(ya, ya, spread(evec[:, 1, :]), ALU.add))
                link(v.tensor_tensor(ya, ya, x1, ALU.add))
                link.close()
                v.sem_inc(s_fin, 1)

            @block.scalar
            def _(s):
                s.wait_ge(s_var9, 1)
                s.activation(rstd, rstd, ACT.Sqrt).then_inc(s_std9, 1)


_IN = ["x", "W_srcT", "W_src", "W_dst", "att", "src", "dst", "kind", "weight"]


def kernel(**inputs):
    import numpy as np
    import concourse.bacc as bacc
    from concourse import mybir
    from concourse.bass_utils import run_bass_kernel_spmd as run

    g = {k: np.asarray(v) for k, v in inputs.items()}
    tiles = lambda v, fill: np.pad(v, (0, EDGE_TILES * P - N_EDGES), constant_values=fill).reshape(EDGE_TILES, P)
    arrays = {
        "x": np.pad(g["x"], ((0, ROWS - N_NODES), (0, 0))),
        "W_srcT": g["L0_gnn_W_src"].T, "W_src": g["L0_gnn_W_src"], "W_dst": g["L0_gnn_W_dst"],
        "att": np.concatenate([g["L0_gnn_att_src"].reshape(T, D), g["L0_gnn_att_dst"].reshape(T, D)]).T,
        "src": tiles(g["src"], 0), "dst": tiles(g["dst"], 4095),
        "kind": tiles(g["edge_type_2"], 0), "weight": tiles(g["edge_weight"], 0),
    }
    arrays.update({
        "vecs": np.stack([g["L0_gnn_" + k] for k in ("bias", "ln1_g", "ln1_b", "ln2_g", "ln2_b", "ffn_b2")]),
        "ffn_W1T": g["L0_gnn_ffn_W1"].T, "ffn_W2T": g["L0_gnn_ffn_W2"].T, "ffn_b1": g["L0_gnn_ffn_b1"].reshape(KF, P).T,
        "gate_w": g["L0_ffn_gate_w"], "gate_b": g["L0_ffn_gate_b"].reshape(1, EXPERTS),
        "ew1": g["L0_ffn_w1"], "eb1": g["L0_ffn_b1"], "ew2": g["L0_ffn_w2"], "eb2": g["L0_ffn_b2"],
        "evecs": np.stack([g["L0_ffn_gamma"], g["L0_ffn_beta"]]),
    })
    arrays = {k: np.ascontiguousarray(v) for k, v in arrays.items()}
    nc = bacc.Bacc("TRN2", target_bir_lowering=False, num_devices=1)
    a = {k: nc.dram_tensor("in_" + k, v.shape, mybir.dt.from_np(v.dtype), kind="ExternalInput").ap() for k, v in arrays.items()}
    f32 = mybir.dt.float32
    KIND = "Internal"
    scratch = {k: nc.dram_tensor(k + "_t", s, f32, kind=KIND).ap() for k, s in
               {"xs": (ROWS, D), "xln": (ROWS, D), "s": (ROWS, 2 * H), "ends": (P, 4), "ends2": (P, 2),
                "x1": (ROWS, D), "xn": (ROWS, D), "xe": (TILES * P, D), "ye": (TILES * P, D)}.items()}
    out = nc.dram_tensor("out", (N_NODES, D), f32, kind="ExternalOutput").ap()
    build(nc, a, out, scratch, 9)
    r = run(nc, [{"in_" + k: v for k, v in arrays.items()}], core_ids=[0])
    return r.results[0]["out"]
```

```python
import concourse.bass as bass
from concourse import mybir
from contextlib import ExitStack

P = 128
N_NODES = 3125
BLOCKS = -(-N_NODES // P)
ROWS = BLOCKS * P
N_EDGES = 50000
EDGE_TILES = -(-N_EDGES // P)
D = 256
KD = D // P
H, C = 8, 32
T = 2
F = 1024
KF = F // P
EXPERTS, FE = 16, 512
KE = FE // P
EPS = 1e-5
LOT = 8
LOTS = 4
STEP = LOTS * LOT
CHUNKS = P // H
PER_CHUNK = -(-(EDGE_TILES + BLOCKS) // CHUNKS)
SLOTS = CHUNKS * PER_CHUNK
STEPS = SLOTS // STEP
SLOT_GROUPS = -(-SLOTS // P)
SCAN = PER_CHUNK * P
NEG = -3.0e38
SUMS = D + 2 * H + 1
ASSIGN = 2 * BLOCKS
TURN = 6
TILES = -(-((2 * ROWS + EXPERTS * (P - 1)) // P) // TURN) * TURN
TILES_AHEAD = TILES + 2
PARTS = 3
QUAD = 32
GROUP = 5
GT = GROUP * P

fp32 = mybir.dt.float32
bf16 = mybir.dt.bfloat16
u32 = mybir.dt.uint32
i32 = mybir.dt.int32
ALU = mybir.AluOpType
ACT = mybir.ActivationFunctionType
AX = mybir.AxisListType.X


def take(eng, sem, n=1):
    eng.wait_ge(sem, n)
    eng.sem_inc(sem, -n)


class Chain:

    def __init__(self, eng, sem):
        self.eng, self.sem, self.n = eng, sem, 0

    def __call__(self, ins):
        ins.then_inc(self.sem, 1)
        self.n += 1
        self.eng.wait_ge(self.sem, self.n)

    def also(self, ins):
        ins.then_inc(self.sem, 1)
        self.n += 1

    def close(self):
        self.eng.wait_ge(self.sem, self.n)
        self.eng.sem_inc(self.sem, -self.n)
        self.n = 0


def numbers(nc, eng, row, most):
    _, got = nc.values_load_multi_w_load_instructions(
        row, engines=[eng.engine], min_val=0, max_val=most,
        skip_runtime_bounds_check_because="the numbers are clamped on the chip when they are made")
    return got


def build(nc, a, out, scratch, stages=9):
    ctx = ExitStack()
    with ctx:
        def sem(name):
            return ctx.enter_context(nc.semaphore(name))

        def sb(name, shape, dt=fp32):
            return ctx.enter_context(nc.sbuf_tensor(name, shape, dt))

        banks = [ctx.enter_context(nc.psum_tensor(f"bank{i}", [P, 512], fp32)) for i in range(8)]

        ident = sb("ident", [P, P])
        ones = sb("ones", [P, P])
        before = sb("before", [P, P])
        lane = sb("lane", [P, P])
        part = sb("part", [P, 1])
        heads = sb("heads", [P, KD, H])
        arena = sb("arena", [P, 44000])

        def at(off, *dims, dt=fp32):
            n = 1
            for d in dims:
                n *= d
            assert off + n <= 44000, (off, n)
            v = arena[:, off:off + n]
            if dt != fp32:
                v = v.bitcast(dt)
            if len(dims) == 2:
                v = v.rearrange("p (a b) -> p a b", b=dims[1])
            elif len(dims) == 3:
                v = v.rearrange("p (a b c) -> p a b c", b=dims[1], c=dims[2])
            return v

        n_sems = []
        s_const = sem("constants_made")
        pool_step = sem("pool_step")
        dve_step = sem("dve_step")
        act_step = sem("act_step")

        dtab = sb("dtab", [P, BLOCKS, 3 * H])
        xb = at(0, BLOCKS, D)
        PW = D + 4 * H
        proj = at(BLOCKS * D, BLOCKS, PW)
        xs, sd = proj[:, :, 0:D], proj[:, :, D:]
        o = BLOCKS * (D + PW)
        wv = at(o, KD, D + 4 * H); o += KD * (D + 4 * H)
        wsrc = at(o, KD, D); o += KD * D
        wdst = at(o, KD, D); o += KD * D
        att = at(o, KD, 2 * T); o += KD * 2 * T
        attm = at(o, KD, 2 * T, H); o += KD * 2 * T * H
        stats = at(o, BLOCKS, 6); o += BLOCKS * 6
        mean = at(o, BLOCKS); o += BLOCKS
        rstd = at(o, BLOCKS); o += BLOCKS
        tmp1 = at(o, BLOCKS); o += BLOCKS
        xl = at(o, GROUP, D); o += GROUP * D
        xt = at(o, GROUP, KD, P); o += GROUP * KD * P

        s_x = sem("x_loaded")
        s_w = sem("proj_weights_loaded")
        s_var = sem("variances_ready")
        s_std = sem("deviations_ready")
        s_attm = sem("masked_attention_ready")
        s_v = sem("score_vectors_ready")
        s_vc = sem("score_vectors_copied")
        s_xl = sem("block_normalised")
        s_tr = sem("block_turned")
        s_xt = sem("turned_copied")
        s_pj = sem("block_projected")
        s_pjfree = sem("projection_copied")
        s_xlfree = sem("normalised_used")
        s_projd = sem("projections_copied")

        def turn_slot(j):
            return banks[j % 3][:, 0:D].rearrange("p (k n) -> p k n", k=KD)

        s_tab = sem("tables_ready")
        s_store = sem("tables_stored")

        def stats_to_scales(v, link, st, mn, rs, t, n_out):
            link(v.tensor_tensor(mn, st[:, :, 1], st[:, :, 4], ALU.add))
            link(v.tensor_tensor(t, st[:, :, 1], st[:, :, 4], ALU.subtract))
            link(v.tensor_scalar(mn, mn, 0.5, None, ALU.mult))
            link(v.tensor_tensor(t, t, t, ALU.mult))
            link(v.tensor_tensor(rs, st[:, :, 2], st[:, :, 5], ALU.add))
            link(v.tensor_scalar(rs, rs, 1.0 / D, EPS, ALU.mult, ALU.add))
            return v.scalar_tensor_tensor(out=rs, in0=t, scalar=0.25, in1=rs, op0=ALU.mult, op1=ALU.add)

        with nc.Block() as block:
            @block.sync
            def _(sp):
                sp.dma_start(xb, a["x"].rearrange("(t p) d -> p t d", p=P)).then_inc(s_x, 16)
                sp.dma_start(wv[:, :, 0:D], a["W_srcT"].rearrange("(k p) n -> p k n", p=P)).then_inc(s_w, 16)
                sp.dma_start(wsrc, a["W_src"].rearrange("(k p) n -> p k n", p=P)).then_inc(s_w, 16)
                sp.dma_start(wdst, a["W_dst"].rearrange("(k p) n -> p k n", p=P)).then_inc(s_w, 16)
                sp.dma_start(att, a["att"].rearrange("(k p) n -> p k n", p=P)).then_inc(s_w, 16)
                sp.wait_ge(s_tab, 1)
                sp.dma_start(scratch["xs"].rearrange("(t p) d -> p t d", p=P), xs).then_inc(s_store, 16)
                sp.dma_start(scratch["xln"].rearrange("(t p) d -> p t d", p=P), xb).then_inc(s_store, 16)
                sp.dma_start(scratch["s"].rearrange("(t p) d -> p t d", p=P), sd[:, :, 0:2 * H]).then_inc(s_store, 16)
                sp.wait_ge(s_store, 48)

            @block.gpsimd
            def _(g):
                link = Chain(g, pool_step)
                link.also(g.memset(ident[:, :], 0.0))
                link.also(g.memset(ones[:, :], 1.0))
                link.also(g.memset(before[:, :], 1.0))
                link.also(g.memset(heads[:, :, :], 1.0))
                link(g.iota(lane[:, :], pattern=[[1, P]], base=0, channel_multiplier=0,
                            allow_small_or_imprecise_dtypes=True))
                link.also(g.iota(part[:, :], pattern=[[1, 1]], base=0, channel_multiplier=1,
                                 allow_small_or_imprecise_dtypes=True))
                link.also(g.affine_select(out=ident[:, :], in_=ident[:, :], compare_op=ALU.not_equal, fill=1.0,
                                          base=0, pattern=[[-1, P]], channel_multiplier=1))
                link.also(g.affine_select(out=before[:, :], in_=before[:, :], compare_op=ALU.is_gt, fill=0.0,
                                          base=0, pattern=[[1, P]], channel_multiplier=-1))
                link(g.affine_select(out=heads[:, :, :], in_=heads[:, :, :], compare_op=ALU.is_ge, fill=0.0,
                                     base=0, pattern=[[P, KD], [-C, H]], channel_multiplier=1))
                link(g.affine_select(out=heads[:, :, :], in_=heads[:, :, :], compare_op=ALU.is_ge, fill=0.0,
                                     base=C - 1, pattern=[[-P, KD], [C, H]], channel_multiplier=-1))
                link.close()
                g.sem_inc(s_const, 1)

            @block.vector
            def _(v):
                link = Chain(v, dve_step)
                v.wait_ge(s_const, 1)
                v.wait_ge(s_w, 64)
                for k in range(KD):
                    for t in range(2 * T):
                        link.also(v.tensor_scalar(attm[:, k, t, :], heads[:, k, :], att[:, k, t:t + 1], None, ALU.mult))
                link.close()
                v.sem_inc(s_attm, 1)
                v.wait_ge(s_x, 16)
                for b in range(BLOCKS):
                    link.also(v.bn_stats(stats[:, b, :], xb[:, b, :]))
                v.wait_ge(dve_step, link.n)
                stats_to_scales(v, link, stats, mean, rstd, tmp1, 1).then_inc(s_var, 1)
                v.wait_ge(s_v, 1)
                v.tensor_copy(wv[:, :, D:], banks[7][:, 0:KD * 4 * H].rearrange("p (k n) -> p k n", k=KD)).then_inc(s_vc, 1)
                v.wait_ge(s_std, 1)
                link(v.reciprocal(rstd, rstd))
                link.close()
                v.sem_inc(s_xlfree, GROUP)
                with v.Fori(0, BLOCKS // GROUP) as g:
                    for j in range(GROUP):
                        b = bass.ds(g * GROUP + j, 1)
                        take(v, s_xlfree)
                        v.tensor_scalar(xl[:, j, :], xb[:, b, :], mean[:, b], rstd[:, b],
                                        ALU.subtract, ALU.mult).then_inc(s_xl, 1)
                for b in range(BLOCKS):
                    link.also(v.tensor_scalar(xb[:, b, :], xb[:, b, :], mean[:, b:b + 1], rstd[:, b:b + 1],
                                              ALU.subtract, ALU.mult))
                v.wait_ge(s_projd, 1)
                link.also(v.tensor_copy(dtab[:, :, 0:2 * H], sd[:, :, 2 * H:4 * H]))
                link(v.tensor_tensor(dtab[:, :, 2 * H:], sd[:, :, 0:H], sd[:, :, 2 * H:3 * H], ALU.add))
                link(v.scalar_tensor_tensor(out=dtab[:, :, 2 * H:], in0=dtab[:, :, 2 * H:], scalar=0.2,
                                            in1=dtab[:, :, 2 * H:], op0=ALU.mult, op1=ALU.max))
                link.close()
                v.sem_inc(s_tab, 1)

            @block.scalar
            def _(s):
                s.wait_ge(s_var, 1)
                s.activation(rstd, rstd, ACT.Sqrt).then_inc(s_std, 1)
                def turned_copy(j):
                    take(s, s_tr)
                    s.activation(xt[:, j, :, :], turn_slot(j), ACT.Copy).then_inc(s_xt, 1)

                def projected_copy(g, j):
                    take(s, s_pj)
                    s.activation(proj[:, bass.ds(g * GROUP + j, 1), :], banks[3 + j][:, 0:PW], ACT.Copy).then_inc(s_pjfree, 1)

                with s.Fori(0, BLOCKS // GROUP) as g:
                    turned_copy(0)
                    for j in range(1, GROUP):
                        turned_copy(j)
                        projected_copy(g, j - 1)
                    projected_copy(g, GROUP - 1)
                s.wait_ge(s_pjfree, GROUP)
                s.sem_inc(s_projd, 1)

            @block.tensor
            def _(pe):
                pe.wait_ge(s_attm, 1)
                for m in range(KD):
                    for w, (wt, c0) in enumerate(((wsrc, 0), (wdst, T))):
                        for k in range(KD):
                            last = pe.matmul(banks[7][:, m * 4 * H + w * 2 * H: m * 4 * H + (w + 1) * 2 * H],
                                             wt[:, k, m * P:(m + 1) * P], attm[:, k, c0:c0 + T, :],
                                             start=(k == 0), stop=(k == KD - 1))
                last.then_inc(s_v, 1)
                pe.wait_ge(s_vc, 1)
                pe.sem_inc(s_pjfree, GROUP)

                def turn(j):
                    take(pe, s_xl)
                    for k in range(KD):
                        last = pe.transpose(turn_slot(j)[:, k, :], xl[:, j, k * P:(k + 1) * P], ident[:, :])
                    last.then_inc(s_tr, 1)

                def project(j):
                    take(pe, s_xt)
                    pe.sem_inc(s_xlfree, 1)
                    take(pe, s_pjfree)
                    for k in range(KD):
                        last = pe.matmul(banks[3 + j][:, 0:PW], xt[:, j, k, :], wv[:, k, :], start=(k == 0), stop=(k == KD - 1))
                    last.then_inc(s_pj, 1)

                with pe.Fori(0, BLOCKS // GROUP) as g:
                    turn(0)
                    for j in range(1, GROUP):
                        turn(j)
                        project(j - 1)
                    project(GROUP - 1)

        if stages == 1:
            return

        AHEAD = LOTS * LOT
        src_at = sb("src_at", [P, SLOTS + AHEAD], u32)
        srct_at = sb("srct_at", [P, SLOTS + AHEAD], u32)
        local = sb("local", [P, SLOTS + LOT])
        key = sb("key", [P, SLOTS])
        kind = sb("kind", [P, SLOTS])
        weight = sb("weight", [P, SLOTS])
        blk = sb("blk", [P, SLOTS], i32)
        o = 0
        lastrow_i = at(o, EDGE_TILES, dt=i32)[0:1, :]; o += EDGE_TILES
        lastrow = at(o, EDGE_TILES)[0:1, :]; o += EDGE_TILES
        tilerow = at(o, EDGE_TILES)[0:1, :]; o += EDGE_TILES
        junk = at(o, EDGE_TILES); o += EDGE_TILES
        slot_tile = at(o, SLOT_GROUPS); o += SLOT_GROUPS
        slot_tile_i = at(o, SLOT_GROUPS, dt=u32); o += SLOT_GROUPS
        slot_blk = at(o, SLOT_GROUPS); o += SLOT_GROUPS
        slot_off = at(o, SLOT_GROUPS); o += SLOT_GROUPS
        slot_no = at(o, SLOT_GROUPS); o += SLOT_GROUPS
        diag = at(o, SLOT_GROUPS, P); o += SLOT_GROUPS * P
        raw = [at(o + i * SLOT_GROUPS * P, SLOT_GROUPS, P, dt=dt) for i, dt in enumerate((i32, i32, i32, fp32))]
        o += 4 * SLOT_GROUPS * P
        rsrc = at(o, SLOT_GROUPS, P); o += SLOT_GROUPS * P
        rsrct = at(o, SLOT_GROUPS, P); o += SLOT_GROUPS * P
        rdst = at(o, SLOT_GROUPS, P); o += SLOT_GROUPS * P
        rkind = at(o, SLOT_GROUPS, P); o += SLOT_GROUPS * P
        rlocal = at(o, SLOT_GROUPS, P); o += SLOT_GROUPS * P
        rok = at(o, SLOT_GROUPS, P); o += SLOT_GROUPS * P
        rkey = at(o, SLOT_GROUPS, P); o += SLOT_GROUPS * P

        s_last = sem("tile_ends_loaded")
        s_iota = sem("tile_numbers_made")
        s_lrow = sem("staircase_row_ready")
        s_lbc = sem("staircase_spread")
        s_stile = sem("slot_tiles_ready")
        s_diag = sem("block_diagonals_ready")
        s_bbc = sem("blocks_spread")
        s_rec = sem("edge_rows_gathered")
        s_rows = sem("slot_rows_ready")
        s_rt = sem("slot_rows_turned")
        s_rtc = sem("turned_rows_copied")
        with nc.Block() as block:
            @block.sync
            def _(sp):
                sp.dma_start(lastrow_i, a["dst"].rearrange("(a t) e -> a t e", a=1)[:, :, P - 1],
                             allow_slow_non_contiguous=True).then_inc(s_last, 16)

            @block.gpsimd
            def _(g):
                g.iota(tilerow, pattern=[[1, EDGE_TILES]], base=0, channel_multiplier=0,
                       allow_small_or_imprecise_dtypes=True).then_inc(s_iota, 1)
                g.wait_ge(s_iota, 1)
                g.iota(slot_no, pattern=[[P, SLOT_GROUPS]], base=0, channel_multiplier=1,
                       allow_small_or_imprecise_dtypes=True).then_inc(s_iota, 1)
                g.wait_ge(s_stile, 1)
                for i, name in enumerate(("src", "dst", "kind", "weight")):
                    for q in range(SLOT_GROUPS):
                        g.indirect_dma_start(out=raw[i][:, q, :], out_offset=None, in_=a[name],
                                             in_offset=bass.IndirectOffsetOnAxis(ap=slot_tile_i[:, q:q + 1], axis=0)
                                             ).then_inc(s_rec, 16)

            @block.vector
            def _(v):
                link = Chain(v, dve_step)
                v.wait_ge(s_last, 16)
                v.wait_ge(s_iota, 2)
                link(v.tensor_single_scalar(lastrow_i, lastrow_i, 7, ALU.arith_shift_right))
                link(v.tensor_copy(lastrow, lastrow_i))
                v.tensor_tensor(lastrow, lastrow, tilerow, ALU.add).then_inc(s_lrow, 1)
                v.wait_ge(s_lbc, 1)
                for q in range(SLOT_GROUPS):
                    link(v.tensor_scalar(junk, banks[0][:, 0:EDGE_TILES], slot_no[:, q:q + 1], 0.0,
                                         ALU.is_lt, ALU.add, accum_out=slot_tile[:, q:q + 1]))
                link(v.tensor_scalar(slot_tile, slot_tile, float(EDGE_TILES - 1), None, ALU.min))
                v.tensor_copy(slot_tile_i, slot_tile).then_inc(s_stile, 1)
                link(v.tensor_tensor(slot_blk, slot_no, slot_tile, ALU.subtract))
                link(v.tensor_scalar(slot_off, slot_blk, float(P), None, ALU.mult))
                for q in range(SLOT_GROUPS):
                    link.also(v.tensor_scalar(diag[:, q, :], ident[:, :], slot_blk[:, q:q + 1], None, ALU.mult))
                link.close()
                v.sem_inc(s_diag, 1)
                v.wait_ge(s_bbc, 1)
                link(v.tensor_scalar(blk[:, :], banks[1][:, 0:SLOTS], float(BLOCKS - 1), None, ALU.min))
                v.wait_ge(s_rec, 16 * 4 * SLOT_GROUPS)
                link.also(v.tensor_copy(rsrc, raw[0]))
                link.also(v.tensor_copy(rdst, raw[1]))
                link(v.tensor_copy(rkind, raw[2]))
                link.also(v.scalar_tensor_tensor(out=rsrct, in0=rsrc, scalar=2.0, in1=rkind, op0=ALU.mult, op1=ALU.add))
                for q in range(SLOT_GROUPS):
                    link(v.tensor_scalar(rlocal[:, q, :], rdst[:, q, :], slot_off[:, q:q + 1], None, ALU.subtract))
                link(v.tensor_scalar(rok, rlocal, 0.0, None, ALU.is_ge))
                link(v.scalar_tensor_tensor(out=rok, in0=rlocal, scalar=float(P), in1=rok, op0=ALU.is_lt, op1=ALU.mult))
                link(v.scalar_tensor_tensor(out=rlocal, in0=rlocal, scalar=1.0, in1=rok, op0=ALU.add, op1=ALU.mult))
                link(v.scalar_tensor_tensor(out=rkey, in0=rdst, scalar=1.0, in1=rok, op0=ALU.add, op1=ALU.mult))
                link.also(v.tensor_scalar(rlocal, rlocal, -1.0, None, ALU.add))
                link(v.tensor_scalar(rkey, rkey, -1.0, None, ALU.add))
                link.close()
                v.sem_inc(s_rows, 1)
                link.also(v.memset(src_at[:, SLOTS:], 0))
                link.also(v.memset(srct_at[:, SLOTS:], 0))
                link.also(v.memset(local[:, SLOTS:], -1.0))
                link.close()
                for i, dst in enumerate((src_at, srct_at, local, key, kind, weight)):
                    v.wait_ge(s_rt, i + 1)
                    v.tensor_copy(dst[:, 0:SLOTS], banks[2 + i % 2][:, 0:SLOTS]).then_inc(s_rtc, 1)
                v.wait_ge(s_rtc, 6)

            @block.tensor
            def _(pe):
                pe.wait_ge(s_lrow, 1)
                pe.matmul(banks[0][:, 0:EDGE_TILES], ones[0:1, :], lastrow, start=True, stop=True).then_inc(s_lbc, 1)
                pe.wait_ge(s_diag, 1)
                pe.matmul(banks[1][:, :], ones[:, :], diag.rearrange("p q n -> p (q n)"), start=True, stop=True).then_inc(s_bbc, 1)
                pe.wait_ge(s_rows, 1)
                for i, rows in enumerate((rsrc, rsrct, rlocal, rkey, rkind, raw[3])):
                    if i >= 2:
                        pe.wait_ge(s_rtc, i - 1)
                    for q in range(SLOT_GROUPS):
                        last = pe.transpose(banks[2 + i % 2][:, q * P:(q + 1) * P], rows[:, q, :], ident[:, :])
                    last.then_inc(s_rt, 1)

        if stages == 2:
            return

        o = 0
        alpha = at(o, SLOTS, H); o += SLOTS * H
        selfe = at(o, SLOTS, H); o += SLOTS * H
        mx = at(o, SLOTS, H); o += SLOTS * H
        edge_end = o
        sg = at(o, STEP, H); o += STEP * H
        idx_a = at(o, STEP, dt=u32); o += STEP
        hot = at(o, 2, LOT * P); o += 2 * LOT * P
        hotT = at(o, 2, LOT * P); o += 2 * LOT * P
        d0 = at(o, LOT, H); o += LOT * H
        d1 = at(o, LOT, H); o += LOT * H
        nkind = at(o, SLOTS); o += SLOTS

        s_ga = [sem(f"source_terms_gathered{h}") for h in range(LOTS)]
        s_gafree = [sem(f"source_terms_used{h}") for h in range(LOTS)]
        s_idx_a = sem("source_term_numbers_ready")
        s_hot = sem("onehots_ready")
        s_hott = sem("onehots_turned")
        s_hotc = sem("turned_onehots_copied")
        s_dsel = sem("destination_terms_selected")
        s_dfree = sem("destination_terms_used")

        def make_hot(v, buf, sl):
            return v.tensor_tensor(buf.rearrange("p (s n) -> p s n", n=P),
                                   lane[:, :].unsqueeze(1).to_broadcast([P, LOT, P]),
                                   local[:, sl].unsqueeze(2).to_broadcast([P, LOT, P]), ALU.is_equal)

        def gather(g, s_idx, s_done, rows, idx, table):
            with g.Fori(0, STEPS) as i:
                for h in range(LOTS):
                    take(g, s_idx)
                    for n in range(h * LOT, (h + 1) * LOT):
                        g.indirect_dma_start(out=rows[:, n, :], out_offset=None, in_=table,
                                             in_offset=bass.IndirectOffsetOnAxis(ap=idx[:, n:n + 1], axis=0)
                                             ).then_inc(s_done[h], 16)

        def copy_numbers(s, s_free, s_idx, idx, numbers_at, i, h):
            n = h % LOTS * LOT
            take(s, s_free[h % LOTS])
            s.activation(idx[:, n:n + LOT], numbers_at[:, bass.ds(i * STEP + h * LOT, LOT)], ACT.Copy).then_inc(s_idx, 1)

        with nc.Block() as block:
            @block.gpsimd
            def _(g):
                gather(g, s_idx_a, s_ga, sg, idx_a, scratch["s"].rearrange("n (t h) -> (n t) h", t=T))

            @block.vector
            def _(v):
                link = Chain(v, dve_step)
                link(v.tensor_scalar(nkind, kind[:, :], -1.0, 1.0, ALU.mult, ALU.add))
                link.close()
                for h in range(LOTS):
                    v.sem_inc(s_gafree[h], 1)
                make_hot(v, hot[:, 0, :], bass.ds(0, LOT)).then_inc(s_hot, 1)
                with v.Fori(0, STEPS) as i:
                    for h in range(LOTS):
                        sl = bass.ds(i * STEP + h * LOT, LOT)
                        make_hot(v, hot[:, (h + 1) % 2, :], bass.ds(i * STEP + (h + 1) * LOT, LOT)).then_inc(s_hot, 1)
                        take(v, s_dsel)
                        dsel = banks[4 + h % 2][:, 0:LOT * 3 * H].rearrange("p (s n) -> p s n", n=3 * H)
                        link.also(v.tensor_copy(selfe[:, sl, :], dsel[:, :, 2 * H:]))
                        link.also(v.tensor_tensor(d0, dsel[:, :, 0:H], nkind[:, sl].unsqueeze(2).to_broadcast([P, LOT, H]), ALU.mult))
                        link(v.tensor_tensor(d1, dsel[:, :, H:2 * H], kind[:, sl].unsqueeze(2).to_broadcast([P, LOT, H]), ALU.mult))
                        v.sem_inc(s_dfree, 1)
                        link(v.tensor_tensor(d0, d0, d1, ALU.add))
                        v.wait_ge(s_ga[h], (i + 1) * (16 * LOT))
                        link(v.tensor_tensor(d0, d0, sg[:, h * LOT:(h + 1) * LOT, :], ALU.add))
                        v.sem_inc(s_gafree[h], 1)
                        link(v.scalar_tensor_tensor(out=alpha[:, sl, :], in0=d0, scalar=0.2, in1=d0, op0=ALU.mult, op1=ALU.max))
                    link.close()

            @block.scalar
            def _(s):
                def turned_copy(h):
                    for q in range(2):
                        take(s, s_hott)
                        s.activation(hotT[:, h % 2, q * 512:(q + 1) * 512], banks[2 * (h % 2) + q][:, :], ACT.Copy).then_inc(s_hotc, 1)

                for h in range(LOTS - 1):
                    copy_numbers(s, s_gafree, s_idx_a, idx_a, srct_at, 0, h)
                turned_copy(0)
                with s.Fori(0, STEPS) as i:
                    for h in range(LOTS):
                        turned_copy(h + 1)
                        copy_numbers(s, s_gafree, s_idx_a, idx_a, srct_at, i, h + LOTS - 1)

            @block.tensor
            def _(pe):
                def turn(h):
                    take(pe, s_hot)
                    for q in range(2):
                        for j in range(4):
                            last = pe.transpose(banks[2 * (h % 2) + q][:, j * P:(j + 1) * P],
                                                hot[:, h % 2, (4 * q + j) * P:(4 * q + j + 1) * P], ident[:, :])
                        last.then_inc(s_hott, 1)

                pe.sem_inc(s_dfree, 2)
                turn(0)
                with pe.Fori(0, STEPS) as i:
                    for h in range(LOTS):
                        blocks = numbers(nc, pe, blk[0:1, bass.ds(i * STEP + h * LOT, LOT)], BLOCKS - 1)
                        take(pe, s_hotc, 2)
                        take(pe, s_dfree)
                        for j in range(LOT):
                            last = pe.matmul(banks[4 + h % 2][:, j * 3 * H:(j + 1) * 3 * H], hotT[:, h % 2, j * P:(j + 1) * P],
                                             dtab[:, bass.ds(blocks[j], 1), :], start=True, stop=True)
                        last.then_inc(s_dsel, 1)
                        turn(h + 1)

        if stages == 3:
            return

        o = edge_end
        both = at(o, 2, SCAN); o += 2 * SCAN
        turned, tkey = both[:, 0, :], both[:, 1, :]
        cut = at(o, SCAN + 1); o += SCAN + 1
        fwd = at(o, SCAN); o += SCAN
        pack = at(o, 2, 2, P); o += 4 * P
        backcol = at(o, 2, P); o += 2 * P
        ends = at(o, 4); o += 4
        endrow = at(o, CHUNKS, 4)[0:H]; o += CHUNKS * 4
        eval_ = at(o, 2 * CHUNKS)[0:H]; o += 2 * CHUNKS
        ekey = at(o, 2 * CHUNKS)[0:H]; o += 2 * CHUNKS
        ecut = at(o, 2 * CHUNKS + 1)[0:H]; o += 2 * CHUNKS + 1
        efwd = at(o, 2 * CHUNKS)[0:H]; o += 2 * CHUNKS
        ebwd = at(o, 2 * CHUNKS)[0:H]; o += 2 * CHUNKS
        eback = at(o, 2); o += 2
        sums_in = at(edge_end, SLOTS, 2 * H + 1)

        s_pack = sem("tile_column_packed")
        s_ptr = sem("tile_column_turned")
        s_pcp = sem("turned_column_copied")
        s_ends = sem("chunk_ends_ready")
        s_cr = sem("chunk_ends_moved")
        s_crback = sem("chunk_maxima_ready")
        s_bk = sem("maxima_column_packed")
        s_bt = sem("maxima_column_turned")
        s_btfree = sem("maxima_column_used")
        s_dif = sem("differences_ready")
        s_exp = sem("exponentials_ready")

        def column(v, k):
            return v.rearrange("p (c k) h -> p k c h", k=PER_CHUNK)[:, bass.ds(k, 1), :, :]

        with nc.Block() as block:
            @block.sync
            def _(sp):
                sp.wait_ge(s_ends, 1)
                sp.dma_start(scratch["ends"], ends).then_inc(s_cr, 16)
                sp.wait_ge(s_cr, 16)
                sp.dma_start(endrow, scratch["ends"].rearrange("(c h) v -> h c v", h=H)).then_inc(s_cr, 16)
                sp.wait_ge(s_crback, 1)
                sp.dma_start(scratch["ends2"].rearrange("(c h) v -> h c v", h=H),
                             ebwd.rearrange("h (c v) -> h c v", v=2)).then_inc(s_cr, 16)
                sp.wait_ge(s_cr, 48)
                sp.dma_start(eback, scratch["ends2"]).then_inc(s_cr, 16)

            @block.vector
            def _(v):
                link = Chain(v, dve_step)
                keyv = key[:, :].rearrange("p (c k) -> p k c", k=PER_CHUNK)
                v.sem_inc(s_pcp, 2)
                with v.Fori(0, PER_CHUNK // 2) as i:
                    for u in range(2):
                        v.wait_ge(s_pcp, 2 * i + (u + 1))
                        link.also(v.tensor_copy(pack[:, u, 0, :].rearrange("p (c h) -> p c h", h=H),
                                                column(alpha, 2 * i + u).rearrange("p a c h -> p (a c) h")))
                        link(v.tensor_copy(pack[:, u, 1, :].rearrange("p (c h) -> p c h", h=H),
                                           keyv[:, bass.ds(2 * i + u, 1), :].rearrange("p a c -> p (a c)").unsqueeze(2).to_broadcast([P, CHUNKS, H])))
                        v.sem_inc(s_pack, 1)
                    link.close()
                v.wait_ge(s_pcp, PER_CHUNK + 2)
                link.also(v.memset(cut[:, 0:1], NEG))
                link.also(v.memset(cut[:, SCAN:], NEG))
                link(v.tensor_tensor(cut[:, 1:SCAN], tkey[:, 1:], tkey[:, 0:SCAN - 1], ALU.not_equal))
                link(v.tensor_scalar(cut[:, 1:SCAN], cut[:, 1:SCAN], NEG, None, ALU.mult))
                link(v.tensor_tensor_scan(fwd, cut[:, 0:SCAN], turned, NEG, ALU.add, ALU.max))
                link(v.tensor_tensor_scan(turned[:, ::-1], cut[:, 1:][:, ::-1], fwd[:, ::-1], NEG, ALU.add, ALU.max))
                link.also(v.tensor_copy(ends[:, 0:1], turned[:, 0:1]))
                link.also(v.tensor_copy(ends[:, 1:2], turned[:, SCAN - 1:SCAN]))
                link.also(v.tensor_copy(ends[:, 2:3], tkey[:, 0:1]))
                link(v.tensor_copy(ends[:, 3:4], tkey[:, SCAN - 1:SCAN]))
                v.sem_inc(s_ends, 1)
                v.wait_ge(s_cr, 32)
                link.also(v.tensor_copy(eval_.rearrange("h (c v) -> h c v", v=2), endrow[:, :, 0:2]))
                link.also(v.tensor_copy(ekey.rearrange("h (c v) -> h c v", v=2), endrow[:, :, 2:4]))
                link.also(v.memset(ecut[:, 0:1], NEG))
                link(v.memset(ecut[:, 2 * CHUNKS:], NEG))
                link(v.tensor_tensor(ecut[:, 1:2 * CHUNKS], ekey[:, 1:], ekey[:, 0:2 * CHUNKS - 1], ALU.not_equal))
                link(v.tensor_scalar(ecut[:, 1:2 * CHUNKS], ecut[:, 1:2 * CHUNKS], NEG, None, ALU.mult))
                link(v.tensor_tensor_scan(efwd, ecut[:, 0:2 * CHUNKS], eval_, NEG, ALU.add, ALU.max))
                link(v.tensor_tensor_scan(ebwd[:, ::-1], ecut[:, 1:][:, ::-1], efwd[:, ::-1], NEG, ALU.add, ALU.max))
                v.sem_inc(s_crback, 1)
                v.wait_ge(s_cr, 64)
                for e in range(2):
                    link(v.tensor_scalar(fwd, tkey, ends[:, 2 + e:3 + e], NEG, ALU.not_equal, ALU.mult))
                    link(v.scalar_tensor_tensor(out=turned, in0=fwd, scalar=eback[:, e:e + 1], in1=turned,
                                                op0=ALU.add, op1=ALU.max))
                link.close()
                with v.Fori(0, PER_CHUNK // 2) as i:
                    for u in range(2):
                        v.tensor_copy(backcol[:, u, :], turned[:, bass.ds((2 * i + u) * P, P)]).then_inc(s_bk, 1)
                    for u in range(2):
                        take(v, s_bt)
                        link(v.tensor_tensor(column(mx, 2 * i + u).rearrange("p a c h -> p (a c) h"),
                                             banks[4 + u][:, 0:P].rearrange("p (c h) -> p c h", h=H),
                                             column(selfe, 2 * i + u).rearrange("p a c h -> p (a c) h"), ALU.max))
                    link.close()
                link.also(v.tensor_tensor(alpha, alpha, mx, ALU.subtract))
                link.also(v.tensor_tensor(selfe, selfe, mx, ALU.subtract))
                link.also(v.memset(sums_in[:, :, 2 * H:], 1.0))
                link.close()
                v.sem_inc(s_dif, 1)
                v.wait_ge(s_exp, 2)
                link(v.tensor_tensor(alpha, sums_in[:, :, 0:H], weight[:, :].unsqueeze(2).to_broadcast([P, SLOTS, H]), ALU.mult))
                link.close()

            @block.scalar
            def _(s):
                with s.Fori(0, PER_CHUNK // 2) as i:
                    for u in range(2):
                        take(s, s_ptr)
                        s.activation(both[:, :, bass.ds((2 * i + u) * P, P)],
                                     banks[u][:, 0:2 * P].rearrange("p (v e) -> p v e", v=2), ACT.Copy).then_inc(s_pcp, 1)
                s.wait_ge(s_dif, 1)
                s.activation(sums_in[:, :, 0:H], alpha, ACT.Exp).then_inc(s_exp, 1)
                s.activation(sums_in[:, :, H:2 * H], selfe, ACT.Exp).then_inc(s_exp, 1)

            @block.tensor
            def _(pe):
                with pe.Fori(0, PER_CHUNK // 2) as i:
                    for u in range(2):
                        take(pe, s_pack)
                        for w in range(2):
                            last = pe.transpose(banks[u][:, w * P:(w + 1) * P], pack[:, u, w, :], ident[:, :])
                        last.then_inc(s_ptr, 1)
                with pe.Fori(0, PER_CHUNK // 2) as i:
                    for u in range(2):
                        take(pe, s_bk)
                        pe.transpose(banks[4 + u][:, 0:P], backcol[:, u, :], ident[:, :]).then_inc(s_bt, 1)

        if stages == 4:
            return

        o = edge_end + SLOTS * (2 * H + 1)
        xg = at(o, STEP, SUMS); o += STEP * SUMS
        idx_b = at(o, STEP, dt=u32); o += STEP
        hot5 = at(o, 2, LOT * P); o += 2 * LOT * P
        acc_at = 30000
        assert o <= acc_at
        acc = at(acc_at, BLOCKS, SUMS)
        acc_odd = at(acc_at + BLOCKS * SUMS, BLOCKS, SUMS)

        s_gb = [sem(f"source_rows_gathered{h}") for h in range(LOTS)]
        s_lot = sem("lot_weighted")
        s_sum = sem("slot_summed")
        s_sumfree = sem("slot_sum_added")
        s_idx_b = sem("source_row_numbers_ready")
        s_part = sem("partial_sums_copied")
        s_partfree = sem("partial_sums_added")
        HB = LOT // 2
        parts = at(SLOTS * H, 4, HB, SUMS)
        with nc.Block() as block:
            @block.gpsimd
            def _(g):
                gather(g, s_idx_b, s_gb, xg[:, :, 0:D], idx_b, scratch["xs"])

            @block.scalar
            def _(s):
                def row_numbers(i, h):
                    n = h % LOTS * LOT
                    s.activation(idx_b[:, n:n + LOT], src_at[:, bass.ds(i * STEP + h * LOT, LOT)], ACT.Copy).then_inc(s_idx_b, 1)

                for h in range(LOTS):
                    row_numbers(0, h)
                s.sem_inc(s_sumfree, 2)
                with s.Fori(0, STEPS) as i:
                    for h in range(LOTS):
                        for q in range(2):
                            take(s, s_partfree)
                            for j in range(HB):
                                take(s, s_sum)
                                s.activation(parts[:, 2 * (h % 2) + q, j, :], banks[HB * q + j][:, 0:SUMS], ACT.Copy).then_inc(act_step, 1)
                            take(s, act_step, HB)
                            s.sem_inc(s_sumfree, 1)
                            s.sem_inc(s_part, 1)
                        row_numbers(i, h + LOTS)

            @block.vector
            def _(v):
                v.sem_inc(s_partfree, 4)
                link = Chain(v, dve_step)
                link.also(v.memset(acc, 0.0))
                link.also(v.memset(acc_odd, 0.0))
                link.close()

                def weigh(i, h):
                    sl = bass.ds(i * STEP + h * LOT, LOT)
                    link.also(make_hot(v, hot5[:, h % 2, :], sl))
                    link.also(v.tensor_copy(xg[:, h * LOT:(h + 1) * LOT, D:], sums_in[:, sl, :]))
                    v.wait_ge(s_gb[h], (i + 1) * (16 * LOT))
                    rows = xg[:, h * LOT:(h + 1) * LOT, 0:D].rearrange("p s (h c) -> p s h c", c=C)
                    link.also(v.tensor_tensor(rows, rows, alpha[:, sl, :].unsqueeze(3).to_broadcast([P, LOT, H, C]), ALU.mult))

                def weighed():
                    link.close()
                    v.sem_inc(s_lot, 1)

                def blocks_of(i, h):
                    return numbers(nc, v, blk[0:1, bass.ds(i * STEP + h * LOT, LOT)], BLOCKS - 1)

                def add(h, blocks):
                    for j in range(LOT):
                        if j % HB == 0:
                            take(v, s_part)
                        into = (acc, acc_odd)[j % 2][:, bass.ds(blocks[j], 1), :]
                        if j >= 2:
                            v.wait_ge(dve_step, link.n - 1)
                        link.also(v.tensor_tensor(into, into, parts[:, 2 * (h % 2) + j // HB, j % HB, :], ALU.add))
                        if j % HB == HB - 1:
                            v.wait_ge(dve_step, link.n)
                            v.sem_inc(s_partfree, 1)

                with v.Fori(0, STEPS) as i:
                    weigh(i, 0)
                    weighed()
                    for h in range(1, LOTS):
                        weigh(i, h)
                        blocks = blocks_of(i, h - 1)
                        weighed()
                        add(h - 1, blocks)
                    add(LOTS - 1, blocks_of(i, LOTS - 1))
                    link.close()
                link(v.tensor_tensor(acc, acc, acc_odd, ALU.add))
                link.close()

            @block.tensor
            def _(pe):
                with pe.Fori(0, STEPS) as i:
                    for h in range(LOTS):
                        take(pe, s_lot)
                        for j in range(LOT):
                            if j % HB == 0:
                                take(pe, s_sumfree)
                            pe.matmul(banks[j][:, 0:SUMS], hot5[:, h % 2, j * P:(j + 1) * P], xg[:, h * LOT + j, :],
                                      start=True, stop=True).then_inc(s_sum, 1)

        if stages == 5:
            return


        h1 = at(0, BLOCKS, D)
        xln = at(BLOCKS * D, BLOCKS, D)
        x1 = at(2 * BLOCKS * D, BLOCKS, D)
        x0 = at(3 * BLOCKS * D, BLOCKS, D)
        o = 4 * BLOCKS * D
        stats = at(o, BLOCKS, 6); o += BLOCKS * 6
        mean = at(o, BLOCKS); o += BLOCKS
        rstd = at(o, BLOCKS); o += BLOCKS
        tmp1 = at(o, BLOCKS); o += BLOCKS
        none_in = at(o, BLOCKS); o += BLOCKS
        rcount = at(o, BLOCKS); o += BLOCKS
        wself = at(o, BLOCKS, H); o += BLOCKS * H
        rden = at(o, BLOCKS, H); o += BLOCKS * H
        fb1 = at(o, KF); o += KF
        assert o <= acc_at
        fturn = at(acc_at, KD * GROUP, P)
        fmid = at(acc_at + KD * GT, KF, GT)
        o = acc_at + BLOCKS * SUMS
        vecs = at(o, 6, D); o += 6 * D
        fw1 = at(o, KD, F); o += KD * F
        fw2 = at(o, KF, D); o += KF * D
        hs = at(o, GROUP, D); o += GROUP * D

        s_nin = sem("node_rows_loaded")
        s_fw = sem("ffn_weights_loaded")
        s_var1 = sem("ln1_variances_ready")
        s_std1 = sem("ln1_deviations_ready")
        s_hs = sem("group_normalised")
        s_ft = sem("group_turned")
        s_ftc = sem("group_turned_copied")
        s_up = sem("hidden_ready")
        s_gelu = sem("gelu_ready")
        s_down = sem("ffn_row_ready")
        s_downfree = sem("ffn_row_used")
        s_var2 = sem("ln2_variances_ready")
        s_std2 = sem("ln2_deviations_ready")
        s_var3 = sem("ln3_variances_ready")
        s_std3 = sem("ln3_deviations_ready")
        s_x1 = sem("layer_output_ready")
        s_xn = sem("normed_output_ready")
        s_x1st = sem("layer_output_stored")

        def spread(vec):
            return vec.unsqueeze(1).to_broadcast([P, BLOCKS, D])

        def all_stats(v, link, rows):
            for b in range(BLOCKS):
                link.also(v.bn_stats(stats[:, b, :], rows[:, b, :]))
            v.wait_ge(dve_step, link.n)
            return stats_to_scales(v, link, stats, mean, rstd, tmp1, 1)

        half = GT // 2
        with nc.Block() as block:
            @block.sync
            def _(sp):
                sp.dma_start(h1, scratch["xs"].rearrange("(t p) d -> p t d", p=P)).then_inc(s_nin, 16)
                sp.dma_start(xln, scratch["xln"].rearrange("(t p) d -> p t d", p=P)).then_inc(s_nin, 16)
                sp.dma_start(x0, a["x"].rearrange("(t p) d -> p t d", p=P)).then_inc(s_nin, 16)
                sp.dma_start(fw1, a["ffn_W1T"].rearrange("(k p) n -> p k n", p=P)).then_inc(s_fw, 16)
                sp.dma_start(fw2, a["ffn_W2T"].rearrange("(k p) n -> p k n", p=P)).then_inc(s_fw, 16)
                sp.wait_ge(s_x1, 1)
                sp.dma_start(scratch["x1"].rearrange("(t p) d -> p t d", p=P), x1).then_inc(s_x1st, 16)
                sp.wait_ge(s_xn, 1)
                sp.dma_start(scratch["xn"].rearrange("(t p) d -> p t d", p=P), h1).then_inc(s_x1st, 16)
                sp.wait_ge(s_x1st, 32)

            @block.scalar
            def _(s):
                for n in range(6):
                    s.dma_start(vecs[:, n, :], a["vecs"][n:n + 1, :].to_broadcast([P, D])).then_inc(s_fw, 16)
                s.dma_start(fb1, a["ffn_b1"]).then_inc(s_fw, 16)
                s.wait_ge(s_var1, 1)
                s.activation(rstd, rstd, ACT.Sqrt).then_inc(s_std1, 1)
                s.wait_ge(s_fw, 16 * 9)
                with s.Fori(0, BLOCKS // GROUP) as i:
                    for q in range(3):
                        take(s, s_ft)
                        n = min(4, KD * GROUP - 4 * q)
                        s.activation(fturn[:, 4 * q:4 * q + n, :], banks[q][:, 0:n * P].rearrange("p (n e) -> p n e", e=P),
                                     ACT.Copy).then_inc(s_ftc, 1)
                    for f in range(KF):
                        for u in range(2):
                            take(s, s_up)
                            s.activation(fmid[:, f, u * half:(u + 1) * half], banks[3 + u][:, 0:half], ACT.Gelu,
                                         bias=fb1[:, f:f + 1]).then_inc(s_gelu, 1)
                s.wait_ge(s_var2, 1)
                s.activation(rstd, rstd, ACT.Sqrt).then_inc(s_std2, 1)
                s.wait_ge(s_var3, 1)
                s.activation(rstd, rstd, ACT.Sqrt).then_inc(s_std3, 1)

            @block.vector
            def _(v):
                link = Chain(v, dve_step)
                count = acc[:, :, D + 2 * H]
                link.also(v.tensor_scalar(none_in, count, 0.0, None, ALU.is_equal))
                link(v.tensor_scalar(rcount, count, 1.0, None, ALU.max))
                link(v.reciprocal(rcount, rcount))
                link(v.tensor_tensor(wself, acc[:, :, D + H:D + 2 * H], none_in.unsqueeze(2).to_broadcast([P, BLOCKS, H]), ALU.add))
                link(v.tensor_tensor(wself, wself, rcount.unsqueeze(2).to_broadcast([P, BLOCKS, H]), ALU.mult))
                link(v.tensor_tensor(rden, acc[:, :, D:D + H], wself, ALU.add))
                link(v.reciprocal(rden, rden))
                link(v.tensor_tensor(wself, wself, rden, ALU.mult))
                sums = acc[:, :, 0:D].rearrange("p t (h c) -> p t h c", c=C)
                link.also(v.tensor_tensor(sums, sums, rden.unsqueeze(3).to_broadcast([P, BLOCKS, H, C]), ALU.mult))
                v.wait_ge(s_nin, 48)
                own = h1.rearrange("p t (h c) -> p (t h) c", c=C)
                link(v.tensor_tensor(own, own, wself.rearrange("p t h -> p (t h)").unsqueeze(2).to_broadcast([P, BLOCKS * H, C]), ALU.mult))
                link(v.tensor_tensor(h1, h1, acc[:, :, 0:D], ALU.add))
                link(v.tensor_tensor(h1, h1, xln, ALU.add))
                v.wait_ge(s_fw, 16 * 9)
                link(v.tensor_tensor(h1, h1, spread(vecs[:, 0, :]), ALU.add))
                all_stats(v, link, h1).then_inc(s_var1, 1)
                v.wait_ge(s_std1, 1)
                link(v.reciprocal(rstd, rstd))
                link.close()
                v.sem_inc(s_downfree, 2)
                with v.Fori(0, BLOCKS // GROUP) as i:
                    for j in range(GROUP):
                        b = bass.ds(i * GROUP + j, 1)
                        link.also(v.tensor_scalar(hs[:, j, :], h1[:, b, :], mean[:, b], rstd[:, b], ALU.subtract, ALU.mult))
                    v.wait_ge(dve_step, link.n)
                    link(v.tensor_tensor(hs, hs, vecs[:, 1, :].unsqueeze(1).to_broadcast([P, GROUP, D]), ALU.mult))
                    link(v.tensor_tensor(hs, hs, vecs[:, 2, :].unsqueeze(1).to_broadcast([P, GROUP, D]), ALU.add))
                    v.sem_inc(s_hs, 1)
                    for j in range(GROUP):
                        take(v, s_down)
                        link(v.tensor_tensor(x1[:, bass.ds(i * GROUP + j, 1), :], banks[5 + j % 2][:, 0:D], hs[:, j, :], ALU.add))
                        v.sem_inc(s_downfree, 1)
                    link.close()
                link(v.tensor_tensor(x1, x1, spread(vecs[:, 5, :]), ALU.add))
                all_stats(v, link, x1).then_inc(s_var2, 1)
                v.wait_ge(s_std2, 1)
                link(v.reciprocal(rstd, rstd))
                for b in range(BLOCKS):
                    link.also(v.tensor_scalar(x1[:, b, :], x1[:, b, :], mean[:, b:b + 1], rstd[:, b:b + 1], ALU.subtract, ALU.mult))
                v.wait_ge(dve_step, link.n)
                link(v.tensor_tensor(x1, x1, spread(vecs[:, 3, :]), ALU.mult))
                link(v.tensor_tensor(x1, x1, spread(vecs[:, 4, :]), ALU.add))
                link(v.tensor_tensor(x1, x1, x0, ALU.add))
                v.sem_inc(s_x1, 1)
                all_stats(v, link, x1).then_inc(s_var3, 1)
                v.wait_ge(s_std3, 1)
                link(v.reciprocal(rstd, rstd))
                for b in range(BLOCKS):
                    link.also(v.tensor_scalar(h1[:, b, :], x1[:, b, :], mean[:, b:b + 1], rstd[:, b:b + 1], ALU.subtract, ALU.mult))
                link.close()
                v.sem_inc(s_xn, 1)

            @block.tensor
            def _(pe):
                pe.wait_ge(s_fw, 16 * 9)
                with pe.Fori(0, BLOCKS // GROUP) as i:
                    take(pe, s_hs)
                    for n in range(KD * GROUP):
                        k, j = divmod(n, GROUP)
                        last = pe.transpose(banks[n // 4][:, n % 4 * P:(n % 4 + 1) * P], hs[:, j, k * P:(k + 1) * P], ident[:, :])
                        if n % 4 == 3 or n == KD * GROUP - 1:
                            last.then_inc(s_ft, 1)
                    take(pe, s_ftc, 3)
                    turned_in = fturn.rearrange("p (k j) e -> p k (j e)", k=KD)
                    for f in range(KF):
                        for u in range(2):
                            if f >= 1:
                                take(pe, s_gelu)
                            for k in range(KD):
                                last = pe.matmul(banks[3 + u][:, 0:half], fw1[:, k, f * P:(f + 1) * P],
                                                 turned_in[:, k, u * half:(u + 1) * half], start=(k == 0), stop=(k == KD - 1))
                            last.then_inc(s_up, 1)
                    take(pe, s_gelu, 2)
                    for j in range(GROUP):
                        take(pe, s_downfree)
                        for f in range(KF):
                            last = pe.matmul(banks[5 + j % 2][:, 0:D], fmid[:, f, j * P:(j + 1) * P], fw2[:, f, :],
                                             start=(f == 0), stop=(f == KF - 1))
                        last.then_inc(s_down, 1)

        if stages == 6:
            return

        xn = at(0, BLOCKS, D)
        o = BLOCKS * D
        gw = at(o, KD, EXPERTS); o += KD * EXPERTS
        gb = at(o, EXPERTS); o += EXPERTS
        cmp = at(o, TILES_AHEAD, EXPERTS); o += TILES_AHEAD * EXPERTS
        logits = at(o, BLOCKS, EXPERTS); o += BLOCKS * EXPERTS
        top = at(o, BLOCKS, 8); o += BLOCKS * 8
        topi = at(o, BLOCKS, 8, dt=u32); o += BLOCKS * 8
        topf = at(o, 2, BLOCKS); o += 2 * BLOCKS
        chosen = at(o, ASSIGN, EXPERTS); o += ASSIGN * EXPERTS
        upto = at(o, ASSIGN, EXPERTS); o += ASSIGN * EXPERTS
        ntile = at(o, EXPERTS); o += EXPERTS
        ntile_i = at(o, EXPERTS, dt=i32); o += EXPERTS
        cum = at(o, EXPERTS); o += EXPERTS
        base = at(o, EXPERTS); o += EXPERTS
        tileno = at(o, TILES_AHEAD); o += TILES_AHEAD
        tile_exp = at(o, TILES_AHEAD); o += TILES_AHEAD
        posf = at(o, ASSIGN); o += ASSIGN
        zeros = at(o, D); o += D
        inpart = at(o, 1); o += 1
        gxr = at(BLOCKS * D + KD * EXPERTS + EXPERTS, GROUP, D)
        gtr = at(BLOCKS * D + KD * EXPERTS + EXPERTS + GROUP * D, GROUP, KD, P)
        ew_at = 44000 - EXPERTS * (KD * FE + KE * D)
        assert o <= ew_at
        ew1 = at(ew_at, EXPERTS, KD * FE)
        ew2 = at(ew_at + EXPERTS * KD * FE, EXPERTS, KE * D)
        mixw = sb("mixw", [P, 2, BLOCKS])
        pos = sb("pos", [P, ASSIGN], u32)
        texp = sb("texp", [P, TILES_AHEAD], i32)
        pick = sb("pick", [PARTS * QUAD, TILES_AHEAD], bf16)

        s_gw = sem("gate_weights_loaded")
        s_zero = sem("zeros_made")
        s_zst = sem("expert_rows_cleared")
        s_tile = sem("tile_numbers_ready")
        s_gx = sem("gate_block_ready")
        s_gxfree = sem("gate_block_used")
        s_gt = sem("gate_block_turned")
        s_gtc = sem("gate_turned_copied")
        s_lg = sem("logits_ready")
        s_e2 = sem("second_difference_ready")
        s_e2x = sem("second_exponential_ready")
        s_chosen = sem("choices_ready")
        s_ranks = sem("ranks_ready")
        s_pos = sem("rows_assigned")
        s_scat = sem("rows_scattered")
        s_ew = sem("expert_weights_loaded")
        s_gates = sem("gate_steps_done")
        CLEAR = 4

        def gate_turn(j):
            return banks[5 + j % 3][:, 0:D].rearrange("p (k n) -> p k n", k=KD)

        with nc.Block() as block:
            @block.sync
            def _(sp):
                sp.dma_start(gw, a["gate_w"].rearrange("(k p) n -> p k n", p=P)).then_inc(s_gw, 16)
                sp.dma_start(gb, a["gate_b"].to_broadcast([P, EXPERTS])).then_inc(s_gw, 16)
                sp.wait_ge(s_zero, 1)
                for n in range(TILES_AHEAD // CLEAR):
                    sp.dma_start(scratch["xe"][n * CLEAR * P:(n + 1) * CLEAR * P, :].rearrange("(t p) d -> p t d", p=P),
                                 zeros.unsqueeze(1).to_broadcast([P, CLEAR, D])).then_inc(s_zst, 16)
                for e in range(EXPERTS):
                    sp.dma_start(ew1[:, e, :].rearrange("p (k f) -> p k f", k=KD), a["ew1"][e].rearrange("(k p) f -> p k f", p=P)).then_inc(s_ew, 16)
                    sp.dma_start(ew2[:, e, :].rearrange("p (k f) -> p k f", k=KE), a["ew2"][e].rearrange("(k p) f -> p k f", p=P)).then_inc(s_ew, 16)

            @block.gpsimd
            def _(g):
                g.memset(zeros, 0.0).then_inc(s_zero, 1)
                g.iota(tileno, pattern=[[1, TILES_AHEAD]], base=0, channel_multiplier=0,
                       allow_small_or_imprecise_dtypes=True).then_inc(s_tile, 1)
                g.wait_ge(s_zst, 16 * (TILES_AHEAD // CLEAR))
                g.wait_ge(s_pos, 1)
                for j in range(ASSIGN):
                    g.indirect_dma_start(out=scratch["xe"], out_offset=bass.IndirectOffsetOnAxis(ap=pos[:, j:j + 1], axis=0),
                                         in_=xn[:, j % BLOCKS, :], in_offset=None).then_inc(s_scat, 16)
                g.wait_ge(s_scat, 16 * ASSIGN)

            @block.vector
            def _(v):
                link = Chain(v, dve_step)
                v.sem_inc(s_gxfree, GROUP)
                v.wait_ge(s_gw, 32)
                with v.Fori(0, BLOCKS // GROUP) as i:
                    for j in range(GROUP):
                        take(v, s_gxfree)
                        v.tensor_copy(gxr[:, j, :], xn[:, bass.ds(i * GROUP + j, 1), :]).then_inc(s_gx, 1)
                v.wait_ge(s_lg, 1)
                link(v.tensor_tensor(logits, banks[1][:, 0:BLOCKS * EXPERTS].rearrange("p (b e) -> p b e", e=EXPERTS),
                                     gb.unsqueeze(1).to_broadcast([P, BLOCKS, EXPERTS]), ALU.add))
                for b in range(BLOCKS):
                    link.also(v.max(top[:, b, :], logits[:, b, :]))
                v.wait_ge(dve_step, link.n)
                for b in range(BLOCKS):
                    link.also(v.max_index(topi[:, b, :], top[:, b, :], logits[:, b, :]))
                link(v.tensor_tensor(mixw[:, 1, :], top[:, :, 1], top[:, :, 0], ALU.subtract))
                v.sem_inc(s_e2, 1)
                link.also(v.tensor_copy(topf[:, 0, :], topi[:, :, 0]))
                link(v.tensor_copy(topf[:, 1, :], topi[:, :, 1]))
                link(v.tensor_tensor(chosen, lane[:, 0:EXPERTS].unsqueeze(1).to_broadcast([P, ASSIGN, EXPERTS]),
                                     topf.rearrange("p k b -> p (k b)").unsqueeze(2).to_broadcast([P, ASSIGN, EXPERTS]), ALU.is_equal))
                v.sem_inc(s_chosen, 1)
                link(v.memset(cmp, 1.0))
                v.wait_ge(s_e2x, 1)
                link(v.tensor_scalar(mixw[:, 0, :], mixw[:, 1, :], 1.0, None, ALU.add))
                link(v.reciprocal(mixw[:, 0, :], mixw[:, 0, :]))
                link.also(v.tensor_tensor(mixw[:, 1, :], mixw[:, 1, :], mixw[:, 0, :], ALU.mult))
                v.wait_ge(s_ranks, 1)
                hw = ASSIGN // 2

                def in_psum(n, u):
                    return banks[n + u][:, 0:hw * EXPERTS].rearrange("p (j e) -> p j e", e=EXPERTS)

                for e in range(EXPERTS):
                    link.also(v.tensor_tensor_scan(upto[:, 0:hw, e], cmp[:, 0:hw, 0], in_psum(4, 0)[:, :, e], 0.0, ALU.mult, ALU.add))
                v.wait_ge(dve_step, link.n)
                for e in range(EXPERTS):
                    link.also(v.tensor_tensor_scan(upto[:, hw:, e], cmp[:, 0:hw, 0], in_psum(4, 1)[:, :, e],
                                                   upto[:, hw - 1, e:e + 1], ALU.mult, ALU.add))
                v.wait_ge(dve_step, link.n)
                link(v.tensor_scalar(ntile_i, upto[:, ASSIGN - 1, :], float(P - 1), None, ALU.add))
                link(v.tensor_single_scalar(ntile_i, ntile_i, 7, ALU.arith_shift_right))
                link(v.tensor_copy(ntile, ntile_i))
                link(v.tensor_tensor_scan(cum, cmp[:, 0, :], ntile, 0.0, ALU.mult, ALU.add))
                link(v.tensor_tensor(base, cum, ntile, ALU.subtract))
                link(v.tensor_scalar(base, base, float(P), None, ALU.mult))
                for n, op in ((4, ALU.subtract), (2, ALU.add)):
                    for u in range(2):
                        cols = upto[:, u * hw:(u + 1) * hw, :]
                        link(v.tensor_tensor(cols, cols, in_psum(n, u), op))
                link(v.tensor_tensor(upto, upto, base.unsqueeze(1).to_broadcast([P, ASSIGN, EXPERTS]), ALU.add))
                link(v.tensor_tensor(upto, upto, chosen, ALU.mult))
                link(v.tensor_reduce(posf, upto, AX, ALU.add))
                link(v.tensor_copy(pos[:, :], posf))
                v.sem_inc(s_pos, 1)
                v.wait_ge(s_tile, 1)
                link(v.tensor_tensor(cmp, cum.unsqueeze(1).to_broadcast([P, TILES_AHEAD, EXPERTS]),
                                     tileno.unsqueeze(2).to_broadcast([P, TILES_AHEAD, EXPERTS]), ALU.is_le))
                link(v.tensor_reduce(tile_exp, cmp, AX, ALU.add))
                link(v.tensor_scalar(tile_exp, tile_exp, float(EXPERTS - 1), None, ALU.min))
                link.also(v.tensor_copy(texp[:, :], tile_exp))
                link(v.tensor_copy(inpart, part[:, :]))
                for n in range(1, PARTS):
                    rows = inpart[n * QUAD:(n + 1) * QUAD]
                    link.also(v.tensor_scalar(rows, rows, -float(n * QUAD), None, ALU.add))
                v.wait_ge(dve_step, link.n)
                link(v.tensor_scalar(pick[:, :], tile_exp[0:PARTS * QUAD], inpart[0:PARTS * QUAD], None, ALU.is_equal))
                link.close()

            @block.scalar
            def _(s):
                with s.Fori(0, BLOCKS // GROUP) as i:
                    for j in range(GROUP):
                        take(s, s_gt)
                        s.activation(gtr[:, j, :, :], gate_turn(j), ACT.Copy).then_inc(s_gtc, 1)
                s.wait_ge(s_e2, 1)
                s.activation(mixw[:, 1, :], mixw[:, 1, :], ACT.Exp).then_inc(s_e2x, 1)

            @block.tensor
            def _(pe):
                pe.wait_ge(s_gw, 32)

                def turn(j):
                    take(pe, s_gx)
                    for k in range(KD):
                        last = pe.transpose(gate_turn(j)[:, k, :], gxr[:, j, k * P:(k + 1) * P], ident[:, :])
                    last.then_inc(s_gt, 1)

                def gate(i, j):
                    take(pe, s_gtc)
                    pe.sem_inc(s_gxfree, 1)
                    for k in range(KD):
                        last = pe.matmul(banks[1][:, bass.ds((i * GROUP + j) * EXPERTS, EXPERTS)], gtr[:, j, k, :], gw[:, k, :],
                                         start=(k == 0), stop=(k == KD - 1))
                    return last

                with pe.Fori(0, BLOCKS // GROUP) as i:
                    turn(0)
                    for j in range(1, GROUP):
                        turn(j)
                        gate(i, j - 1)
                    gate(i, GROUP - 1).then_inc(s_gates, 1)
                pe.wait_ge(s_gates, BLOCKS // GROUP)
                pe.sem_inc(s_lg, 1)
                pe.wait_ge(s_chosen, 1)
                hw = ASSIGN // 2
                for u in range(2):
                    part_of = chosen[:, u * hw:(u + 1) * hw, :].rearrange("p j e -> p (j e)")
                    pe.matmul(banks[2 + u][:, 0:hw * EXPERTS], before[:, :], part_of, start=True, stop=True)
                    last = pe.matmul(banks[4 + u][:, 0:hw * EXPERTS], ones[:, :], part_of, start=True, stop=True)
                last.then_inc(s_ranks, 1)

        if stages == 7:
            return

        NB = FE + D
        o = 0
        ein = at(o, TURN, D); o += TURN * D
        eturn = at(o, 2, KD, P); o += 2 * KD * P
        ehid = at(o, 2, FE); o += 2 * FE
        ehturn = at(o, 2, KE, P); o += 2 * KE * P
        eout = at(o, TURN, D); o += TURN * D
        biases = at(o, NB)[0:PARTS * QUAD]; o += NB
        left = at(o, NB)[0:PARTS * QUAD]; o += NB
        bpart = at(o, NB // 2, dt=bf16)[0:PARTS * QUAD]; o += NB // 2
        bparts = at(o, NB // 2, dt=bf16)[0:PARTS * QUAD]; o += NB // 2
        epick = at(o, P, dt=bf16)[0:PARTS * QUAD].rearrange("p (u n) -> p u n", u=2); o += P
        assert o <= ew_at

        s_bclear = sem("bias_rows_cleared")
        s_bias = sem("biases_loaded")
        s_bparts = sem("bias_parts_ready")
        s_ein = [sem(f"expert_tile_loaded{j}") for j in range(TURN)]
        s_einfree = [sem(f"expert_tile_used{j}") for j in range(TURN)]
        s_epick = sem("expert_picked")
        s_et = sem("expert_tile_turned")
        s_etc = sem("expert_turned_copied")
        s_eh = sem("expert_hidden_ready")
        s_er = sem("expert_hidden_clipped")
        s_eht = sem("expert_hidden_turned")
        s_ehc = sem("expert_hidden_copied")
        s_ey = sem("expert_product_ready")
        s_eyc = [sem(f"expert_output_ready{j}") for j in range(TURN)]
        s_eys = [sem(f"expert_output_stored{j}") for j in range(TURN)]
        s_eofree = [sem(f"expert_output_free{j}") for j in range(TURN)]
        TURNS = TILES // TURN
        xe_t = scratch["xe"].rearrange("(t p) d -> p t d", p=P)
        ye_t = scratch["ye"].rearrange("(t p) d -> p t d", p=P)
        with nc.Block() as block:
            @block.sync
            def _(sp):
                for j in range(2):
                    sp.dma_start(ein[:, j, :], xe_t[:, j, :]).then_inc(s_ein[j], 16)
                sp.wait_ge(s_bclear, 1)
                for n in range(PARTS):
                    sp.dma_start(biases[n * QUAD:n * QUAD + EXPERTS, :], a["ebias"]).then_inc(s_bias, 16)
                with sp.Fori(0, TURNS) as i:
                    for j in range(2, TURN + 2):
                        take(sp, s_einfree[j % TURN])
                        sp.dma_start(ein[:, j % TURN, :], xe_t[:, bass.ds(i * TURN + j, 1), :]).then_inc(s_ein[j % TURN], 16)

            @block.gpsimd
            def _(g):
                with g.Fori(0, TURNS) as i:
                    for j in range(TURN):
                        take(g, s_eyc[j])
                        g.dma_start(ye_t[:, bass.ds(i * TURN + j, 1), :], eout[:, j, :]).then_inc(s_eys[j], 16)
                    for j in range(TURN):
                        g.wait_ge(s_eys[j], 16 * (i + 1))
                        g.sem_inc(s_eofree[j], 1)

            @block.vector
            def _(v):
                for j in range(TURN):
                    v.sem_inc(s_eofree[j], 1)
                for j in range(2, TURN):
                    v.sem_inc(s_einfree[j], 1)
                v.memset(biases, 0.0).then_inc(s_bclear, 1)
                v.wait_ge(s_bias, 16 * PARTS)
                link = Chain(v, dve_step)
                link(v.tensor_copy(bpart, biases))
                link.also(v.tensor_copy(bparts[0:QUAD], bpart[0:QUAD]))
                link(v.tensor_tensor(left, biases, bpart, ALU.subtract))
                link(v.tensor_copy(bpart, left))
                link.also(v.tensor_copy(bparts[QUAD:2 * QUAD], bpart[QUAD:2 * QUAD]))
                link(v.tensor_tensor(left, left, bpart, ALU.subtract))
                link(v.tensor_copy(bparts[2 * QUAD:], left[2 * QUAD:]))
                link.close()
                v.sem_inc(s_bparts, 1)

                def picked(i, j):
                    v.tensor_copy(epick[:, j % 2, :], pick[:, bass.ds(i * TURN + j, 1)].to_broadcast([PARTS * QUAD, P])).then_inc(s_epick, 1)

                picked(0, 0)
                with v.Fori(0, TURNS) as i:
                    for j in range(TURN):
                        picked(i, j + 1)
                        take(v, s_eht)
                        v.tensor_copy(ehturn[:, j % 2, :, :].rearrange("p k n -> p (k n)"), banks[4 + j % 2][:, :]).then_inc(s_ehc, 1)
                        take(v, s_eofree[j])
                        take(v, s_ey)
                        v.tensor_copy(eout[:, j, :], banks[6 + j % 2][:, 0:D]).then_inc(s_eyc[j], 1)

            @block.scalar
            def _(s):
                def turned_copy(j):
                    take(s, s_et)
                    s.activation(eturn[:, j % 2, :, :].rearrange("p k n -> p (k n)"), banks[j % 2][:, 0:D], ACT.Copy).then_inc(s_etc, 1)

                def clip(j):
                    take(s, s_eh)
                    s.activation(ehid[:, j % 2, :], banks[2 + j % 2][:, :], ACT.Relu).then_inc(s_er, 1)

                turned_copy(0)
                turned_copy(1)
                clip(0)
                with s.Fori(0, TURNS) as i:
                    for j in range(TURN):
                        turned_copy(j)
                        clip(j + 1)

            @block.tensor
            def _(pe):
                def turn_in(loads, j):
                    pe.wait_ge(s_ein[j % TURN], 16 * loads)
                    for k in range(KD):
                        last = pe.transpose(banks[j % 2][:, k * P:(k + 1) * P], ein[:, j % TURN, k * P:(k + 1) * P], ident[:, :])
                    last.then_inc(s_et, 1)

                def first_product(i, j):
                    e, = numbers(nc, pe, texp[0:1, bass.ds(i * TURN + j, 1)], EXPERTS - 1)
                    take(pe, s_epick)
                    take(pe, s_etc)
                    pe.sem_inc(s_einfree[j % TURN], 1)
                    hid = banks[2 + j % 2][:, :]
                    pe.matmul(hid, epick[:, j % 2, :], bparts[:, 0:FE], start=True, stop=False)
                    for k in range(KD):
                        last = pe.matmul(hid, eturn[:, j % 2, k, :], ew1[:, bass.ds(e, 1), k * FE:(k + 1) * FE],
                                         start=False, stop=(k == KD - 1))
                    last.then_inc(s_eh, 1)

                pe.wait_ge(s_ew, 16 * 2 * EXPERTS)
                pe.wait_ge(s_bparts, 1)
                turn_in(1, 0)
                turn_in(1, 1)
                first_product(0, 0)
                with pe.Fori(0, TURNS) as i:
                    for j in range(TURN):
                        take(pe, s_er)
                        for k in range(KE):
                            last = pe.transpose(banks[4 + j % 2][:, k * P:(k + 1) * P], ehid[:, j % 2, k * P:(k + 1) * P], ident[:, :])
                        last.then_inc(s_eht, 1)
                        turn_in(i + 1 + (j + 2) // TURN, j + 2)
                        first_product(i, j + 1)
                        e, = numbers(nc, pe, texp[0:1, bass.ds(i * TURN + j, 1)], EXPERTS - 1)
                        prod = banks[6 + j % 2][:, 0:D]
                        pe.matmul(prod, epick[:, j % 2, :], bparts[:, FE:NB], start=True, stop=False)
                        take(pe, s_ehc)
                        for k in range(KE):
                            last = pe.matmul(prod, ehturn[:, j % 2, k, :], ew2[:, bass.ds(e, 1), k * D:(k + 1) * D],
                                             start=False, stop=(k == KE - 1))
                        last.then_inc(s_ey, 1)

        if stages == 8:
            return

        ya = at(0, BLOCKS, D)
        yb = at(BLOCKS * D, BLOCKS, D)
        x1 = at(2 * BLOCKS * D, BLOCKS, D)
        xn = at(3 * BLOCKS * D, BLOCKS, D)
        yn = at(4 * BLOCKS * D, BLOCKS, D)
        o = 5 * BLOCKS * D
        stats = at(o, BLOCKS, 6); o += BLOCKS * 6
        mean = at(o, BLOCKS); o += BLOCKS
        rstd = at(o, BLOCKS); o += BLOCKS
        tmp1 = at(o, BLOCKS); o += BLOCKS
        evec = at(o, 2, D); o += 2 * D
        s_c9 = sem("combine_inputs_loaded")
        s_y = [sem(f"expert_rows_gathered{g}") for g in range(BLOCKS // GROUP)]
        s_var9 = sem("ln4_variances_ready")
        s_std9 = sem("ln4_deviations_ready")
        s_sh9 = sem("ln4_shifts_ready")
        s_nr9 = sem("ln4_normalised")
        s_fin = sem("result_ready")
        s_out = sem("result_stored")
        whole = N_NODES // P
        with nc.Block() as block:
            @block.sync
            def _(sp):
                sp.dma_start(xn, scratch["xn"].rearrange("(t p) d -> p t d", p=P)).then_inc(s_c9, 16)
                sp.dma_start(x1, scratch["x1"].rearrange("(t p) d -> p t d", p=P)).then_inc(s_c9, 16)
                for n in range(2):
                    sp.dma_start(evec[:, n, :], a["evecs"][n:n + 1, :].to_broadcast([P, D])).then_inc(s_c9, 16)
                for g in range(BLOCKS // GROUP):
                    first, last = g * GROUP, min((g + 1) * GROUP, whole)
                    sp.wait_ge(s_fin, g + 1)
                    sp.dma_start(out[first * P:last * P, :].rearrange("(t p) d -> p t d", p=P), yn[:, first:last, :]).then_inc(s_out, 16)
                sp.dma_start(out[whole * P:, :], yn[0:N_NODES - whole * P, whole, :]).then_inc(s_out, 16)
                sp.wait_ge(s_out, 16 * (BLOCKS // GROUP + 1))

            @block.gpsimd
            def _(g):
                for b in range(BLOCKS):
                    for n, rows in enumerate((ya, yb)):
                        g.indirect_dma_start(out=rows[:, b, :], out_offset=None, in_=scratch["ye"],
                                             in_offset=bass.IndirectOffsetOnAxis(ap=pos[:, n * BLOCKS + b:n * BLOCKS + b + 1], axis=0)
                                             ).then_inc(s_y[b // GROUP], 16)

            @block.vector
            def _(v):
                link = Chain(v, dve_step)
                v.wait_ge(s_c9, 64)
                link(v.tensor_tensor(x1, x1, spread(evec[:, 1, :]), ALU.add))

                def finish(g):
                    rows = slice(g * GROUP, (g + 1) * GROUP)
                    v.wait_ge(s_nr9, GROUP * (g + 1))
                    link(v.tensor_tensor(yn[:, rows, :], yn[:, rows, :], evec[:, 0, :].unsqueeze(1).to_broadcast([P, GROUP, D]), ALU.mult))
                    link(v.tensor_tensor(yn[:, rows, :], yn[:, rows, :], x1[:, rows, :], ALU.add))
                    v.sem_inc(s_fin, 1)

                for g in range(BLOCKS // GROUP):
                    rows = slice(g * GROUP, (g + 1) * GROUP)
                    v.wait_ge(s_y[g], 16 * 2 * GROUP)
                    for b in range(g * GROUP, (g + 1) * GROUP):
                        link.also(v.scalar_tensor_tensor(out=ya[:, b, :], in0=ya[:, b, :], scalar=mixw[:, 0, b:b + 1], in1=xn[:, b, :],
                                                         op0=ALU.mult, op1=ALU.add))
                    for n, b in enumerate(range(g * GROUP, (g + 1) * GROUP)):
                        v.wait_ge(dve_step, link.n - GROUP + 1)
                        link.also(v.scalar_tensor_tensor(out=ya[:, b, :], in0=yb[:, b, :], scalar=mixw[:, 1, b:b + 1], in1=ya[:, b, :],
                                                         op0=ALU.mult, op1=ALU.add))
                    for n, b in enumerate(range(g * GROUP, (g + 1) * GROUP)):
                        v.wait_ge(dve_step, link.n - GROUP + 1)
                        link.also(v.bn_stats(stats[:, b, :], ya[:, b, :]))
                    v.wait_ge(dve_step, link.n)
                    stats_to_scales(v, link, stats[:, rows, :], mean[:, rows], rstd[:, rows], tmp1[:, rows], 1).then_inc(s_var9, 1)
                    if g:
                        finish(g - 1)
                    v.wait_ge(s_std9, g + 1)
                    link(v.reciprocal(rstd[:, rows], rstd[:, rows]))
                    link(v.scalar_tensor_tensor(out=mean[:, rows], in0=mean[:, rows], scalar=-1.0, in1=rstd[:, rows],
                                                op0=ALU.mult, op1=ALU.mult))
                    v.sem_inc(s_sh9, 1)
                finish(BLOCKS // GROUP - 1)
                link.close()

            @block.scalar
            def _(s):
                for g in range(BLOCKS // GROUP):
                    rows = slice(g * GROUP, (g + 1) * GROUP)
                    s.wait_ge(s_var9, g + 1)
                    s.activation(rstd[:, rows], rstd[:, rows], ACT.Sqrt).then_inc(s_std9, 1)
                    s.wait_ge(s_sh9, g + 1)
                    for b in range(g * GROUP, (g + 1) * GROUP):
                        s.activation(yn[:, b, :], ya[:, b, :], ACT.Identity, bias=mean[:, b:b + 1], scale=rstd[:, b:b + 1]).then_inc(s_nr9, 1)


_IN = ["x", "W_srcT", "W_src", "W_dst", "att", "src", "dst", "kind", "weight"]


def kernel(**inputs):
    import numpy as np
    import concourse.bacc as bacc
    from concourse import mybir
    from concourse.bass_utils import run_bass_kernel_spmd as run

    g = {k: np.asarray(v) for k, v in inputs.items()}
    tiles = lambda v, fill: np.pad(v, (0, EDGE_TILES * P - N_EDGES), constant_values=fill).reshape(EDGE_TILES, P)
    arrays = {
        "x": np.pad(g["x"], ((0, ROWS - N_NODES), (0, 0))),
        "W_srcT": g["L0_gnn_W_src"].T, "W_src": g["L0_gnn_W_src"], "W_dst": g["L0_gnn_W_dst"],
        "att": np.concatenate([g["L0_gnn_att_src"].reshape(T, D), g["L0_gnn_att_dst"].reshape(T, D)]).T,
        "src": tiles(g["src"], 0), "dst": tiles(g["dst"], 4095),
        "kind": tiles(g["edge_type_2"], 0), "weight": tiles(g["edge_weight"], 0),
    }
    arrays.update({
        "vecs": np.stack([g["L0_gnn_" + k] for k in ("bias", "ln1_g", "ln1_b", "ln2_g", "ln2_b", "ffn_b2")]),
        "ffn_W1T": g["L0_gnn_ffn_W1"].T, "ffn_W2T": g["L0_gnn_ffn_W2"].T, "ffn_b1": g["L0_gnn_ffn_b1"].reshape(KF, P).T,
        "gate_w": g["L0_ffn_gate_w"], "gate_b": g["L0_ffn_gate_b"].reshape(1, EXPERTS),
        "ew1": g["L0_ffn_w1"], "ew2": g["L0_ffn_w2"], "ebias": np.concatenate([g["L0_ffn_b1"], g["L0_ffn_b2"]], 1),
        "evecs": np.stack([g["L0_ffn_gamma"], g["L0_ffn_beta"]]),
    })
    arrays = {k: np.ascontiguousarray(v) for k, v in arrays.items()}
    nc = bacc.Bacc("TRN2", target_bir_lowering=False, num_devices=1)
    a = {k: nc.dram_tensor("in_" + k, v.shape, mybir.dt.from_np(v.dtype), kind="ExternalInput").ap() for k, v in arrays.items()}
    f32 = mybir.dt.float32
    KIND = "Internal"
    scratch = {k: nc.dram_tensor(k + "_t", s, f32, kind=KIND).ap() for k, s in
               {"xs": (ROWS, D), "xln": (ROWS, D), "s": (ROWS, 2 * H), "ends": (P, 4), "ends2": (P, 2),
                "x1": (ROWS, D), "xn": (ROWS, D), "xe": (TILES_AHEAD * P, D), "ye": (TILES * P, D)}.items()}
    out = nc.dram_tensor("out", (N_NODES, D), f32, kind="ExternalOutput").ap()
    build(nc, a, out, scratch, 9)
    r = run(nc, [{"in_" + k: v for k, v in arrays.items()}], core_ids=[0])
    return r.results[0]["out"]
```

```python
import concourse.bass as bass
from concourse import mybir
from contextlib import ExitStack

P = 128
N_NODES = 3125
BLOCKS = -(-N_NODES // P)
ROWS = BLOCKS * P
N_EDGES = 50000
EDGE_TILES = -(-N_EDGES // P)
NO_NODE = (BLOCKS + 1) * P
D = 256
KD = D // P
H, C = 8, 32
T = 2
F = 1024
KF = F // P
EXPERTS, FE = 16, 512
KE = FE // P
EPS = 1e-5
LOT = 8
LOTS = 4
SELECTED = 2
STEP = LOTS * LOT
CHUNKS = P // H
PER_CHUNK = -(-(EDGE_TILES + BLOCKS) // CHUNKS)
SLOTS = CHUNKS * PER_CHUNK
STEPS = SLOTS // STEP
SLOT_GROUPS = -(-SLOTS // P)
SCAN = PER_CHUNK * P
SCAN_LOT = 4
NEG = -3.0e38
SUMS = D + 2 * H + 1
ASSIGN = 2 * BLOCKS
TURN = 8
TILES = -(-((2 * N_NODES + EXPERTS * (P - 1)) // P) // TURN) * TURN
TILES_AHEAD = TILES + 2
PARTS = 3
QUAD = 32
GROUP = 5
GT = GROUP * P
GROUPS = BLOCKS // GROUP
ARENA = 44000

fp32 = mybir.dt.float32
bf16 = mybir.dt.bfloat16
u32 = mybir.dt.uint32
i32 = mybir.dt.int32
ALU = mybir.AluOpType
ACT = mybir.ActivationFunctionType
AX = mybir.AxisListType.X


def take(eng, sem, n=1):
    eng.wait_ge(sem, n)
    eng.sem_inc(sem, -n)


class Chain:

    def __init__(self, eng, sem):
        self.eng, self.sem, self.n = eng, sem, 0

    def __call__(self, ins):
        ins.then_inc(self.sem, 1)
        self.n += 1
        self.eng.wait_ge(self.sem, self.n)

    def also(self, ins):
        ins.then_inc(self.sem, 1)
        self.n += 1

    def close(self):
        self.eng.wait_ge(self.sem, self.n)
        self.eng.sem_inc(self.sem, -self.n)
        self.n = 0


def numbers(nc, eng, row, most):
    _, got = nc.values_load_multi_w_load_instructions(
        row, engines=[eng.engine], min_val=0, max_val=most,
        skip_runtime_bounds_check_because="the numbers are clamped on the chip when they are made")
    return got


def build(nc, a, out, scratch):
    ctx = ExitStack()
    with ctx:
        def sem(name):
            return ctx.enter_context(nc.semaphore(name))

        def sb(name, shape, dt=fp32):
            return ctx.enter_context(nc.sbuf_tensor(name, shape, dt))

        banks = [ctx.enter_context(nc.psum_tensor(f"bank{i}", [P, 512], fp32)) for i in range(8)]

        ident = sb("ident", [P, P])
        ones = sb("ones", [P, P])
        from_on = sb("from_on", [P, P])
        lane = sb("lane", [P, P])
        part = sb("part", [P, 1])
        heads = sb("heads", [P, KD, H])
        arena = sb("arena", [P, ARENA])

        def at(off, *dims, dt=fp32):
            n = 1
            for d in dims:
                n *= d
            assert off + n <= ARENA, (off, n)
            v = arena[:, off:off + n]
            if dt != fp32:
                v = v.bitcast(dt)
            if len(dims) == 2:
                v = v.rearrange("p (a b) -> p a b", b=dims[1])
            elif len(dims) == 3:
                v = v.rearrange("p (a b c) -> p a b c", b=dims[1], c=dims[2])
            return v

        s_const = sem("constants_made")
        pool_step = sem("pool_step")
        dve_step = sem("dve_step")
        act_step = sem("act_step")

        dtab = sb("dtab", [P, BLOCKS, 3 * H])
        xb = at(0, BLOCKS, D)
        PW = D + 4 * H
        proj = at(BLOCKS * D, BLOCKS, PW)
        xs, sd = proj[:, :, 0:D], proj[:, :, D:]
        o = BLOCKS * (D + PW)
        wv = at(o, KD, D + 4 * H); o += KD * (D + 4 * H)
        wsrc = at(o, KD, D); o += KD * D
        wdst = at(o, KD, D); o += KD * D
        att = at(o, KD, 2 * T); o += KD * 2 * T
        attm = at(o, KD, 2 * T, H); o += KD * 2 * T * H
        stats = at(o, BLOCKS, 6); o += BLOCKS * 6
        mean = at(o, BLOCKS); o += BLOCKS
        rstd = at(o, BLOCKS); o += BLOCKS
        tmp1 = at(o, BLOCKS); o += BLOCKS
        xl = at(o, GROUP, D); o += GROUP * D
        xt = at(o, GROUP, KD, P); o += GROUP * KD * P

        s_x = (sem("first_x_rows_loaded"), sem("x_loaded"))
        s_w = sem("proj_weights_loaded")
        s_var = sem("variances_ready")
        s_std = sem("deviations_ready")
        s_attm = sem("masked_attention_ready")
        s_v = sem("score_vectors_ready")
        s_vc = sem("score_vectors_copied")
        s_xl = sem("block_normalised")
        s_tr = sem("block_turned")
        s_xt = sem("turned_copied")
        s_pj = sem("block_projected")
        s_pjfree = sem("projection_copied")
        s_xlfree = sem("normalised_used")
        s_projd = sem("projections_copied")

        def turn_slot(j):
            return banks[j % 3][:, 0:D].rearrange("p (k n) -> p k n", k=KD)

        keep_at = 30000
        stab = at(keep_at, BLOCKS * T * H)
        s_ln = sem("rows_normalised")
        s_store = sem("tables_stored")

        def stats_to_scales(v, link, st, mn, rs, t):
            link(v.tensor_tensor(mn, st[:, :, 1], st[:, :, 4], ALU.add))
            link(v.tensor_tensor(t, st[:, :, 1], st[:, :, 4], ALU.subtract))
            link(v.tensor_scalar(mn, mn, 0.5, None, ALU.mult))
            link(v.tensor_tensor(t, t, t, ALU.mult))
            link(v.tensor_tensor(rs, st[:, :, 2], st[:, :, 5], ALU.add))
            link(v.tensor_scalar(rs, rs, 1.0 / D, EPS, ALU.mult, ALU.add))
            return v.scalar_tensor_tensor(out=rs, in0=t, scalar=0.25, in1=rs, op0=ALU.mult, op1=ALU.add)

        AHEAD = LOTS * LOT
        src_at = sb("src_at", [P, SLOTS + AHEAD], u32)
        srct_at = sb("srct_at", [P, SLOTS + AHEAD], u32)
        local = sb("local", [P, SLOTS + LOT])
        key = sb("key", [P, SLOTS])
        kind = sb("kind", [P, SLOTS])
        weight = sb("weight", [P, SLOTS])
        blk = sb("blk", [P, SLOTS], i32)
        lane_at = at(keep_at + BLOCKS * T * H, SLOTS + LOT)
        pair_at = at(keep_at + BLOCKS * T * H + SLOTS + LOT, SLOTS)
        lastrow_i = at(o, EDGE_TILES, dt=i32)[0:1, :]; o += EDGE_TILES
        lastrow = at(o, EDGE_TILES)[0:1, :]; o += EDGE_TILES
        tilerow = at(o, EDGE_TILES)[0:1, :]; o += EDGE_TILES
        junk = at(o, EDGE_TILES); o += EDGE_TILES
        slot_tile = at(o, SLOT_GROUPS); o += SLOT_GROUPS
        slot_tile_i = at(o, SLOT_GROUPS, dt=u32); o += SLOT_GROUPS
        slot_blk = at(o, SLOT_GROUPS); o += SLOT_GROUPS
        slot_off = at(o, SLOT_GROUPS); o += SLOT_GROUPS
        slot_no = at(o, SLOT_GROUPS); o += SLOT_GROUPS
        diag = at(o, SLOT_GROUPS, P); o += SLOT_GROUPS * P
        raw = [at(o + i * SLOT_GROUPS * P, SLOT_GROUPS, P, dt=dt) for i, dt in enumerate((i32, i32, i32, fp32))]
        o += 4 * SLOT_GROUPS * P
        rsrc = at(o, SLOT_GROUPS, P); o += SLOT_GROUPS * P
        rsrct = at(o, SLOT_GROUPS, P); o += SLOT_GROUPS * P
        rdst = at(o, SLOT_GROUPS, P); o += SLOT_GROUPS * P
        rkind = at(o, SLOT_GROUPS, P); o += SLOT_GROUPS * P
        rlocal = at(o, SLOT_GROUPS, P); o += SLOT_GROUPS * P
        rok = at(o, SLOT_GROUPS, P); o += SLOT_GROUPS * P
        rkey = at(o, SLOT_GROUPS, P); o += SLOT_GROUPS * P
        rblk_i = at(o, SLOT_GROUPS, P, dt=i32); o += SLOT_GROUPS * P
        rblk = at(o, SLOT_GROUPS, P); o += SLOT_GROUPS * P
        rlane = at(o, SLOT_GROUPS, P); o += SLOT_GROUPS * P
        rpair = at(o, SLOT_GROUPS, P); o += SLOT_GROUPS * P
        assert o <= keep_at, o

        s_last = sem("tile_ends_loaded")
        s_iota = sem("tile_numbers_made")
        s_lrow = sem("staircase_row_ready")
        s_lbc = sem("staircase_spread")
        s_stile = sem("slot_tiles_ready")
        s_diag = sem("block_diagonals_ready")
        s_bbc = sem("blocks_spread")
        s_rec = sem("edge_rows_gathered")
        s_rows = sem("slot_rows_ready")
        s_rt = sem("slot_rows_turned")
        s_rtc = sem("turned_rows_copied")
        with nc.Block() as block:
            @block.sync
            def _(sp):
                sp.dma_start(lastrow_i, a["dst"].rearrange("(a t) e -> a t e", a=1)[:, :, P - 1],
                             allow_slow_non_contiguous=True).then_inc(s_last, 16)
                x_rows = a["x"].rearrange("(t p) d -> p t d", p=P)
                sp.dma_start(xb[:, 0:GROUP, :], x_rows[:, 0:GROUP, :]).then_inc(s_x[0], 16)
                sp.dma_start(wv[:, :, 0:D], a["W_srcT"].rearrange("(k p) n -> p k n", p=P)).then_inc(s_w, 16)
                sp.dma_start(wsrc, a["W_src"].rearrange("(k p) n -> p k n", p=P)).then_inc(s_w, 16)
                sp.dma_start(wdst, a["W_dst"].rearrange("(k p) n -> p k n", p=P)).then_inc(s_w, 16)
                sp.dma_start(att, a["att"].rearrange("(k p) n -> p k n", p=P)).then_inc(s_w, 16)
                sp.dma_start(xb[:, GROUP:, :], x_rows[:, GROUP:, :]).then_inc(s_x[1], 16)
                sp.wait_ge(s_ln, BLOCKS)
                sp.dma_start(scratch["xln"].rearrange("(t p) d -> p t d", p=P), xb).then_inc(s_store, 16)
                sp.wait_ge(s_projd, 1)
                sp.dma_start(scratch["s"].rearrange("(t p) d -> p t d", p=P), sd[:, :, 0:2 * H]).then_inc(s_store, 16)
                sp.dma_start(scratch["xs"].rearrange("(t p) d -> p t d", p=P), xs).then_inc(s_store, 16)
                sp.wait_ge(s_store, 48)

            @block.gpsimd
            def _(g):
                link = Chain(g, pool_step)
                link.also(g.memset(ident[:, :], 0.0))
                link.also(g.memset(ones[:, :], 1.0))
                link.also(g.memset(from_on[:, :], -1.0))
                link.also(g.memset(heads[:, :, :], 1.0))
                link(g.iota(lane[:, :], pattern=[[1, P]], base=0, channel_multiplier=0,
                            allow_small_or_imprecise_dtypes=True))
                link.also(g.iota(part[:, :], pattern=[[1, 1]], base=0, channel_multiplier=1,
                                 allow_small_or_imprecise_dtypes=True))
                link.also(g.affine_select(out=ident[:, :], in_=ident[:, :], compare_op=ALU.not_equal, fill=1.0,
                                          base=0, pattern=[[-1, P]], channel_multiplier=1))
                link.also(g.affine_select(out=from_on[:, :], in_=from_on[:, :], compare_op=ALU.is_ge, fill=0.0,
                                          base=0, pattern=[[-1, P]], channel_multiplier=1))
                link(g.affine_select(out=heads[:, :, :], in_=heads[:, :, :], compare_op=ALU.is_ge, fill=0.0,
                                     base=0, pattern=[[P, KD], [-C, H]], channel_multiplier=1))
                link(g.affine_select(out=heads[:, :, :], in_=heads[:, :, :], compare_op=ALU.is_ge, fill=0.0,
                                     base=C - 1, pattern=[[-P, KD], [C, H]], channel_multiplier=-1))
                link.close()
                g.sem_inc(s_const, 1)
                g.iota(tilerow, pattern=[[1, EDGE_TILES]], base=0, channel_multiplier=0,
                       allow_small_or_imprecise_dtypes=True).then_inc(s_iota, 1)
                g.wait_ge(s_iota, 1)
                g.iota(slot_no, pattern=[[P, SLOT_GROUPS]], base=0, channel_multiplier=1,
                       allow_small_or_imprecise_dtypes=True).then_inc(s_iota, 1)
                g.wait_ge(s_stile, 1)
                for i, name in enumerate(("src", "dst", "kind", "weight")):
                    for q in range(SLOT_GROUPS):
                        g.indirect_dma_start(out=raw[i][:, q, :], out_offset=None, in_=a[name],
                                             in_offset=bass.IndirectOffsetOnAxis(ap=slot_tile_i[:, q:q + 1], axis=0)
                                             ).then_inc(s_rec, 16)

            @block.vector
            def _(v):
                link = Chain(v, dve_step)
                v.wait_ge(s_const, 1)
                v.wait_ge(s_last, 16)
                v.wait_ge(s_iota, 2)
                link(v.tensor_single_scalar(lastrow_i, lastrow_i, 7, ALU.arith_shift_right))
                link(v.tensor_copy(lastrow, lastrow_i))
                v.tensor_tensor(lastrow, lastrow, tilerow, ALU.add).then_inc(s_lrow, 1)
                v.wait_ge(s_lbc, 1)
                for q in range(SLOT_GROUPS):
                    link(v.tensor_scalar(junk, banks[0][:, 0:EDGE_TILES], slot_no[:, q:q + 1], 0.0,
                                         ALU.is_lt, ALU.add, accum_out=slot_tile[:, q:q + 1]))
                link(v.tensor_scalar(slot_tile, slot_tile, float(EDGE_TILES - 1), None, ALU.min))
                v.tensor_copy(slot_tile_i, slot_tile).then_inc(s_stile, 1)
                link(v.tensor_tensor(slot_blk, slot_no, slot_tile, ALU.subtract))
                link(v.tensor_scalar(slot_off, slot_blk, float(P), None, ALU.mult))
                for q in range(SLOT_GROUPS):
                    link.also(v.tensor_scalar(diag[:, q, :], ident[:, :], slot_blk[:, q:q + 1], None, ALU.mult))
                link.close()
                v.sem_inc(s_diag, 1)
                v.wait_ge(s_bbc, 1)
                link(v.tensor_scalar(blk[:, :], banks[1][:, 0:SLOTS], float(BLOCKS - 1), None, ALU.min))
                link.close()
                v.wait_ge(s_w, 64)
                for k in range(KD):
                    for t in range(2 * T):
                        link.also(v.tensor_scalar(attm[:, k, t, :], heads[:, k, :], att[:, k, t:t + 1], None, ALU.mult))
                link.close()
                v.sem_inc(s_attm, 1)

                def block_stats(first, last, n):
                    v.wait_ge(s_x[n], 16)
                    for b in range(first, last):
                        link.also(v.bn_stats(stats[:, b, :], xb[:, b, :]))
                    v.wait_ge(dve_step, link.n)
                    rows = slice(first, last)
                    stats_to_scales(v, link, stats[:, rows, :], mean[:, rows], rstd[:, rows], tmp1[:, rows]).then_inc(s_var, 1)

                def normalise(g):
                    for j in range(GROUP):
                        b = bass.ds(g * GROUP + j, 1)
                        take(v, s_xlfree)
                        v.tensor_scalar(xl[:, j, :], xb[:, b, :], mean[:, b], rstd[:, b],
                                        ALU.subtract, ALU.mult).then_inc(s_xl, 1)
                        v.tensor_scalar(xb[:, b, :], xb[:, b, :], mean[:, b], rstd[:, b],
                                        ALU.subtract, ALU.mult).then_inc(s_ln, 1)

                block_stats(0, GROUP, 0)
                v.wait_ge(s_v, 1)
                v.tensor_copy(wv[:, :, D:], banks[7][:, 0:KD * 4 * H].rearrange("p (k n) -> p k n", k=KD)).then_inc(s_vc, 1)
                v.sem_inc(s_xlfree, GROUP)
                v.wait_ge(s_std, 1)
                link(v.reciprocal(rstd[:, 0:GROUP], rstd[:, 0:GROUP]))
                normalise(0)
                block_stats(GROUP, BLOCKS, 1)
                v.wait_ge(s_std, 2)
                link(v.reciprocal(rstd[:, GROUP:], rstd[:, GROUP:]))
                link.close()
                with v.Fori(1, GROUPS) as g:
                    normalise(g)
                v.wait_ge(s_rec, 16 * 4 * SLOT_GROUPS)
                link.also(v.tensor_copy(rsrc, raw[0]))
                link.also(v.tensor_copy(rdst, raw[1]))
                link.also(v.tensor_single_scalar(rblk_i, raw[0], 7, ALU.arith_shift_right))
                link(v.tensor_copy(rkind, raw[2]))
                link(v.tensor_copy(rblk, rblk_i))
                link.also(v.scalar_tensor_tensor(out=rlane, in0=rblk, scalar=-float(P), in1=rsrc, op0=ALU.mult, op1=ALU.add))
                link.also(v.scalar_tensor_tensor(out=rpair, in0=rblk, scalar=2.0, in1=rkind, op0=ALU.mult, op1=ALU.add))
                link.also(v.scalar_tensor_tensor(out=rsrct, in0=rsrc, scalar=2.0, in1=rkind, op0=ALU.mult, op1=ALU.add))
                for q in range(SLOT_GROUPS):
                    link(v.tensor_scalar(rlocal[:, q, :], rdst[:, q, :], slot_off[:, q:q + 1], None, ALU.subtract))
                link(v.tensor_scalar(rok, rlocal, 0.0, None, ALU.is_ge))
                link(v.scalar_tensor_tensor(out=rok, in0=rlocal, scalar=float(P), in1=rok, op0=ALU.is_lt, op1=ALU.mult))
                link(v.scalar_tensor_tensor(out=rlocal, in0=rlocal, scalar=1.0, in1=rok, op0=ALU.add, op1=ALU.mult))
                link(v.scalar_tensor_tensor(out=rkey, in0=rdst, scalar=1.0, in1=rok, op0=ALU.add, op1=ALU.mult))
                link.also(v.tensor_scalar(rlocal, rlocal, -1.0, None, ALU.add))
                link(v.tensor_scalar(rkey, rkey, -1.0, None, ALU.add))
                link.close()
                v.sem_inc(s_rows, 1)
                v.wait_ge(s_projd, 1)
                link.also(v.tensor_copy(dtab[:, :, 0:2 * H], sd[:, :, 2 * H:4 * H]))
                link.also(v.tensor_copy(stab.rearrange("p (b n) -> p b n", b=BLOCKS), sd[:, :, 0:2 * H]))
                link(v.tensor_tensor(dtab[:, :, 2 * H:], sd[:, :, 0:H], sd[:, :, 2 * H:3 * H], ALU.add))
                link(v.scalar_tensor_tensor(out=dtab[:, :, 2 * H:], in0=dtab[:, :, 2 * H:], scalar=0.2,
                                            in1=dtab[:, :, 2 * H:], op0=ALU.mult, op1=ALU.max))
                link.also(v.memset(src_at[:, SLOTS:], 0))
                link.also(v.memset(srct_at[:, SLOTS:], 0))
                link.also(v.memset(local[:, SLOTS:], -1.0))
                link.also(v.memset(lane_at[:, SLOTS:], -1.0))
                link.close()
                for i, dst in enumerate((src_at, srct_at, local, key, kind, weight, lane_at, pair_at)):
                    v.wait_ge(s_rt, i + 1)
                    v.tensor_copy(dst[:, 0:SLOTS], banks[2 + i % 2][:, 0:SLOTS]).then_inc(s_rtc, 1)
                v.wait_ge(s_rtc, 8)

            @block.scalar
            def _(s):
                def turned_copy(j):
                    take(s, s_tr)
                    s.activation(xt[:, j, :, :], turn_slot(j), ACT.Copy).then_inc(s_xt, 1)

                def projected_copy(g, j):
                    take(s, s_pj)
                    s.activation(proj[:, bass.ds(g * GROUP + j, 1), :], banks[3 + j][:, 0:PW], ACT.Copy).then_inc(s_pjfree, 1)

                def copies(g):
                    turned_copy(0)
                    for j in range(1, GROUP):
                        turned_copy(j)
                        projected_copy(g, j - 1)
                    projected_copy(g, GROUP - 1)

                s.wait_ge(s_var, 1)
                s.activation(rstd[:, 0:GROUP], rstd[:, 0:GROUP], ACT.Sqrt).then_inc(s_std, 1)
                copies(0)
                s.wait_ge(s_var, 2)
                s.activation(rstd[:, GROUP:], rstd[:, GROUP:], ACT.Sqrt).then_inc(s_std, 1)
                with s.Fori(1, GROUPS) as g:
                    copies(g)
                s.wait_ge(s_pjfree, GROUP)
                s.sem_inc(s_projd, 1)

            @block.tensor
            def _(pe):
                pe.wait_ge(s_lrow, 1)
                pe.matmul(banks[0][:, 0:EDGE_TILES], ones[0:1, :], lastrow, start=True, stop=True).then_inc(s_lbc, 1)
                pe.wait_ge(s_diag, 1)
                pe.matmul(banks[1][:, :], ones[:, :], diag.rearrange("p q n -> p (q n)"), start=True, stop=True).then_inc(s_bbc, 1)
                pe.wait_ge(s_attm, 1)
                for m in range(KD):
                    for w, (wt, c0) in enumerate(((wsrc, 0), (wdst, T))):
                        for k in range(KD):
                            last = pe.matmul(banks[7][:, m * 4 * H + w * 2 * H: m * 4 * H + (w + 1) * 2 * H],
                                             wt[:, k, m * P:(m + 1) * P], attm[:, k, c0:c0 + T, :],
                                             start=(k == 0), stop=(k == KD - 1))
                last.then_inc(s_v, 1)
                pe.wait_ge(s_vc, 1)
                pe.sem_inc(s_pjfree, GROUP)

                def turn(j):
                    take(pe, s_xl)
                    for k in range(KD):
                        last = pe.transpose(turn_slot(j)[:, k, :], xl[:, j, k * P:(k + 1) * P], ident[:, :])
                    last.then_inc(s_tr, 1)

                def project(j):
                    take(pe, s_xt)
                    pe.sem_inc(s_xlfree, 1)
                    take(pe, s_pjfree)
                    for k in range(KD):
                        last = pe.matmul(banks[3 + j][:, 0:PW], xt[:, j, k, :], wv[:, k, :], start=(k == 0), stop=(k == KD - 1))
                    last.then_inc(s_pj, 1)

                with pe.Fori(0, GROUPS) as g:
                    turn(0)
                    for j in range(1, GROUP):
                        turn(j)
                        project(j - 1)
                    project(GROUP - 1)
                pe.wait_ge(s_projd, 1)
                pe.wait_ge(s_rows, 1)
                for i, rows in enumerate((rsrc, rsrct, rlocal, rkey, rkind, raw[3], rlane, rpair)):
                    if i >= 2:
                        pe.wait_ge(s_rtc, i - 1)
                    for q in range(SLOT_GROUPS):
                        last = pe.transpose(banks[2 + i % 2][:, q * P:(q + 1) * P], rows[:, q, :], ident[:, :])
                    last.then_inc(s_rt, 1)

        o = 0
        alpha = at(o, SLOTS, H); o += SLOTS * H
        selfe = at(o, SLOTS, H); o += SLOTS * H
        mx = at(o, SLOTS, H); o += SLOTS * H
        edge_end = o
        sg = at(o, STEP, H); o += STEP * H
        idx_a = at(o, STEP, dt=u32); o += STEP
        hot = at(o, 2, LOT * P); o += 2 * LOT * P
        hotT = at(o, 2, LOT * P); o += 2 * LOT * P
        d0 = at(o, LOT, H); o += LOT * H
        d1 = at(o, LOT, H); o += LOT * H
        nkind = at(o, SLOTS); o += SLOTS
        PAIRS = BLOCKS * T
        shot = at(keep_at + BLOCKS * T * H + 2 * SLOTS + LOT, 2, SELECTED * P)
        shotT = at(keep_at + BLOCKS * T * H + 2 * SLOTS + LOT + 2 * SELECTED * P, 2, SELECTED * P)
        pairs = at(keep_at + BLOCKS * T * H + 2 * SLOTS + LOT + 4 * SELECTED * P, SELECTED, PAIRS)
        picks = at(keep_at + BLOCKS * T * H + 2 * SLOTS + LOT + 4 * SELECTED * P + SELECTED * PAIRS, SELECTED, PAIRS * H)
        scan_at = edge_end + SLOTS * (2 * H + 1) - SCAN
        assert o <= scan_at + SCAN, (o, scan_at)
        tkey = at(scan_at + SCAN, SCAN)
        cut = at(scan_at + 2 * SCAN, SCAN + 1)
        key4 = at(scan_at + 3 * SCAN + 1, 2, SCAN_LOT, P)

        GATHERED = LOT - SELECTED
        SOURCE_BANKS = (6, 7)
        s_ga = [sem(f"source_terms_gathered{h}") for h in range(LOTS)]
        s_gafree = sem("source_terms_used")
        s_idx_a = sem("source_term_numbers_ready")
        s_hot = sem("onehots_ready")
        s_hott = sem("onehots_turned")
        s_hotc = sem("turned_onehots_copied")
        s_dsel = sem("destination_terms_selected")
        s_dfree = sem("destination_terms_used")
        s_shot = sem("source_onehots_ready")
        s_ssel = sem("source_terms_selected")
        s_sfree = sem("selected_source_terms_used")
        s_kpack = sem("tile_destinations_packed")
        s_kturn = sem("tile_destinations_turned")
        s_kcopy = sem("turned_destinations_copied")

        def scan_lots():
            return [(n, k, min(SCAN_LOT, PER_CHUNK - k)) for n, k in enumerate(range(0, PER_CHUNK, SCAN_LOT))]

        def by_tile(rows, k, n):
            if len(rows.shape) == 2:
                return rows.rearrange("p (c k) -> p k c", k=PER_CHUNK)[:, k:k + n, :]
            return rows.rearrange("p (c k) h -> p k c h", k=PER_CHUNK)[:, k:k + n, :, :]

        def make_hot(v, buf, sl):
            return v.tensor_tensor(buf.rearrange("p (s n) -> p s n", n=P),
                                   lane[:, :].unsqueeze(1).to_broadcast([P, LOT, P]),
                                   local[:, sl].unsqueeze(2).to_broadcast([P, LOT, P]), ALU.is_equal)

        def gather(g, s_idx, s_done, rows, idx, table, slots=LOT):
            with g.Fori(0, STEPS) as i:
                for h in range(LOTS):
                    take(g, s_idx)
                    for n in range(h * LOT, h * LOT + slots):
                        g.indirect_dma_start(out=rows[:, n, :], out_offset=None, in_=table,
                                             in_offset=bass.IndirectOffsetOnAxis(ap=idx[:, n:n + 1], axis=0)
                                             ).then_inc(s_done[h], 16)

        def copy_numbers(s, s_free, s_idx, idx, numbers_at, i, h):
            n = h % LOTS * LOT
            take(s, s_free)
            s.activation(idx[:, n:n + LOT], numbers_at[:, bass.ds(i * STEP + h * LOT, LOT)], ACT.Copy).then_inc(s_idx, 1)

        with nc.Block() as block:
            @block.gpsimd
            def _(g):
                gather(g, s_idx_a, s_ga, sg, idx_a, scratch["s"].rearrange("n (t h) -> (n t) h", t=T), GATHERED)

            @block.vector
            def _(v):
                link = Chain(v, dve_step)
                link(v.tensor_scalar(nkind, kind[:, :], -1.0, 1.0, ALU.mult, ALU.add))
                link.close()
                v.sem_inc(s_gafree, LOTS)
                for m, k, n in scan_lots():
                    if m >= 2:
                        v.wait_ge(s_kturn, m - 1)
                    v.tensor_copy(key4[:, m % 2, 0:n, :].rearrange("p k (c h) -> p k c h", h=H),
                                  by_tile(key[:, :], k, n).unsqueeze(3).to_broadcast([P, n, CHUNKS, H])).then_inc(s_kpack, 1)
                link.also(v.memset(cut[:, 0:1], NEG))
                link.also(v.memset(cut[:, SCAN:], NEG))
                v.wait_ge(s_kcopy, len(scan_lots()))
                link(v.tensor_tensor(cut[:, 1:SCAN], tkey[:, 1:], tkey[:, 0:SCAN - 1], ALU.not_equal))
                link(v.tensor_scalar(cut[:, 1:SCAN], cut[:, 1:SCAN], NEG, None, ALU.mult))
                link.close()
                def source_hot(i, h):
                    return v.tensor_tensor(shot[:, h % 2, :].rearrange("p (s n) -> p s n", n=P),
                                           lane[:, :].unsqueeze(1).to_broadcast([P, SELECTED, P]),
                                           lane_at[:, bass.ds(i * STEP + h * LOT + GATHERED, SELECTED)].unsqueeze(2).to_broadcast([P, SELECTED, P]),
                                           ALU.is_equal)

                v.sem_inc(s_sfree, 1)
                make_hot(v, hot[:, 0, :], bass.ds(0, LOT)).then_inc(s_hot, 1)
                source_hot(0, 0).then_inc(s_shot, 1)
                with v.Fori(0, STEPS) as i:
                    for h in range(LOTS):
                        sl = bass.ds(i * STEP + h * LOT, LOT)
                        make_hot(v, hot[:, (h + 1) % 2, :], bass.ds(i * STEP + (h + 1) * LOT, LOT)).then_inc(s_hot, 1)
                        source_hot(i, h + 1).then_inc(s_shot, 1)
                        link(v.tensor_tensor(pairs, lane[:, 0:PAIRS].unsqueeze(1).to_broadcast([P, SELECTED, PAIRS]),
                                             pair_at[:, bass.ds(i * STEP + h * LOT + GATHERED, SELECTED)].unsqueeze(2).to_broadcast([P, SELECTED, PAIRS]),
                                             ALU.is_equal))
                        take(v, s_ssel)
                        for n in range(SELECTED):
                            link.also(v.tensor_tensor(picks[:, n, :].rearrange("p (b h) -> p b h", h=H),
                                                      banks[SOURCE_BANKS[n]][:, 0:PAIRS * H].rearrange("p (b h) -> p b h", h=H),
                                                      pairs[:, n, :].unsqueeze(2).to_broadcast([P, PAIRS, H]), ALU.mult))
                        v.wait_ge(dve_step, link.n)
                        v.sem_inc(s_sfree, 1)
                        link.also(v.tensor_reduce(sg[:, h * LOT + GATHERED:(h + 1) * LOT, :],
                                                  picks.rearrange("p s (b h) -> p s h b", h=H), AX, ALU.add))
                        take(v, s_dsel)
                        dsel = banks[4 + h % 2][:, 0:LOT * 3 * H].rearrange("p (s n) -> p s n", n=3 * H)
                        link.also(v.tensor_copy(selfe[:, sl, :], dsel[:, :, 2 * H:]))
                        link.also(v.tensor_tensor(d0, dsel[:, :, 0:H], nkind[:, sl].unsqueeze(2).to_broadcast([P, LOT, H]), ALU.mult))
                        link(v.tensor_tensor(d1, dsel[:, :, H:2 * H], kind[:, sl].unsqueeze(2).to_broadcast([P, LOT, H]), ALU.mult))
                        v.sem_inc(s_dfree, 1)
                        link(v.tensor_tensor(d0, d0, d1, ALU.add))
                        v.wait_ge(s_ga[h], (i + 1) * (16 * GATHERED))
                        link(v.tensor_tensor(d0, d0, sg[:, h * LOT:(h + 1) * LOT, :], ALU.add))
                        v.sem_inc(s_gafree, 1)
                        link(v.scalar_tensor_tensor(out=alpha[:, sl, :], in0=d0, scalar=0.2, in1=d0, op0=ALU.mult, op1=ALU.max))
                    link.close()

            @block.scalar
            def _(s):
                def turned_copy(h):
                    for q in range(2):
                        take(s, s_hott)
                        s.activation(hotT[:, h % 2, q * 512:(q + 1) * 512], banks[q][:, :], ACT.Copy).then_inc(s_hotc, 1)
                    take(s, s_hott)
                    s.activation(shotT[:, h % 2, :], banks[2][:, 0:SELECTED * P], ACT.Copy).then_inc(s_hotc, 1)

                for h in range(LOTS - 1):
                    copy_numbers(s, s_gafree, s_idx_a, idx_a, srct_at, 0, h)
                for m, k, n in scan_lots():
                    s.wait_ge(s_kturn, m + 1)
                    s.activation(tkey[:, k * P:(k + n) * P], banks[m % 2][:, 0:n * P], ACT.Copy).then_inc(s_kcopy, 1)
                turned_copy(0)
                with s.Fori(0, STEPS) as i:
                    for h in range(LOTS):
                        turned_copy(h + 1)
                        copy_numbers(s, s_gafree, s_idx_a, idx_a, srct_at, i, h + LOTS - 1)

            @block.tensor
            def _(pe):
                def turn(h):
                    take(pe, s_hot)
                    for q in range(2):
                        for j in range(4):
                            last = pe.transpose(banks[q][:, j * P:(j + 1) * P],
                                                hot[:, h % 2, (4 * q + j) * P:(4 * q + j + 1) * P], ident[:, :])
                        last.then_inc(s_hott, 1)
                    take(pe, s_shot)
                    for j in range(SELECTED):
                        last = pe.transpose(banks[2][:, j * P:(j + 1) * P], shot[:, h % 2, j * P:(j + 1) * P], ident[:, :])
                    last.then_inc(s_hott, 1)

                for m, k, n in scan_lots():
                    pe.wait_ge(s_kpack, m + 1)
                    if m >= 2:
                        pe.wait_ge(s_kcopy, m - 1)
                    for j in range(n):
                        last = pe.transpose(banks[m % 2][:, j * P:(j + 1) * P], key4[:, m % 2, j, :], ident[:, :])
                    last.then_inc(s_kturn, 1)
                pe.wait_ge(s_kcopy, len(scan_lots()))
                pe.sem_inc(s_dfree, 2)
                turn(0)
                with pe.Fori(0, STEPS) as i:
                    for h in range(LOTS):
                        blocks = numbers(nc, pe, blk[0:1, bass.ds(i * STEP + h * LOT, LOT)], BLOCKS - 1)
                        take(pe, s_hotc, 3)
                        take(pe, s_sfree)
                        for n in range(SELECTED):
                            last = pe.matmul(banks[SOURCE_BANKS[n]][:, 0:PAIRS * H], shotT[:, h % 2, n * P:(n + 1) * P], stab, start=True, stop=True)
                        last.then_inc(s_ssel, 1)
                        take(pe, s_dfree)
                        for j in range(LOT):
                            last = pe.matmul(banks[4 + h % 2][:, j * 3 * H:(j + 1) * 3 * H], hotT[:, h % 2, j * P:(j + 1) * P],
                                             dtab[:, bass.ds(blocks[j], 1), :], start=True, stop=True)
                        last.then_inc(s_dsel, 1)
                        turn(h + 1)

        turned = at(scan_at, SCAN)
        o = scan_at + 3 * SCAN + 1
        fwd = at(o, SCAN); o += SCAN
        packed = fwd
        mask = (cut[:, 0:SCAN], fwd)
        ends = at(o, 4); o += 4
        endrow = at(o, CHUNKS, 4)[0:H]; o += CHUNKS * 4
        eval_ = at(o, 2 * CHUNKS)[0:H]; o += 2 * CHUNKS
        ekey = at(o, 2 * CHUNKS)[0:H]; o += 2 * CHUNKS
        ecut = at(o, 2 * CHUNKS + 1)[0:H]; o += 2 * CHUNKS + 1
        efwd = at(o, 2 * CHUNKS)[0:H]; o += 2 * CHUNKS
        ebwd = at(o, 2 * CHUNKS)[0:H]; o += 2 * CHUNKS
        eback = at(o, 2); o += 2
        idx_b = at(o, STEP, dt=u32); o += STEP
        acc_at = 30000
        assert o <= acc_at
        sums_in = at(edge_end, SLOTS, 2 * H + 1)
        o = edge_end + SLOTS * (2 * H + 1)
        xg = at(o, STEP, SUMS); o += STEP * SUMS
        hot5 = at(acc_at - 2 * LOT * P, 2, LOT * P)
        assert o <= acc_at - 2 * LOT * P
        acc = at(acc_at, BLOCKS, SUMS)
        acc_odd = at(acc_at + BLOCKS * SUMS, BLOCKS, SUMS)
        HB = LOT // 2
        parts = at(SLOTS * H, 4, HB, SUMS)

        s_cleared = sem("accumulators_cleared")
        s_pack = sem("scores_packed")
        s_ptr = sem("scores_turned")
        s_pcp = sem("turned_scores_copied")
        s_ends = sem("chunk_ends_ready")
        s_cr = sem("chunk_ends_moved")
        s_crback = sem("chunk_maxima_ready")
        s_max = sem("maxima_ready")
        s_bt = sem("maxima_turned")
        s_btfree = sem("turned_maxima_used")
        s_dif = sem("differences_ready")
        s_exp = sem("exponentials_ready")
        s_gb = [sem(f"source_rows_gathered{h}") for h in range(LOTS)]
        s_lot = sem("lot_weighted")
        s_sum = sem("slot_summed")
        s_sumfree = sem("slot_sum_added")
        s_idx_b = sem("source_row_numbers_ready")
        s_part = sem("partial_sums_copied")
        s_partfree = sem("partial_sums_added")

        with nc.Block() as block:
            @block.sync
            def _(sp):
                sp.wait_ge(s_ends, 1)
                sp.dma_start(scratch["ends"], ends).then_inc(s_cr, 16)
                sp.wait_ge(s_cr, 16)
                sp.dma_start(endrow, scratch["ends"].rearrange("(c h) v -> h c v", h=H)).then_inc(s_cr, 16)
                sp.wait_ge(s_crback, 1)
                sp.dma_start(scratch["ends2"].rearrange("(c h) v -> h c v", h=H),
                             ebwd.rearrange("h (c v) -> h c v", v=2)).then_inc(s_cr, 16)
                sp.wait_ge(s_cr, 48)
                sp.dma_start(eback, scratch["ends2"]).then_inc(s_cr, 16)

            @block.gpsimd
            def _(g):
                g.memset(acc, 0.0).then_inc(s_cleared, 1)
                g.memset(acc_odd, 0.0).then_inc(s_cleared, 1)
                g.wait_ge(s_max, 1)
                gather(g, s_idx_b, s_gb, xg[:, :, 0:D], idx_b, scratch["xs"])

            @block.vector
            def _(v):
                link = Chain(v, dve_step)
                for m, k, n in scan_lots():
                    v.tensor_copy(packed[:, k * P:(k + n) * P].rearrange("p (k c h) -> p k c h", c=CHUNKS, h=H),
                                  by_tile(alpha, k, n)).then_inc(s_pack, 1)
                v.wait_ge(s_pcp, len(scan_lots()))
                link(v.tensor_tensor_scan(fwd, cut[:, 0:SCAN], turned, NEG, ALU.add, ALU.max))
                link(v.tensor_tensor_scan(turned[:, ::-1], cut[:, 1:][:, ::-1], fwd[:, ::-1], NEG, ALU.add, ALU.max))
                link.also(v.tensor_copy(ends[:, 0:1], turned[:, 0:1]))
                link.also(v.tensor_copy(ends[:, 1:2], turned[:, SCAN - 1:SCAN]))
                link.also(v.tensor_copy(ends[:, 2:3], tkey[:, 0:1]))
                link(v.tensor_copy(ends[:, 3:4], tkey[:, SCAN - 1:SCAN]))
                v.sem_inc(s_ends, 1)
                for e in range(2):
                    link.also(v.tensor_scalar(mask[e], tkey, ends[:, 2 + e:3 + e], NEG, ALU.not_equal, ALU.mult))
                v.wait_ge(s_cr, 32)
                link.also(v.tensor_copy(eval_.rearrange("h (c v) -> h c v", v=2), endrow[:, :, 0:2]))
                link.also(v.tensor_copy(ekey.rearrange("h (c v) -> h c v", v=2), endrow[:, :, 2:4]))
                link.also(v.memset(ecut[:, 0:1], NEG))
                link(v.memset(ecut[:, 2 * CHUNKS:], NEG))
                link(v.tensor_tensor(ecut[:, 1:2 * CHUNKS], ekey[:, 1:], ekey[:, 0:2 * CHUNKS - 1], ALU.not_equal))
                link(v.tensor_scalar(ecut[:, 1:2 * CHUNKS], ecut[:, 1:2 * CHUNKS], NEG, None, ALU.mult))
                link(v.tensor_tensor_scan(efwd, ecut[:, 0:2 * CHUNKS], eval_, NEG, ALU.add, ALU.max))
                link(v.tensor_tensor_scan(ebwd[:, ::-1], ecut[:, 1:][:, ::-1], efwd[:, ::-1], NEG, ALU.add, ALU.max))
                v.sem_inc(s_crback, 1)
                v.wait_ge(s_cr, 64)
                for e in range(2):
                    link(v.scalar_tensor_tensor(out=turned, in0=mask[e], scalar=eback[:, e:e + 1], in1=turned,
                                                op0=ALU.add, op1=ALU.max))
                v.sem_inc(s_max, 2)
                for m, k, n in scan_lots():
                    v.wait_ge(s_bt, m + 1)
                    v.tensor_tensor(by_tile(mx, k, n), banks[4 + m % 2][:, 0:n * P].rearrange("p (k c h) -> p k c h", c=CHUNKS, h=H),
                                    by_tile(selfe, k, n), ALU.max).then_inc(s_btfree, 1)
                v.wait_ge(s_btfree, len(scan_lots()))
                v.tensor_tensor(alpha, alpha, mx, ALU.subtract).then_inc(s_dif, 1)
                v.tensor_tensor(selfe, selfe, mx, ALU.subtract).then_inc(s_dif, 1)
                link.also(v.memset(sums_in[:, :, 2 * H:], 1.0))
                v.wait_ge(s_exp, 1)
                link(v.tensor_tensor(alpha, sums_in[:, :, 0:H], weight[:, :].unsqueeze(2).to_broadcast([P, SLOTS, H]), ALU.mult))
                link.close()
                v.wait_ge(s_exp, 2)
                v.wait_ge(s_cleared, 2)

                v.sem_inc(s_partfree, 4)

                def weigh(i, h):
                    sl = bass.ds(i * STEP + h * LOT, LOT)
                    link.also(make_hot(v, hot5[:, h % 2, :], sl))
                    link.also(v.tensor_copy(xg[:, h * LOT:(h + 1) * LOT, D:], sums_in[:, sl, :]))
                    v.wait_ge(s_gb[h], (i + 1) * (16 * LOT))
                    rows = xg[:, h * LOT:(h + 1) * LOT, 0:D].rearrange("p s (h c) -> p s h c", c=C)
                    link.also(v.tensor_tensor(rows, rows, alpha[:, sl, :].unsqueeze(3).to_broadcast([P, LOT, H, C]), ALU.mult))

                def weighed():
                    link.close()
                    v.sem_inc(s_lot, 1)

                def blocks_of(i, h):
                    return numbers(nc, v, blk[0:1, bass.ds(i * STEP + h * LOT, LOT)], BLOCKS - 1)

                def add(h, blocks):
                    for j in range(LOT):
                        if j % HB == 0:
                            take(v, s_part)
                        into = (acc, acc_odd)[j % 2][:, bass.ds(blocks[j], 1), :]
                        if j >= 2:
                            v.wait_ge(dve_step, link.n - 1)
                        link.also(v.tensor_tensor(into, into, parts[:, 2 * (h % 2) + j // HB, j % HB, :], ALU.add))
                        if j % HB == HB - 1:
                            v.wait_ge(dve_step, link.n)
                            v.sem_inc(s_partfree, 1)

                with v.Fori(0, STEPS) as i:
                    weigh(i, 0)
                    weighed()
                    for h in range(1, LOTS):
                        weigh(i, h)
                        blocks = blocks_of(i, h - 1)
                        weighed()
                        add(h - 1, blocks)
                    add(LOTS - 1, blocks_of(i, LOTS - 1))
                    link.close()

            @block.scalar
            def _(s):
                def row_numbers(i, h):
                    n = h % LOTS * LOT
                    s.activation(idx_b[:, n:n + LOT], src_at[:, bass.ds(i * STEP + h * LOT, LOT)], ACT.Copy).then_inc(s_idx_b, 1)

                for m, k, n in scan_lots():
                    s.wait_ge(s_ptr, m + 1)
                    s.activation(turned[:, k * P:(k + n) * P], banks[m % 4][:, 0:n * P], ACT.Copy).then_inc(s_pcp, 1)
                for h in range(LOTS):
                    row_numbers(0, h)
                s.wait_ge(s_dif, 1)
                s.activation(sums_in[:, :, 0:H], alpha, ACT.Exp).then_inc(s_exp, 1)
                s.wait_ge(s_dif, 2)
                s.activation(sums_in[:, :, H:2 * H], selfe, ACT.Exp).then_inc(s_exp, 1)

                s.sem_inc(s_sumfree, 2)
                with s.Fori(0, STEPS) as i:
                    for h in range(LOTS):
                        for q in range(2):
                            take(s, s_partfree)
                            for j in range(HB):
                                take(s, s_sum)
                                s.activation(parts[:, 2 * (h % 2) + q, j, :], banks[HB * q + j][:, 0:SUMS], ACT.Copy).then_inc(act_step, 1)
                            take(s, act_step, HB)
                            s.sem_inc(s_sumfree, 1)
                            s.sem_inc(s_part, 1)
                        row_numbers(i, h + LOTS)

            @block.tensor
            def _(pe):
                for m, k, n in scan_lots():
                    pe.wait_ge(s_pack, m + 1)
                    if m >= 4:
                        pe.wait_ge(s_pcp, m - 3)
                    for j in range(n):
                        last = pe.transpose(banks[m % 4][:, j * P:(j + 1) * P],
                                            packed[:, (k + j) * P:(k + j + 1) * P], ident[:, :])
                    last.then_inc(s_ptr, 1)
                pe.wait_ge(s_max, 2)
                for m, k, n in scan_lots():
                    if m >= 2:
                        pe.wait_ge(s_btfree, m - 1)
                    for j in range(n):
                        last = pe.transpose(banks[4 + m % 2][:, j * P:(j + 1) * P], turned[:, (k + j) * P:(k + j + 1) * P], ident[:, :])
                    last.then_inc(s_bt, 1)

                with pe.Fori(0, STEPS) as i:
                    for h in range(LOTS):
                        take(pe, s_lot)
                        for j in range(LOT):
                            if j % HB == 0:
                                take(pe, s_sumfree)
                            pe.matmul(banks[j][:, 0:SUMS], hot5[:, h % 2, j * P:(j + 1) * P], xg[:, h * LOT + j, :],
                                      start=True, stop=True).then_inc(s_sum, 1)

        h1 = at(0, BLOCKS, D)
        xln = at(BLOCKS * D, BLOCKS, D)
        x1 = at(2 * BLOCKS * D, BLOCKS, D)
        o = 3 * BLOCKS * D
        stats = at(o, 3, BLOCKS, 6); o += 3 * BLOCKS * 6
        mean = at(o, 3, BLOCKS); o += 3 * BLOCKS
        rstd = at(o, 3, BLOCKS); o += 3 * BLOCKS
        tmp1 = at(o, BLOCKS); o += BLOCKS
        none_in = at(o, BLOCKS); o += BLOCKS
        rcount = at(o, BLOCKS); o += BLOCKS
        wself = at(o, BLOCKS, H); o += BLOCKS * H
        rden = at(o, BLOCKS, H); o += BLOCKS * H
        fb1 = at(o, KF); o += KF
        vecs = at(o, 6, D); o += 6 * D
        fw1 = at(o, KD, F); o += KD * F
        fw2 = at(o, KF, D); o += KF * D
        hs = at(o, GROUP, D); o += GROUP * D
        assert o <= acc_at
        o = acc_at + BLOCKS * SUMS
        fturn = at(o, KD * GROUP, P); o += KD * GT
        fmid = at(o, KF, GT); o += KF * GT
        gturn = at(o - KF * GT, 2, KD * GROUP, P)
        logits = key[:, 0:BLOCKS * EXPERTS].rearrange("p (b e) -> p b e", e=EXPERTS)
        top = kind[:, 0:BLOCKS * 8].rearrange("p (b n) -> p b n", n=8)
        topi = srct_at[:, 0:BLOCKS * 8].rearrange("p (b n) -> p b n", n=8)
        gw = local[:, 0:KD * EXPERTS].rearrange("p (k e) -> p k e", k=KD)
        gb = local[:, KD * EXPERTS:(KD + 1) * EXPERTS]
        beta = src_at[:, 0:D].bitcast(fp32)
        zeros = weight[:, 0:D]
        DOWN_BANKS = 3
        CLEAR = 6

        s_nin = [sem(f"node_rows_loaded{g}") for g in range(GROUPS)]
        s_x0in = sem("x_rows_loaded")
        s_fw = sem("ffn_weights_loaded")
        s_vec = sem("row_vectors_loaded")
        s_self = sem("self_weights_ready")
        s_own = sem("own_part_ready")
        s_keep = sem("group_kept")
        s_shift = sem("shifted_x_ready")
        s_var1 = sem("ln1_variances_ready")
        s_std1 = sem("ln1_deviations_ready")
        s_hs = sem("group_normalised")
        s_hs_pe = sem("group_to_turn")
        s_ft = sem("group_turned")
        s_ftc = sem("group_turned_copied")
        s_up = sem("hidden_ready")
        s_gelu = sem("gelu_ready")
        s_down = sem("ffn_row_ready")
        s_downfree = sem("ffn_row_used")
        s_var2 = sem("ln2_variances_ready")
        s_std2 = sem("ln2_deviations_ready")
        s_var3 = sem("ln3_variances_ready")
        s_std3 = sem("ln3_deviations_ready")
        s_x1 = sem("layer_output_ready")
        s_x1b = sem("layer_output_shifted")
        s_xn = sem("normed_output_ready")
        s_gw = sem("gate_weights_loaded")
        s_gt = sem("group_turned_for_gate")
        s_gtc = sem("gate_turned_copied")
        s_lg = sem("logits_ready")
        s_zero = sem("zeros_made")
        s_zst = sem("expert_rows_cleared")
        s_x1st = sem("layer_output_stored")

        def spread(vec, n=BLOCKS):
            return vec.unsqueeze(1).to_broadcast([P, n, D])

        def of_group(g):
            return slice(g * GROUP, (g + 1) * GROUP)

        half = GT // 2
        with nc.Block() as block:
            @block.sync
            def _(sp):
                def rows_in(g, buf, src):
                    return sp.dma_start(buf[:, of_group(g), :], src.rearrange("(t p) d -> p t d", p=P)[:, of_group(g), :])

                for g in range(GROUPS):
                    rows_in(g, h1, scratch["xs"]).then_inc(s_nin[g], 16)
                    rows_in(g, xln, scratch["xln"]).then_inc(s_nin[g], 16)
                    if g == 0:
                        sp.wait_ge(s_nin[0], 32)
                        sp.dma_start(fw1, a["ffn_W1T"].rearrange("(k p) n -> p k n", p=P)).then_inc(s_fw, 16)
                        sp.dma_start(fw2, a["ffn_W2T"].rearrange("(k p) n -> p k n", p=P)).then_inc(s_fw, 16)
                sp.dma_start(x1, a["x"].rearrange("(t p) d -> p t d", p=P)).then_inc(s_x0in, 16)
                sp.dma_start(gw, a["gate_w"].rearrange("(k p) n -> p k n", p=P)).then_inc(s_gw, 16)
                sp.dma_start(gb, a["gate_b"].to_broadcast([P, EXPERTS])).then_inc(s_gw, 16)
                sp.dma_start(beta, a["evecs"][1:2, :].to_broadcast([P, D])).then_inc(s_gw, 16)
                sp.wait_ge(s_zero, 1)
                for n in range(TILES_AHEAD // CLEAR):
                    sp.dma_start(scratch["xe"][n * CLEAR * P:(n + 1) * CLEAR * P, :].rearrange("(t p) d -> p t d", p=P),
                                 zeros.unsqueeze(1).to_broadcast([P, CLEAR, D])).then_inc(s_zst, 16)
                for g in range(GROUPS):
                    for ready, name, buf in ((s_xn, "xn", h1), (s_x1b, "x1", x1)):
                        sp.wait_ge(ready, g + 1)
                        sp.dma_start(scratch[name].rearrange("(t p) d -> p t d", p=P)[:, of_group(g), :],
                                     buf[:, of_group(g), :]).then_inc(s_x1st, 16)
                sp.wait_ge(s_x1st, 16 * 2 * GROUPS)
                sp.wait_ge(s_zst, 16 * (TILES_AHEAD // CLEAR))

            @block.gpsimd
            def _(p):
                link = Chain(p, pool_step)

                def own_part(g):
                    rows = of_group(g)
                    p.wait_ge(s_nin[g], 32)
                    own = h1[:, rows, :].rearrange("p t (h c) -> p (t h) c", c=C)
                    if g == 0:
                        p.tensor_tensor(own, own, wself[:, rows, :].rearrange("p t h -> p (t h)").unsqueeze(2).to_broadcast([P, GROUP * H, C]), ALU.mult).then_inc(s_own, 1)
                        return
                    link.also(p.tensor_tensor(xln[:, rows, :], xln[:, rows, :], spread(vecs[:, 0, :], GROUP), ALU.add))
                    link(p.tensor_tensor(own, own, wself[:, rows, :].rearrange("p t h -> p (t h)").unsqueeze(2).to_broadcast([P, GROUP * H, C]), ALU.mult))
                    p.tensor_tensor(xln[:, rows, :], xln[:, rows, :], h1[:, rows, :], ALU.add).then_inc(s_own, 1)

                def keep(g):
                    p.wait_ge(s_hs, g + 1)
                    p.wait_ge(s_own, g + 1)
                    p.tensor_tensor(h1[:, of_group(g), :], hs, spread(vecs[:, 5, :], GROUP), ALU.add).then_inc(s_keep, 1)

                p.memset(zeros, 0.0).then_inc(s_zero, 1)
                p.wait_ge(s_vec, 16 * 6)
                p.wait_ge(s_self, 1)
                own_part(0)
                for g in range(GROUPS):
                    if g + 1 < GROUPS:
                        own_part(g + 1)
                    keep(g)
                    if g == 0:
                        p.wait_ge(s_x0in, 16)
                        p.tensor_tensor(x1, x1, spread(vecs[:, 4, :]), ALU.add).then_inc(s_shift, 1)
                p.wait_ge(s_gw, 48)
                for g in range(GROUPS):
                    rows = of_group(g)
                    p.wait_ge(s_xn, g + 1)
                    p.tensor_tensor(x1[:, rows, :], x1[:, rows, :], spread(beta, GROUP), ALU.add).then_inc(s_x1b, 1)
                link.close()

            @block.scalar
            def _(s):
                for n in range(6):
                    s.dma_start(vecs[:, n, :], a["vecs"][n:n + 1, :].to_broadcast([P, D])).then_inc(s_vec, 16)
                s.dma_start(fb1, a["ffn_b1"]).then_inc(s_fw, 16)

                def root(g, n, s_var, s_std):
                    if 0 <= g < GROUPS:
                        s.wait_ge(s_var, g + 1)
                        s.activation(rstd[:, n, of_group(g)], rstd[:, n, of_group(g)], ACT.Sqrt).then_inc(s_std, 1)

                def turned_copies(g):
                    for q in range(3):
                        s.wait_ge(s_ft, 3 * g + q + 1)
                        n = min(4, KD * GROUP - 4 * q)
                        s.activation(fturn[:, 4 * q:4 * q + n, :], banks[q][:, 0:n * P].rearrange("p (n e) -> p n e", e=P),
                                     ACT.Copy).then_inc(s_ftc, 1)

                root(0, 0, s_var1, s_std1)
                turned_copies(0)
                s.wait_ge(s_fw, 16 * 3)
                for g in range(GROUPS):
                    for f in range(KF):
                        for u in range(2):
                            s.wait_ge(s_up, 2 * (g * KF + f) + u + 1)
                            s.activation(fmid[:, f, u * half:(u + 1) * half], banks[3 + u][:, 0:half], ACT.Gelu,
                                         bias=fb1[:, f:f + 1]).then_inc(s_gelu, 1)
                    root(g + 1, 0, s_var1, s_std1)
                    root(g - 1, 1, s_var2, s_std2)
                    root(g - 2, 2, s_var3, s_std3)
                    if g + 1 < GROUPS:
                        turned_copies(g + 1)
                root(GROUPS - 1, 1, s_var2, s_std2)
                for g in range(GROUPS):
                    if g == 2:
                        root(GROUPS - 2, 2, s_var3, s_std3)
                    if g == GROUPS - 2:
                        root(GROUPS - 1, 2, s_var3, s_std3)
                    for q in range(3):
                        s.wait_ge(s_gt, 3 * g + q + 1)
                        n = min(4, KD * GROUP - 4 * q)
                        s.activation(gturn[:, g % 2, 4 * q:4 * q + n, :], banks[q][:, 0:n * P].rearrange("p (n e) -> p n e", e=P),
                                     ACT.Copy).then_inc(s_gtc, 1)

            @block.vector
            def _(v):
                link = Chain(v, dve_step)
                link(v.tensor_tensor(acc[:, :, D:], acc[:, :, D:], acc_odd[:, :, D:], ALU.add))
                count = acc[:, :, D + 2 * H]
                link.also(v.tensor_scalar(none_in, count, 0.0, None, ALU.is_equal))
                link(v.tensor_scalar(rcount, count, 1.0, None, ALU.max))
                link(v.reciprocal(rcount, rcount))
                link(v.tensor_tensor(wself, acc[:, :, D + H:D + 2 * H], none_in.unsqueeze(2).to_broadcast([P, BLOCKS, H]), ALU.add))
                link(v.tensor_tensor(wself, wself, rcount.unsqueeze(2).to_broadcast([P, BLOCKS, H]), ALU.mult))
                link(v.tensor_tensor(rden, acc[:, :, D:D + H], wself, ALU.add))
                link(v.reciprocal(rden, rden))
                link(v.tensor_tensor(wself, wself, rden, ALU.mult))
                v.sem_inc(s_self, 1)
                v.sem_inc(s_downfree, GROUP)
                link(v.tensor_tensor(acc[:, :, 0:D], acc[:, :, 0:D], acc_odd[:, :, 0:D], ALU.add))

                def scales(g, n, s_var):
                    rows = of_group(g)
                    v.wait_ge(dve_step, link.n)
                    stats_to_scales(v, link, stats[:, n, rows, :], mean[:, n, rows], rstd[:, n, rows], tmp1[:, rows]).then_inc(s_var, 1)

                def one_over(g, n, s_std):
                    v.wait_ge(s_std, g + 1)
                    link(v.reciprocal(rstd[:, n, of_group(g)], rstd[:, n, of_group(g)]))

                def normed(g, n, src, gain, shift, dst):
                    for b in range(g * GROUP, (g + 1) * GROUP):
                        link.also(v.scalar_tensor_tensor(out=src[:, b, 0:D], in0=src[:, b, 0:D], scalar=mean[:, n, b:b + 1], in1=gain,
                                                         op0=ALU.subtract, op1=ALU.mult))
                    for b in range(g * GROUP, (g + 1) * GROUP):
                        v.wait_ge(dve_step, link.n - GROUP + 1)
                        link.also(v.scalar_tensor_tensor(out=dst(b), in0=src[:, b, 0:D], scalar=rstd[:, n, b:b + 1], in1=shift(b),
                                                         op0=ALU.mult, op1=ALU.add))
                    v.wait_ge(dve_step, link.n)

                def attention(g):
                    rows = of_group(g)
                    got = acc[:, rows, 0:D]
                    sums = got.rearrange("p t (h c) -> p t h c", c=C)
                    link(v.tensor_tensor(sums, sums, rden[:, rows, :].unsqueeze(3).to_broadcast([P, GROUP, H, C]), ALU.mult))
                    if g == 0:
                        v.wait_ge(s_nin[0], 32)
                        v.wait_ge(s_vec, 16 * 6)
                        link(v.tensor_tensor(xln[:, rows, :], xln[:, rows, :], spread(vecs[:, 0, :], GROUP), ALU.add))
                        link(v.tensor_tensor(got, got, xln[:, rows, :], ALU.add))
                        v.wait_ge(s_own, 1)
                        link(v.tensor_tensor(got, got, h1[:, rows, :], ALU.add))
                    else:
                        v.wait_ge(s_own, g + 1)
                        link(v.tensor_tensor(got, got, xln[:, rows, :], ALU.add))
                    for b in range(g * GROUP, (g + 1) * GROUP):
                        link.also(v.bn_stats(stats[:, 0, b, :], acc[:, b, 0:D]))
                    scales(g, 0, s_var1)

                def first_norm(g):
                    one_over(g, 0, s_std1)
                    if g:
                        v.wait_ge(s_ft, 3 * g)
                        v.wait_ge(s_keep, g)
                    normed(g, 0, acc, vecs[:, 1, :], lambda b: vecs[:, 2, :], lambda b: hs[:, b % GROUP, :])
                    v.sem_inc(s_hs, 1)
                    v.sem_inc(s_hs_pe, 1)

                def residual(g):
                    v.wait_ge(s_keep, g + 1)
                    for j in range(GROUP):
                        b = g * GROUP + j
                        v.wait_ge(s_down, b + 1)
                        link(v.tensor_tensor(xln[:, b, :], banks[5 + j % DOWN_BANKS][:, 0:D], h1[:, b, :], ALU.add))
                        v.sem_inc(s_downfree, 1)
                        link.also(v.bn_stats(stats[:, 1, b, :], xln[:, b, :]))
                    scales(g, 1, s_var2)

                def second_norm(g):
                    one_over(g, 1, s_std2)
                    v.wait_ge(s_shift, 1)
                    normed(g, 1, xln, vecs[:, 3, :], lambda b: x1[:, b, :], lambda b: x1[:, b, :])
                    v.sem_inc(s_x1, 1)
                    for b in range(g * GROUP, (g + 1) * GROUP):
                        link.also(v.bn_stats(stats[:, 2, b, :], x1[:, b, :]))
                    scales(g, 2, s_var3)

                def third_norm(g):
                    one_over(g, 2, s_std3)
                    for b in range(g * GROUP, (g + 1) * GROUP):
                        link.also(v.tensor_scalar(h1[:, b, :], x1[:, b, :], mean[:, 2, b:b + 1], rstd[:, 2, b:b + 1], ALU.subtract, ALU.mult))
                    v.wait_ge(dve_step, link.n)
                    v.sem_inc(s_xn, 1)

                def choose(g):
                    if g == 0:
                        v.wait_ge(s_gw, 48)
                    rows = of_group(g)
                    v.wait_ge(s_lg, g + 1)
                    link(v.tensor_tensor(logits[:, rows, :], banks[3 + g][:, 0:GROUP * EXPERTS].rearrange("p (b e) -> p b e", e=EXPERTS),
                                         gb.unsqueeze(1).to_broadcast([P, GROUP, EXPERTS]), ALU.add))
                    for b in range(g * GROUP, (g + 1) * GROUP):
                        link.also(v.max(top[:, b, :], logits[:, b, :]))
                    v.wait_ge(dve_step, link.n)
                    for b in range(g * GROUP, (g + 1) * GROUP):
                        link.also(v.max_index(topi[:, b, :], top[:, b, :], logits[:, b, :]))

                attention(0)
                first_norm(0)
                for g in range(GROUPS + 2):
                    if g + 1 < GROUPS:
                        attention(g + 1)
                        first_norm(g + 1)
                    if g < GROUPS:
                        residual(g)
                    if 0 <= g - 1 < GROUPS:
                        second_norm(g - 1)
                    if g == GROUPS + 1:
                        for c in range(GROUPS - 2):
                            choose(c)
                    if 0 <= g - 2 < GROUPS:
                        third_norm(g - 2)
                for c in range(GROUPS - 2, GROUPS):
                    choose(c)
                link.close()

            @block.tensor
            def _(pe):
                def turn():
                    take(pe, s_hs_pe)
                    for n in range(KD * GROUP):
                        k, j = divmod(n, GROUP)
                        last = pe.transpose(banks[n // 4][:, n % 4 * P:(n % 4 + 1) * P], hs[:, j, k * P:(k + 1) * P], ident[:, :])
                        if n % 4 == 3 or n == KD * GROUP - 1:
                            last.then_inc(s_ft, 1)

                def up():
                    take(pe, s_ftc, 3)
                    turned_in = fturn.rearrange("p (k j) e -> p k (j e)", k=KD)
                    for f in range(KF):
                        for u in range(2):
                            if f >= 1:
                                take(pe, s_gelu)
                            for k in range(KD):
                                last = pe.matmul(banks[3 + u][:, 0:half], fw1[:, k, f * P:(f + 1) * P],
                                                 turned_in[:, k, u * half:(u + 1) * half], start=(k == 0), stop=(k == KD - 1))
                            last.then_inc(s_up, 1)

                def down(j):
                    if j == 0:
                        take(pe, s_downfree, GROUP)
                        take(pe, s_gelu, 2)
                    elif j >= DOWN_BANKS:
                        pe.wait_ge(s_downfree, j - DOWN_BANKS + 1)
                    for f in range(KF):
                        last = pe.matmul(banks[5 + j % DOWN_BANKS][:, 0:D], fmid[:, f, j * P:(j + 1) * P], fw2[:, f, :],
                                         start=(f == 0), stop=(f == KF - 1))
                    last.then_inc(s_down, 1)

                pe.wait_ge(s_fw, 16 * 3)
                turn()
                with pe.Fori(0, GROUPS - 1) as i:
                    up()
                    down(0)
                    down(1)
                    turn()
                    for j in range(2, GROUP):
                        down(j)
                up()
                for j in range(GROUP):
                    down(j)

                def gate_turn(g):
                    pe.wait_ge(s_xn, g + 1)
                    for n in range(KD * GROUP):
                        k, j = divmod(n, GROUP)
                        last = pe.transpose(banks[n // 4][:, n % 4 * P:(n % 4 + 1) * P], h1[:, g * GROUP + j, k * P:(k + 1) * P], ident[:, :])
                        if n % 4 == 3 or n == KD * GROUP - 1:
                            last.then_inc(s_gt, 1)

                pe.wait_ge(s_gw, 48)
                gate_turn(0)
                for g in range(GROUPS):
                    if 3 + g == 5:
                        pe.wait_ge(s_downfree, GROUP)
                    pe.wait_ge(s_gtc, 3 * (g + 1))
                    for j in range(GROUP):
                        for k in range(KD):
                            last = pe.matmul(banks[3 + g][:, j * EXPERTS:(j + 1) * EXPERTS], gturn[:, g % 2, k * GROUP + j, :], gw[:, k, :],
                                             start=(k == 0), stop=(k == KD - 1))
                    last.then_inc(s_lg, 1)
                    if g + 1 < GROUPS:
                        gate_turn(g + 1)

        xn = at(0, BLOCKS, D)
        o = BLOCKS * D
        cmp = at(o, TILES_AHEAD, EXPERTS); o += TILES_AHEAD * EXPERTS
        topf = at(o, 2, BLOCKS); o += 2 * BLOCKS
        chosen = at(o, ASSIGN, EXPERTS); o += ASSIGN * EXPERTS
        upto = at(o, ASSIGN, EXPERTS); o += ASSIGN * EXPERTS
        ntile = at(o, EXPERTS); o += EXPERTS
        ntile_i = at(o, EXPERTS, dt=i32); o += EXPERTS
        cum = at(o, EXPERTS); o += EXPERTS
        base = at(o, EXPERTS); o += EXPERTS
        tileno = at(o, TILES_AHEAD); o += TILES_AHEAD
        tile_exp = at(o, TILES_AHEAD); o += TILES_AHEAD
        posf = at(o, ASSIGN); o += ASSIGN
        real = at(o, 1); o += 1
        spare = at(o, 2); o += 2
        inpart = at(o, 1); o += 1
        ew_at = ARENA - EXPERTS * (KD * FE + KE * D)
        NB = FE + D
        bias_at = ew_at - 2 * NB
        biases = at(bias_at, NB)[0:PARTS * QUAD]
        bpart = at(bias_at + NB, NB // 2, dt=bf16)[0:PARTS * QUAD]
        bparts = at(bias_at + NB + NB // 2, NB // 2, dt=bf16)[0:PARTS * QUAD]
        assert o <= bias_at
        ew1 = at(ew_at, EXPERTS, KD * FE)
        ew2 = at(ew_at + EXPERTS * KD * FE, EXPERTS, KE * D)
        mixw = sb("mixw", [P, 2, BLOCKS])
        pos = sb("pos", [P, ASSIGN], u32)
        texp = sb("texp", [P, TILES_AHEAD], i32)
        pick = sb("pick", [PARTS * QUAD, TILES_AHEAD], bf16)

        s_tile = sem("tile_numbers_ready")
        s_bclear = sem("bias_rows_cleared")
        s_bias = sem("biases_loaded")
        s_e2 = sem("second_difference_ready")
        s_e2x = sem("second_exponential_ready")
        s_chosen = sem("choices_ready")
        s_ranks = sem("ranks_ready")
        s_pos = sem("rows_assigned")
        s_scat = sem("rows_scattered")
        s_ew = sem("expert_weights_loaded")
        with nc.Block() as block:
            @block.sync
            def _(sp):
                sp.wait_ge(s_bclear, 1)
                for n in range(PARTS):
                    sp.dma_start(biases[n * QUAD:n * QUAD + EXPERTS, :], a["ebias"]).then_inc(s_bias, 16)
                for e in range(EXPERTS):
                    sp.dma_start(ew1[:, e, :].rearrange("p (k f) -> p k f", k=KD), a["ew1"][e].rearrange("(k p) f -> p k f", p=P)).then_inc(s_ew, 16)
                    sp.dma_start(ew2[:, e, :].rearrange("p (k f) -> p k f", k=KE), a["ew2"][e].rearrange("(k p) f -> p k f", p=P)).then_inc(s_ew, 16)

            @block.gpsimd
            def _(g):
                g.memset(biases, 0.0).then_inc(s_bclear, 1)
                g.iota(tileno, pattern=[[1, TILES_AHEAD]], base=0, channel_multiplier=0,
                       allow_small_or_imprecise_dtypes=True).then_inc(s_tile, 1)
                g.wait_ge(s_pos, 1)
                for j in range(ASSIGN):
                    g.indirect_dma_start(out=scratch["xe"], out_offset=bass.IndirectOffsetOnAxis(ap=pos[:, j:j + 1], axis=0),
                                         in_=xn[:, j % BLOCKS, :], in_offset=None).then_inc(s_scat, 16)
                g.wait_ge(s_scat, 16 * ASSIGN)

            @block.vector
            def _(v):
                link = Chain(v, dve_step)
                link(v.tensor_tensor(mixw[:, 1, :], top[:, :, 1], top[:, :, 0], ALU.subtract))
                v.sem_inc(s_e2, 1)
                link.also(v.tensor_copy(topf[:, 0, :], topi[:, :, 0]))
                link.also(v.tensor_scalar(real, part[:, :], float(N_NODES - (BLOCKS - 1) * P), None, ALU.is_lt))
                link(v.tensor_copy(topf[:, 1, :], topi[:, :, 1]))
                link(v.tensor_tensor(chosen, lane[:, 0:EXPERTS].unsqueeze(1).to_broadcast([P, ASSIGN, EXPERTS]),
                                     topf.rearrange("p k b -> p (k b)").unsqueeze(2).to_broadcast([P, ASSIGN, EXPERTS]), ALU.is_equal))
                for n in (BLOCKS - 1, ASSIGN - 1):
                    link.also(v.tensor_scalar(chosen[:, n, :], chosen[:, n, :], real, None, ALU.mult))
                v.wait_ge(dve_step, link.n)
                v.sem_inc(s_chosen, 1)
                link(v.memset(cmp, 1.0))
                v.wait_ge(s_e2x, 1)
                link(v.tensor_scalar(mixw[:, 0, :], mixw[:, 1, :], 1.0, None, ALU.add))
                link(v.reciprocal(mixw[:, 0, :], mixw[:, 0, :]))
                link.also(v.tensor_tensor(mixw[:, 1, :], mixw[:, 1, :], mixw[:, 0, :], ALU.mult))
                for n in range(2):
                    link.also(v.tensor_scalar(spare[:, n:n + 1], part[:, :], float((TILES + n) * P), None, ALU.add))
                    v.wait_ge(dve_step, link.n)
                    link.also(v.scalar_tensor_tensor(out=spare[:, n:n + 1], in0=real, scalar=0.0, in1=spare[:, n:n + 1],
                                                     op0=ALU.is_equal, op1=ALU.mult))
                hw = ASSIGN // 2

                def in_psum(n, u):
                    return banks[n + u][:, 0:hw * EXPERTS].rearrange("p (j e) -> p j e", e=EXPERTS)

                v.wait_ge(s_ranks, 2)
                for e in range(EXPERTS):
                    link.also(v.tensor_tensor_scan(upto[:, 0:hw, e], cmp[:, 0:hw, 0], in_psum(4, 0)[:, :, e], 0.0, ALU.mult, ALU.add))
                v.wait_ge(dve_step, link.n)
                for e in range(EXPERTS):
                    link.also(v.tensor_tensor_scan(upto[:, hw:, e], cmp[:, 0:hw, 0], in_psum(4, 1)[:, :, e],
                                                   upto[:, hw - 1, e:e + 1], ALU.mult, ALU.add))
                v.wait_ge(dve_step, link.n)
                link(v.tensor_scalar(ntile_i, upto[:, ASSIGN - 1, :], float(P - 1), None, ALU.add))
                link(v.tensor_single_scalar(ntile_i, ntile_i, 7, ALU.arith_shift_right))
                link(v.tensor_copy(ntile, ntile_i))
                link(v.tensor_tensor_scan(cum, cmp[:, 0, :], ntile, 0.0, ALU.mult, ALU.add))
                link(v.tensor_tensor(base, cum, ntile, ALU.subtract))
                link(v.tensor_scalar(base, base, float(P), None, ALU.mult))
                v.wait_ge(s_ranks, 4)
                for u in range(2):
                    cols = upto[:, u * hw:(u + 1) * hw, :]
                    link.also(v.tensor_tensor(cols, cols, in_psum(2, u), ALU.add))
                v.wait_ge(dve_step, link.n)
                link(v.tensor_tensor(upto, upto, base.unsqueeze(1).to_broadcast([P, ASSIGN, EXPERTS]), ALU.add))
                link(v.tensor_tensor(upto, upto, chosen, ALU.mult))
                link(v.tensor_reduce(posf, upto, AX, ALU.add))
                for n, column in enumerate((BLOCKS - 1, ASSIGN - 1)):
                    link.also(v.tensor_tensor(posf[:, column:column + 1], posf[:, column:column + 1], spare[:, n:n + 1], ALU.add))
                v.wait_ge(dve_step, link.n)
                link(v.tensor_copy(pos[:, :], posf))
                v.sem_inc(s_pos, 1)
                v.wait_ge(s_tile, 1)
                link(v.tensor_tensor(cmp, cum.unsqueeze(1).to_broadcast([P, TILES_AHEAD, EXPERTS]),
                                     tileno.unsqueeze(2).to_broadcast([P, TILES_AHEAD, EXPERTS]), ALU.is_le))
                link(v.tensor_reduce(tile_exp, cmp, AX, ALU.add))
                link(v.tensor_scalar(tile_exp, tile_exp, float(EXPERTS - 1), None, ALU.min))
                link.also(v.tensor_copy(texp[:, :], tile_exp))
                link(v.tensor_copy(inpart, part[:, :]))
                for n in range(1, PARTS):
                    rows = inpart[n * QUAD:(n + 1) * QUAD]
                    link.also(v.tensor_scalar(rows, rows, -float(n * QUAD), None, ALU.add))
                v.wait_ge(dve_step, link.n)
                link(v.tensor_scalar(pick[:, :], tile_exp[0:PARTS * QUAD], inpart[0:PARTS * QUAD], None, ALU.is_equal))
                v.wait_ge(s_bias, 16 * PARTS)
                link(v.tensor_copy(bpart, biases))
                link.also(v.tensor_copy(bparts[0:QUAD], bpart[0:QUAD]))
                link(v.tensor_tensor(biases, biases, bpart, ALU.subtract))
                link(v.tensor_copy(bpart, biases))
                link.also(v.tensor_copy(bparts[QUAD:2 * QUAD], bpart[QUAD:2 * QUAD]))
                link(v.tensor_tensor(biases, biases, bpart, ALU.subtract))
                link(v.tensor_copy(bparts[2 * QUAD:], biases[2 * QUAD:]))
                link.close()

            @block.scalar
            def _(s):
                s.wait_ge(s_e2, 1)
                s.activation(mixw[:, 1, :], mixw[:, 1, :], ACT.Exp).then_inc(s_e2x, 1)

            @block.tensor
            def _(pe):
                pe.wait_ge(s_chosen, 1)
                hw = ASSIGN // 2
                for bank, which in ((4, ones), (2, from_on)):
                    for u in range(2):
                        part_of = chosen[:, u * hw:(u + 1) * hw, :].rearrange("p j e -> p (j e)")
                        pe.matmul(banks[bank + u][:, 0:hw * EXPERTS], which[:, :], part_of, start=True, stop=True).then_inc(s_ranks, 1)

        o = 0
        ein = at(o, TURN, D); o += TURN * D
        eturn = at(o, 2, KD, P); o += 2 * KD * P
        ehid = at(o, 2, FE); o += 2 * FE
        ehturn = at(o, 2, KE, P); o += 2 * KE * P
        eout = at(o, TURN, D); o += TURN * D
        PICKS = 4
        epick = at(o, PICKS * P // 2, dt=bf16)[0:PARTS * QUAD].rearrange("p (u n) -> p u n", u=PICKS); o += PICKS * P // 2
        assert o <= bias_at

        s_ein = [sem(f"expert_tile_loaded{j}") for j in range(TURN)]
        s_einfree = sem("expert_tile_used")
        s_epick = sem("expert_picked")
        s_et = sem("expert_tile_turned")
        s_etc = sem("expert_turned_copied")
        s_eh = sem("expert_hidden_ready")
        s_er = sem("expert_hidden_clipped")
        s_eht = sem("expert_hidden_turned")
        s_ehc = sem("expert_hidden_copied")
        s_ey = sem("expert_product_ready")
        s_eyc = sem("expert_output_ready")
        s_eys = [sem(f"expert_output_stored{j}") for j in range(TURN)]
        s_eofree = sem("expert_output_free")
        TURNS = TILES // TURN
        xe_t = scratch["xe"].rearrange("(t p) d -> p t d", p=P)
        ye_t = scratch["ye"].rearrange("(t p) d -> p t d", p=P)
        with nc.Block() as block:
            @block.sync
            def _(sp):
                for j in range(2):
                    sp.dma_start(ein[:, j, :], xe_t[:, j, :]).then_inc(s_ein[j], 16)
                with sp.Fori(0, TURNS) as i:
                    for j in range(2, TURN + 2):
                        take(sp, s_einfree)
                        sp.dma_start(ein[:, j % TURN, :], xe_t[:, bass.ds(i * TURN + j, 1), :]).then_inc(s_ein[j % TURN], 16)

            @block.gpsimd
            def _(g):
                with g.Fori(0, TURNS) as i:
                    for j in range(TURN):
                        take(g, s_eyc)
                        g.dma_start(ye_t[:, bass.ds(i * TURN + j, 1), :], eout[:, j, :]).then_inc(s_eys[j], 16)
                    for j in range(TURN):
                        g.wait_ge(s_eys[j], 16 * (i + 1))
                        g.sem_inc(s_eofree, 1)

            @block.vector
            def _(v):
                link = Chain(v, dve_step)
                link(v.tensor_single_scalar(pos[:, :], pos[:, :], TILES * P - 1, ALU.min))
                link.close()
                v.sem_inc(s_eofree, TURN)
                v.sem_inc(s_einfree, TURN - 2)

                def picked(i, j):
                    v.tensor_copy(epick[:, j % PICKS, :], pick[:, bass.ds(i * TURN + j, 1)].to_broadcast([PARTS * QUAD, P])).then_inc(s_epick, 1)

                picked(0, 0)
                picked(0, 1)
                with v.Fori(0, TURNS) as i:
                    for j in range(TURN):
                        picked(i, j + 2)
                        take(v, s_eht)
                        v.tensor_copy(ehturn[:, j % 2, :, :].rearrange("p k n -> p (k n)"), banks[4 + j % 2][:, :]).then_inc(s_ehc, 1)
                        take(v, s_eofree)
                        take(v, s_ey)
                        v.tensor_copy(eout[:, j, :], banks[6 + j % 2][:, 0:D]).then_inc(s_eyc, 1)

            @block.scalar
            def _(s):
                def turned_copy(j):
                    take(s, s_et)
                    s.activation(eturn[:, j % 2, :, :].rearrange("p k n -> p (k n)"), banks[j % 2][:, 0:D], ACT.Copy).then_inc(s_etc, 1)

                def clip(j):
                    take(s, s_eh)
                    s.activation(ehid[:, j % 2, :], banks[2 + j % 2][:, :], ACT.Relu).then_inc(s_er, 1)

                turned_copy(0)
                turned_copy(1)
                clip(0)
                with s.Fori(0, TURNS) as i:
                    for j in range(TURN):
                        turned_copy(j)
                        clip(j + 1)

            @block.tensor
            def _(pe):
                def turn_in(loads, j):
                    pe.wait_ge(s_ein[j % TURN], 16 * loads)
                    for k in range(KD):
                        last = pe.transpose(banks[j % 2][:, k * P:(k + 1) * P], ein[:, j % TURN, k * P:(k + 1) * P], ident[:, :])
                    last.then_inc(s_et, 1)

                def first_product(i, j):
                    e, = numbers(nc, pe, texp[0:1, bass.ds(i * TURN + j, 1)], EXPERTS - 1)
                    take(pe, s_epick)
                    take(pe, s_etc)
                    pe.sem_inc(s_einfree, 1)
                    hid = banks[2 + j % 2][:, :]
                    pe.matmul(hid, epick[:, j % PICKS, :], bparts[:, 0:FE], start=True, stop=False)
                    for k in range(KD):
                        last = pe.matmul(hid, eturn[:, j % 2, k, :], ew1[:, bass.ds(e, 1), k * FE:(k + 1) * FE],
                                         start=False, stop=(k == KD - 1))
                    last.then_inc(s_eh, 1)

                pe.wait_ge(s_ew, 16 * 2 * EXPERTS)
                turn_in(1, 0)
                turn_in(1, 1)
                first_product(0, 0)
                with pe.Fori(0, TURNS) as i:
                    for j in range(TURN):
                        take(pe, s_er)
                        for k in range(KE):
                            last = pe.transpose(banks[4 + j % 2][:, k * P:(k + 1) * P], ehid[:, j % 2, k * P:(k + 1) * P], ident[:, :])
                        last.then_inc(s_eht, 1)
                        turn_in(i + 1 + (j + 2) // TURN, j + 2)
                        first_product(i, j + 1)
                        e, = numbers(nc, pe, texp[0:1, bass.ds(i * TURN + j, 1)], EXPERTS - 1)
                        prod = banks[6 + j % 2][:, 0:D]
                        pe.matmul(prod, epick[:, j % PICKS, :], bparts[:, FE:NB], start=True, stop=False)
                        take(pe, s_ehc)
                        for k in range(KE):
                            last = pe.matmul(prod, ehturn[:, j % 2, k, :], ew2[:, bass.ds(e, 1), k * D:(k + 1) * D],
                                             start=False, stop=(k == KE - 1))
                        last.then_inc(s_ey, 1)

        ya = at(0, BLOCKS, D)
        yb = at(BLOCKS * D, BLOCKS, D)
        x1 = at(2 * BLOCKS * D, BLOCKS, D)
        xn = at(3 * BLOCKS * D, BLOCKS, D)
        yn = at(4 * BLOCKS * D, BLOCKS, D)
        o = 5 * BLOCKS * D
        stats = at(o, BLOCKS, 6); o += BLOCKS * 6
        mean = at(o, BLOCKS); o += BLOCKS
        rstd = at(o, BLOCKS); o += BLOCKS
        tmp1 = at(o, BLOCKS); o += BLOCKS
        gamma = at(o, D); o += D
        s_c9 = sem("combine_rows_loaded")
        s_gamma = sem("gamma_loaded")
        s_y = [sem(f"expert_rows_gathered{g}") for g in range(GROUPS)]
        s_var9 = sem("ln4_variances_ready")
        s_std9 = sem("ln4_deviations_ready")
        s_sh9 = sem("ln4_shifts_ready")
        s_nr9 = sem("ln4_normalised")
        s_fin = sem("result_ready")
        s_out = sem("result_stored")
        whole = N_NODES // P
        with nc.Block() as block:
            @block.sync
            def _(sp):
                for g in range(GROUPS):
                    for buf, name in ((xn, "xn"), (x1, "x1")):
                        sp.dma_start(buf[:, of_group(g), :], scratch[name].rearrange("(t p) d -> p t d", p=P)[:, of_group(g), :]
                                     ).then_inc(s_c9, 16)
                    sp.wait_ge(s_c9, 32 * (g + 1))
                    if g == 0:
                        sp.dma_start(gamma, a["evecs"][0:1, :].to_broadcast([P, D])).then_inc(s_gamma, 16)
                for g in range(GROUPS):
                    first, last = g * GROUP, min((g + 1) * GROUP, whole)
                    sp.wait_ge(s_fin, g + 1)
                    sp.dma_start(out[first * P:last * P, :].rearrange("(t p) d -> p t d", p=P), yn[:, first:last, :]).then_inc(s_out, 16)
                sp.dma_start(out[whole * P:, :], yn[0:N_NODES - whole * P, whole, :]).then_inc(s_out, 16)
                sp.wait_ge(s_out, 16 * (BLOCKS // GROUP + 1))

            @block.gpsimd
            def _(g):
                for b in range(BLOCKS):
                    for n, rows in enumerate((ya, yb)):
                        g.indirect_dma_start(out=rows[:, b, :], out_offset=None, in_=scratch["ye"],
                                             in_offset=bass.IndirectOffsetOnAxis(ap=pos[:, n * BLOCKS + b:n * BLOCKS + b + 1], axis=0)
                                             ).then_inc(s_y[b // GROUP], 16)

            @block.vector
            def _(v):
                link = Chain(v, dve_step)
                v.wait_ge(s_gamma, 16)

                def finish(g):
                    rows = slice(g * GROUP, (g + 1) * GROUP)
                    v.wait_ge(s_nr9, GROUP * (g + 1))
                    link(v.tensor_tensor(yn[:, rows, :], yn[:, rows, :], spread(gamma, GROUP), ALU.mult))
                    link(v.tensor_tensor(yn[:, rows, :], yn[:, rows, :], x1[:, rows, :], ALU.add))
                    v.sem_inc(s_fin, 1)

                for g in range(GROUPS):
                    rows = slice(g * GROUP, (g + 1) * GROUP)
                    v.wait_ge(s_c9, 32 * (g + 1))
                    v.wait_ge(s_y[g], 16 * 2 * GROUP)
                    for b in range(g * GROUP, (g + 1) * GROUP):
                        link.also(v.scalar_tensor_tensor(out=ya[:, b, :], in0=ya[:, b, :], scalar=mixw[:, 0, b:b + 1], in1=xn[:, b, :],
                                                         op0=ALU.mult, op1=ALU.add))
                    for n, b in enumerate(range(g * GROUP, (g + 1) * GROUP)):
                        v.wait_ge(dve_step, link.n - GROUP + 1)
                        link.also(v.scalar_tensor_tensor(out=ya[:, b, :], in0=yb[:, b, :], scalar=mixw[:, 1, b:b + 1], in1=ya[:, b, :],
                                                         op0=ALU.mult, op1=ALU.add))
                    for n, b in enumerate(range(g * GROUP, (g + 1) * GROUP)):
                        v.wait_ge(dve_step, link.n - GROUP + 1)
                        link.also(v.bn_stats(stats[:, b, :], ya[:, b, :]))
                    v.wait_ge(dve_step, link.n)
                    stats_to_scales(v, link, stats[:, rows, :], mean[:, rows], rstd[:, rows], tmp1[:, rows]).then_inc(s_var9, 1)
                    if g:
                        finish(g - 1)
                    v.wait_ge(s_std9, g + 1)
                    link(v.reciprocal(rstd[:, rows], rstd[:, rows]))
                    link(v.scalar_tensor_tensor(out=mean[:, rows], in0=mean[:, rows], scalar=-1.0, in1=rstd[:, rows],
                                                op0=ALU.mult, op1=ALU.mult))
                    v.sem_inc(s_sh9, 1)
                finish(GROUPS - 1)
                link.close()

            @block.scalar
            def _(s):
                for g in range(GROUPS):
                    rows = slice(g * GROUP, (g + 1) * GROUP)
                    s.wait_ge(s_var9, g + 1)
                    s.activation(rstd[:, rows], rstd[:, rows], ACT.Sqrt).then_inc(s_std9, 1)
                    s.wait_ge(s_sh9, g + 1)
                    for b in range(g * GROUP, (g + 1) * GROUP):
                        s.activation(yn[:, b, :], ya[:, b, :], ACT.Identity, bias=mean[:, b:b + 1], scale=rstd[:, b:b + 1]).then_inc(s_nr9, 1)


def kernel(**inputs):
    import numpy as np
    import concourse.bacc as bacc
    from concourse import mybir
    from concourse.bass_utils import run_bass_kernel_spmd as run

    g = {k: np.asarray(v) for k, v in inputs.items()}
    tiles = lambda v, fill: np.pad(v, (0, EDGE_TILES * P - N_EDGES), constant_values=fill).reshape(EDGE_TILES, P)
    arrays = {
        "x": np.pad(g["x"], ((0, ROWS - N_NODES), (0, 0))),
        "W_srcT": g["L0_gnn_W_src"].T, "W_src": g["L0_gnn_W_src"], "W_dst": g["L0_gnn_W_dst"],
        "att": np.concatenate([g["L0_gnn_att_src"].reshape(T, D), g["L0_gnn_att_dst"].reshape(T, D)]).T,
        "src": tiles(g["src"], 0), "dst": tiles(g["dst"], NO_NODE),
        "kind": tiles(g["edge_type_2"], 0), "weight": tiles(g["edge_weight"], 0),
    }
    arrays.update({
        "vecs": np.stack([g["L0_gnn_" + k] for k in ("bias", "ln1_g", "ln1_b", "ln2_g", "ln2_b", "ffn_b2")]),
        "ffn_W1T": g["L0_gnn_ffn_W1"].T, "ffn_W2T": g["L0_gnn_ffn_W2"].T, "ffn_b1": g["L0_gnn_ffn_b1"].reshape(KF, P).T,
        "gate_w": g["L0_ffn_gate_w"], "gate_b": g["L0_ffn_gate_b"].reshape(1, EXPERTS),
        "ew1": g["L0_ffn_w1"], "ew2": g["L0_ffn_w2"], "ebias": np.concatenate([g["L0_ffn_b1"], g["L0_ffn_b2"]], 1),
        "evecs": np.stack([g["L0_ffn_gamma"], g["L0_ffn_beta"]]),
    })
    arrays = {k: np.ascontiguousarray(v) for k, v in arrays.items()}
    nc = bacc.Bacc("TRN2", target_bir_lowering=False, num_devices=1)
    a = {k: nc.dram_tensor("in_" + k, v.shape, mybir.dt.from_np(v.dtype), kind="ExternalInput").ap() for k, v in arrays.items()}
    f32 = mybir.dt.float32
    scratch = {k: nc.dram_tensor(k + "_t", s, f32, kind="Internal").ap() for k, s in
               {"xs": (ROWS, D), "xln": (ROWS, D), "s": (ROWS, 2 * H), "ends": (P, 4), "ends2": (P, 2),
                "x1": (ROWS, D), "xn": (ROWS, D), "xe": (TILES_AHEAD * P, D), "ye": (TILES * P, D)}.items()}
    out = nc.dram_tensor("out", (N_NODES, D), f32, kind="ExternalOutput").ap()
    build(nc, a, out, scratch)
    r = run(nc, [{"in_" + k: v for k, v in arrays.items()}], core_ids=[0])
    return r.results[0]["out"]
```
